# Optimizing a Trainium2 kernel written in Bass

```python
import numpy as np
import jax
import jax.numpy as jnp

def _softmax(x, axis=-1):
    return jax.nn.softmax(x, axis=axis)

def _gelu(x):
    return jax.nn.gelu(x, approximate=True)

def _silu(x):
    return jax.nn.silu(x)

def _sigmoid(x):
    return jax.nn.sigmoid(x)

def _layernorm(x, axis=-1, eps=1e-05):
    m = jnp.mean(x, axis=axis, keepdims=True)
    v = jnp.var(x, axis=axis, keepdims=True)
    return (x - m) / jnp.sqrt(v + eps)

def _scatter_add(tgt, idx, src, axis=0):
    return tgt.at[idx].add(src)

def _segment_sum(src, seg, n):
    return jax.ops.segment_sum(src, seg, n)
kernel_name = 'mk_gnn_resnorm_d4_gnn_r64_7b9101'

def setup_inputs(seed: int=0):
    np.random.seed(seed)
    _w = jnp.asarray

    def _rec_inputs():
        import jax
        import jax.numpy as jnp
        _gk = jax.random.key(seed)
        x = -0.0003713 + 1 * jax.random.normal(jax.random.fold_in(_gk, 1), (50000, 128), jnp.float32)
        src = jax.random.randint(jax.random.fold_in(_gk, 2), (25000,), 0, 50000, jnp.int32)
        dst = jnp.minimum((50000 * jax.random.uniform(jax.random.fold_in(_gk, 3), (25000,)) ** 2.0).astype(jnp.int32), 49999)
        _o = jnp.argsort(dst, stable=True)
        src = src[_o]
        dst = dst[_o]
        edge_type_8 = jax.random.randint(jax.random.fold_in(_gk, 13), (25000,), 0, 8, jnp.int32)
        edge_weight = jax.random.uniform(jax.random.fold_in(_gk, 14), (25000,), jnp.float32, 0.0, 1)
        return (x, src, dst, edge_type_8, edge_weight)
    x, src, dst, edge_type_8, edge_weight = _rec_inputs()

    def _L0_gnn_setup():
        import jax, jax.numpy as jnp
        import numpy as np
        N_NODES = 100000
        N_EDGES = 9375
        HIDDEN = 128
        N_REL = 8
        LN_EPS = 1e-05
        key = jax.random.key(seed)
        ks = jax.random.split(key, 6)
        h = jax.random.normal(ks[0], (N_NODES, HIDDEN), dtype=jnp.float32)
        edge_index = jax.random.randint(ks[1], (2, N_EDGES), 0, N_NODES, dtype=jnp.int64)
        edge_type = jax.random.randint(ks[2], (N_EDGES,), 0, N_REL, dtype=jnp.int64)
        s = 1.0 / np.sqrt(HIDDEN)
        W_self = jax.random.uniform(ks[3], (HIDDEN, HIDDEN), jnp.float32, -s, s)
        b_self = jax.random.uniform(ks[4], (HIDDEN,), jnp.float32, -s, s)
        W_rel = jax.random.uniform(ks[5], (N_REL, HIDDEN, HIDDEN), jnp.float32, -s, s)
        gamma = jnp.ones((HIDDEN,), jnp.float32)
        beta = jnp.zeros((HIDDEN,), jnp.float32)
        return {'h': h, 'edge_index': edge_index, 'edge_type': edge_type, 'W_self': W_self, 'b_self': b_self, 'W_rel': W_rel, 'gamma': gamma, 'beta': beta}
    _L0_gnn_all = _L0_gnn_setup()
    _L0_gnn_in = {k: v for k, v in _L0_gnn_all.items() if k in ('W_self', 'b_self', 'W_rel', 'gamma', 'beta')}
    del _L0_gnn_all

    def _L1_gnn_setup():
        import jax, jax.numpy as jnp
        import numpy as np
        N = 50000
        E = 9375
        D = 128
        LN_EPS = 1e-05

        def _sage_layer(x, src, dst, W_l, b_l, W_r, gamma, beta):
            n = x.shape[0]
            msg = x[src]
            summed = jax.ops.segment_sum(msg, dst, num_segments=n)
            cnt = jax.ops.segment_sum(jnp.ones_like(dst, dtype=x.dtype), dst, num_segments=n)
            agg = summed / jnp.maximum(cnt, 1.0)[:, None]
            out = agg @ W_l.T + b_l + x @ W_r.T
            mu = jnp.mean(out, axis=-1, keepdims=True)
            var = jnp.var(out, axis=-1, keepdims=True)
            out = (out - mu) * jax.lax.rsqrt(var + LN_EPS) * gamma + beta
            return jax.nn.relu(out)
        key = jax.random.key(seed)
        ks = jax.random.split(key, 12)
        s = 1.0 / np.sqrt(D)
        inp = {'x': jax.random.normal(ks[0], (N, D), jnp.float32), 'edge_index': jax.random.randint(ks[1], (2, E), 0, N, dtype=jnp.int64)}
        for i in range(2):
            inp[f'W_l{i}'] = jax.random.normal(ks[2 + 5 * i], (D, D), jnp.float32) * s
            inp[f'b_l{i}'] = jnp.zeros((D,), jnp.float32)
            inp[f'W_r{i}'] = jax.random.normal(ks[3 + 5 * i], (D, D), jnp.float32) * s
            inp[f'gamma{i}'] = jnp.ones((D,), jnp.float32)
            inp[f'beta{i}'] = jnp.zeros((D,), jnp.float32)
        return inp
    _L1_gnn_all = _L1_gnn_setup()
    _L1_gnn_in = {k: v for k, v in _L1_gnn_all.items() if k in ('W_l0', 'b_l0', 'W_r0', 'gamma0', 'beta0', 'W_l1', 'b_l1', 'W_r1', 'gamma1', 'beta1')}
    del _L1_gnn_all

    def _L2_gnn_setup():
        import jax, jax.numpy as jnp
        import numpy as np
        NUM_LAYERS = 3

        def _spmm(edge_row, edge_col, edge_val, emb, num_nodes):
            msgs = edge_val[:, None] * emb[edge_col]
            return jax.ops.segment_sum(msgs, edge_row, num_segments=num_nodes)
        key = jax.random.key(seed)
        k1, k2, k3, k4 = jax.random.split(key, 4)
        N, D, E = (100000, 128, 50000)
        x = jax.random.normal(k1, (N, D), dtype=jnp.float32)
        edge_row = jax.random.randint(k2, (E,), 0, N, dtype=jnp.int64 if jax.config.jax_enable_x64 else jnp.int32)
        edge_col = jax.random.randint(k3, (E,), 0, N, dtype=jnp.int64 if jax.config.jax_enable_x64 else jnp.int32)
        edge_val = jax.random.uniform(k4, (E,), dtype=jnp.float32)
        return {'x': x, 'edge_row': edge_row, 'edge_col': edge_col, 'edge_val': edge_val}
    _L2_gnn_all = _L2_gnn_setup()
    _L2_gnn_in = {k: v for k, v in _L2_gnn_all.items() if k in ()}
    del _L2_gnn_all

    def _L3_gnn_setup():
        import jax, jax.numpy as jnp
        import numpy as np
        N_NODES = 50000
        N_EDGES = 12500
        IN_DIM = 128
        HIDDEN = 32
        HEADS = 4
        OUT_DIM = 128
        NEG_SLOPE = 0.2
        LN_EPS = 1e-05

        def _gat_conv(x, src, dst, W, a_src, a_dst, b, concat):
            N = x.shape[0]
            H, C = a_src.shape
            h = (x @ W).reshape(N, H, C)
            al_s = jnp.einsum('nhc,hc->nh', h, a_src)
            al_d = jnp.einsum('nhc,hc->nh', h, a_dst)
            e = jax.nn.leaky_relu(al_s[src] + al_d[dst], NEG_SLOPE)
            m = jax.ops.segment_max(e, dst, num_segments=N)
            p = jnp.exp(e - m[dst])
            z = jax.ops.segment_sum(p, dst, num_segments=N)
            alpha = p / (z[dst] + 1e-16)
            msg = h[src] * alpha[:, :, None]
            out = jax.ops.segment_sum(msg, dst, num_segments=N)
            out = out.reshape(N, H * C) if concat else out.mean(axis=1)
            return out + b
        key = jax.random.key(seed)
        ks = jax.random.split(key, 16)
        HC = HIDDEN * HEADS
        s = 0.1
        return {'x': jax.random.normal(ks[0], (N_NODES, IN_DIM), dtype=jnp.float32), 'edge_index': jax.random.randint(ks[1], (2, N_EDGES), 0, N_NODES, dtype=jnp.int32), 'W0': jax.random.normal(ks[2], (IN_DIM, HC), dtype=jnp.float32) * s, 'a_src0': jax.random.normal(ks[3], (HEADS, HIDDEN), dtype=jnp.float32) * s, 'a_dst0': jax.random.normal(ks[4], (HEADS, HIDDEN), dtype=jnp.float32) * s, 'b0': jnp.zeros((HC,), dtype=jnp.float32), 'W1': jax.random.normal(ks[5], (HC, HC), dtype=jnp.float32) * s, 'a_src1': jax.random.normal(ks[6], (HEADS, HIDDEN), dtype=jnp.float32) * s, 'a_dst1': jax.random.normal(ks[7], (HEADS, HIDDEN), dtype=jnp.float32) * s, 'b1': jnp.zeros((HC,), dtype=jnp.float32), 'W2': jax.random.normal(ks[8], (HC, OUT_DIM), dtype=jnp.float32) * s, 'a_src2': jax.random.normal(ks[9], (1, OUT_DIM), dtype=jnp.float32) * s, 'a_dst2': jax.random.normal(ks[10], (1, OUT_DIM), dtype=jnp.float32) * s, 'b2': jnp.zeros((OUT_DIM,), dtype=jnp.float32), 'gamma': jnp.ones((OUT_DIM,), dtype=jnp.float32), 'beta': jnp.zeros((OUT_DIM,), dtype=jnp.float32)}
    _L3_gnn_all = _L3_gnn_setup()
    _L3_gnn_in = {k: v for k, v in _L3_gnn_all.items() if k in ('W0', 'a_src0', 'a_dst0', 'b0', 'W1', 'a_src1', 'a_dst1', 'b1', 'W2', 'a_src2', 'a_dst2', 'b2', 'gamma', 'beta')}
    del _L3_gnn_all
    return {'x': x, 'src': src, 'dst': dst, 'edge_type_8': edge_type_8, 'edge_weight': edge_weight, 'L0_gnn_W_self': _L0_gnn_in['W_self'], 'L0_gnn_b_self': _L0_gnn_in['b_self'], 'L0_gnn_W_rel': _L0_gnn_in['W_rel'], 'L0_gnn_gamma': _L0_gnn_in['gamma'], 'L0_gnn_beta': _L0_gnn_in['beta'], 'L1_gnn_W_l0': _L1_gnn_in['W_l0'], 'L1_gnn_b_l0': _L1_gnn_in['b_l0'], 'L1_gnn_W_r0': _L1_gnn_in['W_r0'], 'L1_gnn_gamma0': _L1_gnn_in['gamma0'], 'L1_gnn_beta0': _L1_gnn_in['beta0'], 'L1_gnn_W_l1': _L1_gnn_in['W_l1'], 'L1_gnn_b_l1': _L1_gnn_in['b_l1'], 'L1_gnn_W_r1': _L1_gnn_in['W_r1'], 'L1_gnn_gamma1': _L1_gnn_in['gamma1'], 'L1_gnn_beta1': _L1_gnn_in['beta1'], 'L3_gnn_W0': _L3_gnn_in['W0'], 'L3_gnn_a_src0': _L3_gnn_in['a_src0'], 'L3_gnn_a_dst0': _L3_gnn_in['a_dst0'], 'L3_gnn_b0': _L3_gnn_in['b0'], 'L3_gnn_W1': _L3_gnn_in['W1'], 'L3_gnn_a_src1': _L3_gnn_in['a_src1'], 'L3_gnn_a_dst1': _L3_gnn_in['a_dst1'], 'L3_gnn_b1': _L3_gnn_in['b1'], 'L3_gnn_W2': _L3_gnn_in['W2'], 'L3_gnn_a_src2': _L3_gnn_in['a_src2'], 'L3_gnn_a_dst2': _L3_gnn_in['a_dst2'], 'L3_gnn_b2': _L3_gnn_in['b2'], 'L3_gnn_gamma': _L3_gnn_in['gamma'], 'L3_gnn_beta': _L3_gnn_in['beta']}

def reference(x, src, dst, edge_type_8, edge_weight, L0_gnn_W_self, L0_gnn_b_self, L0_gnn_W_rel, L0_gnn_gamma, L0_gnn_beta, L1_gnn_W_l0, L1_gnn_b_l0, L1_gnn_W_r0, L1_gnn_gamma0, L1_gnn_beta0, L1_gnn_W_l1, L1_gnn_b_l1, L1_gnn_W_r1, L1_gnn_gamma1, L1_gnn_beta1, L3_gnn_W0, L3_gnn_a_src0, L3_gnn_a_dst0, L3_gnn_b0, L3_gnn_W1, L3_gnn_a_src1, L3_gnn_a_dst1, L3_gnn_b1, L3_gnn_W2, L3_gnn_a_src2, L3_gnn_a_dst2, L3_gnn_b2, L3_gnn_gamma, L3_gnn_beta):
    import jax
    import jax.numpy as jnp

    def _L0_gnn_ref(h, edge_index, edge_type, W_self, b_self, W_rel, gamma, beta):
        import jax, jax.numpy as jnp
        import numpy as np
        N_NODES = 100000
        N_EDGES = 9375
        HIDDEN = 128
        N_REL = 8
        LN_EPS = 1e-05
        N = h.shape[0]
        out = h @ W_self.T + b_self
        src, dst = (edge_index[0], edge_index[1])
        h_src = h[src]
        R = W_rel.shape[0]
        for rid in range(R):
            w = (edge_type == rid).astype(h.dtype)
            msgs = h_src * w[:, None] @ W_rel[rid].T
            agg = jax.ops.segment_sum(msgs, dst, num_segments=N)
            deg = jax.ops.segment_sum(w, dst, num_segments=N)
            out = out + agg / jnp.maximum(deg, 1.0)[:, None]
        x = jax.nn.relu(out)
        mu = jnp.mean(x, axis=-1, keepdims=True)
        var = jnp.mean(jnp.square(x - mu), axis=-1, keepdims=True)
        xn = (x - mu) * jax.lax.rsqrt(var + LN_EPS)
        return xn * gamma + beta

    def _L1_gnn_ref(x, edge_index, W_l0, b_l0, W_r0, gamma0, beta0, W_l1, b_l1, W_r1, gamma1, beta1):
        import jax, jax.numpy as jnp
        import numpy as np
        N = 50000
        E = 9375
        D = 128
        LN_EPS = 1e-05

        def _sage_layer(x, src, dst, W_l, b_l, W_r, gamma, beta):
            n = x.shape[0]
            msg = x[src]
            summed = jax.ops.segment_sum(msg, dst, num_segments=n)
            cnt = jax.ops.segment_sum(jnp.ones_like(dst, dtype=x.dtype), dst, num_segments=n)
            agg = summed / jnp.maximum(cnt, 1.0)[:, None]
            out = agg @ W_l.T + b_l + x @ W_r.T
            mu = jnp.mean(out, axis=-1, keepdims=True)
            var = jnp.var(out, axis=-1, keepdims=True)
            out = (out - mu) * jax.lax.rsqrt(var + LN_EPS) * gamma + beta
            return jax.nn.relu(out)
        src, dst = (edge_index[0], edge_index[1])
        x = _sage_layer(x, src, dst, W_l0, b_l0, W_r0, gamma0, beta0)
        x = _sage_layer(x, src, dst, W_l1, b_l1, W_r1, gamma1, beta1)
        return x

    def _L2_gnn_ref(x, edge_row, edge_col, edge_val):
        import jax, jax.numpy as jnp
        import numpy as np
        NUM_LAYERS = 3

        def _spmm(edge_row, edge_col, edge_val, emb, num_nodes):
            msgs = edge_val[:, None] * emb[edge_col]
            return jax.ops.segment_sum(msgs, edge_row, num_segments=num_nodes)
        N = x.shape[0]
        emb = x
        acc = x
        for _ in range(NUM_LAYERS):
            emb = _spmm(edge_row, edge_col, edge_val, emb, N)
            acc = acc + emb
        return acc / jnp.float32(NUM_LAYERS + 1)

    def _L3_gnn_ref(x, edge_index, W0, a_src0, a_dst0, b0, W1, a_src1, a_dst1, b1, W2, a_src2, a_dst2, b2, gamma, beta):
        import jax, jax.numpy as jnp
        import numpy as np
        N_NODES = 50000
        N_EDGES = 12500
        IN_DIM = 128
        HIDDEN = 32
        HEADS = 4
        OUT_DIM = 128
        NEG_SLOPE = 0.2
        LN_EPS = 1e-05

        def _gat_conv(x, src, dst, W, a_src, a_dst, b, concat):
            N = x.shape[0]
            H, C = a_src.shape
            h = (x @ W).reshape(N, H, C)
            al_s = jnp.einsum('nhc,hc->nh', h, a_src)
            al_d = jnp.einsum('nhc,hc->nh', h, a_dst)
            e = jax.nn.leaky_relu(al_s[src] + al_d[dst], NEG_SLOPE)
            m = jax.ops.segment_max(e, dst, num_segments=N)
            p = jnp.exp(e - m[dst])
            z = jax.ops.segment_sum(p, dst, num_segments=N)
            alpha = p / (z[dst] + 1e-16)
            msg = h[src] * alpha[:, :, None]
            out = jax.ops.segment_sum(msg, dst, num_segments=N)
            out = out.reshape(N, H * C) if concat else out.mean(axis=1)
            return out + b
        N = x.shape[0]
        loop = jnp.arange(N, dtype=edge_index.dtype)
        src = jnp.concatenate([edge_index[0], loop])
        dst = jnp.concatenate([edge_index[1], loop])
        h = _gat_conv(x, src, dst, W0, a_src0, a_dst0, b0, concat=True)
        h = jax.nn.relu(h)
        h = _gat_conv(h, src, dst, W1, a_src1, a_dst1, b1, concat=True)
        h = jax.nn.relu(h)
        h = _gat_conv(h, src, dst, W2, a_src2, a_dst2, b2, concat=False)
        mu = h.mean(axis=-1, keepdims=True)
        var = jnp.mean((h - mu) ** 2, axis=-1, keepdims=True)
        return (h - mu) * jax.lax.rsqrt(var + LN_EPS) * gamma + beta
    edge_index = jnp.stack([src, dst])
    x = _layernorm(x + _L0_gnn_ref(x, edge_index, edge_type_8, L0_gnn_W_self, L0_gnn_b_self, L0_gnn_W_rel, L0_gnn_gamma, L0_gnn_beta), axis=-1)
    x = _layernorm(x + _L1_gnn_ref(x, edge_index, L1_gnn_W_l0, L1_gnn_b_l0, L1_gnn_W_r0, L1_gnn_gamma0, L1_gnn_beta0, L1_gnn_W_l1, L1_gnn_b_l1, L1_gnn_W_r1, L1_gnn_gamma1, L1_gnn_beta1), axis=-1)
    x = _layernorm(x + _L2_gnn_ref(x, src, dst, edge_weight), axis=-1)
    x = _layernorm(x + _L3_gnn_ref(x, edge_index, L3_gnn_W0, L3_gnn_a_src0, L3_gnn_a_dst0, L3_gnn_b0, L3_gnn_W1, L3_gnn_a_src1, L3_gnn_a_dst1, L3_gnn_b1, L3_gnn_W2, L3_gnn_a_src2, L3_gnn_a_dst2, L3_gnn_b2, L3_gnn_gamma, L3_gnn_beta), axis=-1)
    return x

_drawn_inputs = setup_inputs


def setup_inputs(seed=0):
    import zlib

    import numpy as np

    out = dict(_drawn_inputs(seed))
    spreads = {'L0_gnn_gamma': (1.0, 0.2),
     'L0_gnn_beta': (0.0, 0.1),
     'L1_gnn_b_l0': (0.0, 0.1),
     'L1_gnn_gamma0': (1.0, 0.2),
     'L1_gnn_beta0': (0.0, 0.1),
     'L1_gnn_b_l1': (0.0, 0.1),
     'L1_gnn_gamma1': (1.0, 0.2),
     'L1_gnn_beta1': (0.0, 0.1),
     'L3_gnn_b0': (0.0, 0.1),
     'L3_gnn_b1': (0.0, 0.1),
     'L3_gnn_b2': (0.0, 0.1),
     'L3_gnn_gamma': (1.0, 0.2),
     'L3_gnn_beta': (0.0, 0.1)}
    factors = {'L3_gnn_a_dst0': 4.903,
     'L3_gnn_a_src1': 4.075,
     'L3_gnn_a_dst1': 8.0,
     'L3_gnn_a_src2': 3.574,
     'L3_gnn_a_dst2': 7.028}
    for name, (base, spread) in spreads.items():
        noise = np.random.default_rng([zlib.crc32(name.encode()), seed]).standard_normal(out[name].shape)
        drawn = base * np.exp(spread * noise) if base else spread * noise
        out[name] = jnp.asarray(drawn.astype(out[name].dtype))
    for name, factor in factors.items():
        out[name] = (out[name] * factor).astype(out[name].dtype)
    return out
```

```python
import concourse.bass as bass
from concourse import mybir
from contextlib import ExitStack

fp32 = mybir.dt.float32
i32 = mybir.dt.int32
ALU = mybir.AluOpType
ACT = mybir.ActivationFunctionType
AX = mybir.AxisListType

P = 128
N, D, E = 50000, 128, 25000
R = 8
EPP = -(-E // P)
TS = 4
TN = 8
U = TS + TN
STEPS = EPP // TS + 1
TP = STEPS * TS
SIDE = EPP
NPAD = STEPS * TN * P
NSLOT = TP * P
PAD_NODE = NPAD - 1
OUT_OF_RANGE = 1 << 20
KH = N // P + 2
PAD_KEY = KH * P - 1
H, C = 4, 32
TW = D + 2 * H
EPS = 1e-5
BIG = 1e30


def wait(eng, sem, value):
    if isinstance(value, int) and value <= 0:
        return
    eng.wait_ge(sem, value)


class Step:

    def __init__(self, n, par):
        self.n, self.par = n, par
        self.last = isinstance(n, int) and n == STEPS - 1


def pipelined(eng, order):
    def run(base, par):
        for part, off in order:
            if isinstance(base, int) and not 0 <= base + off < STEPS:
                continue
            part(Step(base + off, (par + off) % 2))

    for base in range(-2, 4):
        run(base, base % 2)
    with eng.Fori(2, STEPS // 2 - 2) as i:
        run(i * 2, 0)
        run(i * 2 + 1, 1)
    for base in range(STEPS - 4, STEPS + 1):
        run(base, base % 2)


class Chain:

    def __init__(self, eng, sem, per):
        self.eng, self.sem, self.per, self.n, self.base = eng, sem, per, 0, 0

    def begin(self, step=None):
        assert step is None or self.n in (0, self.per), (self.n, self.per)
        self.base = 0 if step is None else step.n * self.per
        if step is not None:
            self.n = 0

    def mark(self, ins):
        ins.then_inc(self.sem, 1)
        self.n += 1
        return self.base + self.n

    def link(self, ins):
        self.eng.wait_ge(self.sem, self.mark(ins))


def gnn_kernel(nc, a, out):
    ctx = ExitStack()
    with ctx:
        def sb(name, shape, dt=fp32, c=ctx):
            return c.enter_context(nc.sbuf_tensor(name, shape, dt))

        def pb(name, shape, c=ctx):
            return c.enter_context(nc.psum_tensor(name, shape, fp32))

        used = []

        def sem(name):
            s = ctx.enter_context(nc.semaphore(name))
            used.append(s)
            return s

        def dram(name, shape, dt=fp32):
            return nc.dram_tensor(name, shape, dt, kind="Internal").ap()

        row_of_node = dram("row_of_node", (NPAD, 1), i32)
        X1 = dram("X1", (NPAD + NSLOT, D))
        H1 = dram("H1", (NPAD + NSLOT, D))
        X2 = dram("X2", (NPAD + NSLOT, D))
        X3 = dram("X3", (NPAD + NSLOT, D))
        E1 = dram("E1", (NPAD, D))
        E2 = dram("E2", (NPAD, D))
        E3 = dram("E3", (NPAD, D))
        records = dram("records", (P * EPP, 4))
        T1 = dram("T1", (NPAD + NSLOT, TW))
        T2 = dram("T2", (NPAD + NSLOT, TW))
        T3 = dram("T3", (NPAD + NSLOT, TW))

        def node_rows(t, n):
            return t[0:NPAD, :].rearrange("(n p j) f -> n p j f", p=P, j=TN)[n]

        def slot_rows(t, n):
            base = t.shape[0] - NSLOT if t.shape[0] > NPAD else 0
            return t[base:base + NSLOT, :].rearrange("(p t) f -> p t f", p=P)[:, bass.ds(n * TS, TS), :]

        ident = sb("ident", [P, P])
        ones = sb("ones", [P, P])
        epsc = sb("epsc", [P, 1])
        wself = sb("wself", [P, D])
        wrel = sb("wrel", [P, R, D])
        wsage = sb("wsage", [P, 4, D])
        gatbias = sb("gatbias", [P, 2])
        wgat = sb("wgat", [P, 3, TW])
        rows = {k: sb("row_" + k, [P, D]) for k in (
            "L0_gnn_gamma", "L0_gnn_beta", "L1_gnn_gamma0", "L1_gnn_beta0", "L1_gnn_gamma1", "L1_gnn_beta1",
            "L3_gnn_b2", "L3_gnn_gamma", "L3_gnn_beta")}
        biases = {k: sb("bias_" + k, [1, TS, D]) for k in ("L0_gnn_b_self", "L1_gnn_b_l0", "L1_gnn_b_l1")}
        same = sb("same", [P, TP])
        lead = sb("lead", [P, TP])
        weight = sb("weight", [P, TP])
        rdeg = sb("rdeg", [P, TP])
        coef = sb("coef", [P, TP, R])
        mleft = sb("mleft", [P, P])
        mright = sb("mright", [P, P])
        mside = sb("mside", [P, P])
        mainend = sb("mainend", [P, TP])
        sidend = sb("sidend", [P, TP])
        trail = sb("trail", [P, TP])
        sameb = sb("sameb", [P, TP])
        leadb = sb("leadb", [P, TP])
        weightb = sb("weightb", [P, TP])
        mleftb = sb("mleftb", [P, P])
        dstb = sb("dstb", [P, TP], i32)
        outb = sb("outb", [P, TP], i32)
        goes = sb("goes", [P, EPP])
        linkl = sb("linkl", [P, P])
        linkr = sb("linkr", [P, P])
        sideact = sb("sideact", [P, 1])
        srcidx = sb("srcidx", [P, TP], i32)
        ownidx = sb("ownidx", [P, TP], i32)
        endidx = sb("endidx", [P, TP], i32)
        endrow = sb("endrow", [P, TP], i32)
        outidx = sb("outidx", [P, TP], i32)
        gidx = sb("gidx", [P, TP], i32)

        with ExitStack() as c:
            s_set, s_ld, s_ch, s_wt, s_wc, s_bc, s_cl, s_cnt, s_cross, s_iota, s_map, s_zero, s_am = (
                sem("prep_" + k) for k in ("set", "loaded", "chain", "weights_transposed", "weights_copied",
                                           "rows_spread", "masks", "scans", "crossed", "iota", "map", "zero_rows", "score_vectors"))
            dsti = sb("dsti", [P, TP], i32, c)
            typi = sb("typi", [P, EPP], i32, c)
            previ = sb("previ", [P, 1], i32, c)
            nexti = sb("nexti", [P, 1], i32, c)
            d = sb("d", [P, EPP], fp32, c)
            prev = sb("prev", [P, EPP], fp32, c)
            nxt = sb("nxt", [P, EPP], fp32, c)
            typ = sb("typ", [P, EPP], fp32, c)
            eq = sb("eq", [P, R, EPP], fp32, c)
            fw = sb("fw", [P, R, EPP], fp32, c)
            bw = sb("bw", [P, R, EPP], fp32, c)
            cont = sb("cont", [P, 1], fp32, c)
            endm = sb("endm", [P, EPP], fp32, c)
            t0 = sb("t0", [P, TP], fp32, c)
            t1 = sb("t1", [P, TP], fp32, c)
            t2 = sb("t2", [P, TP], fp32, c)
            slotrow = sb("slotrow", [P, TP], fp32, c)
            siderow = sb("siderow", [P, 1], fp32, c)
            dg = sb("dg", [P, 2, P], fp32, c)
            crossed = sb("crossed", [P, 2, R], fp32, c)
            less = sb("less", [P, P], fp32, c)
            more = sb("more", [P, P], fp32, c)
            nodeid = sb("nodeid", [P, NPAD // P], i32, c)
            wnat = sb("wnat", [P, R + 8, D], fp32, c)
            wgt = sb("wgt", [P, 3, D], fp32, c)
            heads = sb("heads", [P, H], fp32, c)
            avec = sb("avec", [P, 6], fp32, c)
            amat = sb("amat", [P, 3, 2 * H], fp32, c)
            psw = [pb(f"psw{i}", [P, 512], c) for i in range(4)]
            psa = pb("psa", [P, 3, 2 * H], c)
            psr = pb("psr", [P, 2, P], c)
            psx = pb("psx", [P, 2, R], c)
            LASTN = E - (P - 1) * EPP

            with nc.Block() as block:
                @block.sync
                def _(sp):
                    sp.wait_ge(s_set, 6)
                    n = 0
                    def ld(dst, src, **kw):
                        nonlocal n
                        sp.dma_start(dst, src, **kw).then_inc(s_ld, 16)
                        n += 1
                    for buf, name in ((dsti, "dst"), (srcidx, "src"), (typi, "edge_type_8")):
                        ld(buf[0:P - 1, 0:EPP], a[name][0:(P - 1) * EPP].rearrange("(p t) -> p t", t=EPP))
                        ld(buf[P - 1:P, 0:LASTN], a[name][(P - 1) * EPP:E].rearrange("(p t) -> p t", p=1))
                    ld(weight[0:P - 1, 0:EPP], a["edge_weight"][0:(P - 1) * EPP].rearrange("(p t) -> p t", t=EPP))
                    ld(weight[P - 1:P, 0:LASTN], a["edge_weight"][(P - 1) * EPP:E].rearrange("(p t) -> p t", p=1))
                    ld(previ[1:P, :], a["dst"][EPP - 1:E].rearrange("(p t) -> p t", p=1)[:, 0:1 + EPP * (P - 2):EPP].rearrange("p t -> t p"), allow_slow_non_contiguous=True)
                    ld(nexti[0:P - 1, :], a["dst"][EPP:E].rearrange("(p t) -> p t", p=1)[:, 0:1 + EPP * (P - 2):EPP].rearrange("p t -> t p"), allow_slow_non_contiguous=True)
                    ld(wnat[:, 0, :], a["L0_gnn_W_self"])
                    ld(wnat[:, 1:R + 1, :], a["L0_gnn_W_rel"].rearrange("r o f -> o r f"))
                    for k, name in enumerate(("W_l0", "W_r0", "W_l1", "W_r1")):
                        ld(wnat[:, R + 1 + k, :], a["L1_gnn_" + name])
                    for k in range(2):
                        ld(gatbias[:, k:k + 1], a[f"L3_gnn_b{k}"].unsqueeze(1), allow_slow_non_contiguous=True)
                    for k in range(3):
                        ld(wnat[:, R + 5 + k, :], a[f"L3_gnn_W{k}"])
                        for l, name in enumerate(("a_src", "a_dst")):
                            ld(avec[:, 2 * k + l:2 * k + l + 1], a[f"L3_gnn_{name}{k}"].rearrange("h c -> (h c)").unsqueeze(1), allow_slow_non_contiguous=True)
                    for k, t in rows.items():
                        ld(t[:, :], a[k].partition_broadcast(P))
                    for k, t in biases.items():
                        for j in range(TS):
                            ld(t[0:1, j, :], a[k].rearrange("(a f) -> a f", a=1))
                    assert 16 * n == PREP_LOADS
                    sp.wait_ge(s_iota, 1)
                    sp.dma_start(row_of_node.rearrange("(p t) o -> p (t o)", p=P), nodeid[:, :]).then_inc(s_map, 16)


                @block.gpsimd
                def _(pool):
                    nc.gpsimd.iota(nodeid[:, :], [[1, NPAD // P]], base=0, channel_multiplier=NPAD // P).then_inc(s_iota, 1)
                    nc.gpsimd.iota(slotrow[:, :], [[1, TP]], base=NPAD, channel_multiplier=TP, allow_small_or_imprecise_dtypes=True).then_inc(s_iota, 1)
                    nc.gpsimd.iota(siderow[:, :], [[1, 1]], base=NPAD + SIDE, channel_multiplier=TP, allow_small_or_imprecise_dtypes=True).then_inc(s_iota, 1)
                    pool.wait_ge(s_cl, 3)
                    nc.gpsimd.affine_select(out=ident[:, :], in_=ones[:, :], compare_op=ALU.is_equal, fill=0.0, base=0, pattern=[[-1, P]], channel_multiplier=1).then_inc(s_iota, 1)
                    nc.gpsimd.affine_select(out=less[:, :], in_=ones[:, :], compare_op=ALU.is_gt, fill=0.0, base=0, pattern=[[1, P]], channel_multiplier=-1).then_inc(s_iota, 1)
                    nc.gpsimd.affine_select(out=more[:, :], in_=ones[:, :], compare_op=ALU.is_gt, fill=0.0, base=0, pattern=[[-1, P]], channel_multiplier=1).then_inc(s_iota, 1)

                    nc.gpsimd.affine_select(out=heads[:, :], in_=ones[:, 0:H], compare_op=ALU.is_ge, fill=0.0, base=0, pattern=[[-C, H]], channel_multiplier=1).then_inc(s_iota, 1)
                    pool.wait_ge(s_iota, 7)
                    nc.gpsimd.affine_select(out=heads[:, :], in_=heads[:, :], compare_op=ALU.is_ge, fill=0.0, base=C - 1, pattern=[[C, H]], channel_multiplier=-1).then_inc(s_iota, 1)

                @block.tensor
                def _(pe):
                    pe.wait_ge(s_iota, 4)
                    pe.wait_ge(s_ld, PREP_LOADS)
                    for k in range(R + 8):
                        m = nc.tensor.transpose(psw[k // 4][:, (k % 4) * P:(k % 4 + 1) * P], wnat[:, k, :], ident[:, :])
                    m.then_inc(s_wt, 1)
                    pe.wait_ge(s_am, 1)
                    pe.wait_ge(s_wc, R + 8)
                    for k in range(3):
                        m = nc.tensor.matmul(psa[:, k, :], wgt[:, k, :], amat[:, k, :], start=True, stop=True)
                    m.then_inc(s_wt, 1)
                    pe.wait_ge(s_bc, 1)
                    for k in range(2):
                        m = nc.tensor.matmul(psr[:, k, :], ones[:, :], dg[:, k, :], start=True, stop=True)
                    m.then_inc(s_wt, 1)
                    pe.wait_ge(s_cnt, 1)
                    nc.tensor.matmul(psx[:, 0, :], mleft[:, :], fw[:, :, EPP - 1], start=True, stop=True)
                    nc.tensor.matmul(psx[:, 1, :], mright[:, :], bw[:, :, 0], start=True, stop=True).then_inc(s_cross, 1)

                @block.scalar
                def _(act):
                    act.wait_ge(s_wt, 1)
                    nc.scalar.copy(wself[:, :], psw[0][:, 0:P]).then_inc(s_wc, 1)
                    for k in range(1, R + 1):
                        nc.scalar.copy(wrel[:, k - 1, :], psw[k // 4][:, (k % 4) * P:(k % 4 + 1) * P]).then_inc(s_wc, 1)
                    for k in range(R + 1, R + 8):
                        dst = wsage[:, k - R - 1, :] if k < R + 5 else wgt[:, k - R - 5, :]
                        nc.scalar.copy(dst, psw[k // 4][:, (k % 4) * P:(k % 4 + 1) * P]).then_inc(s_wc, 1)
                    act.wait_ge(s_wt, 2)
                    nc.scalar.copy(wgat[:, :, D:TW], psa[:, :, :]).then_inc(s_wc, 1)
                    nc.scalar.copy(wgat[:, :, 0:D], wnat[:, R + 5:R + 8, :]).then_inc(s_wc, 1)

                @block.vector
                def _(dve):
                    ch = Chain(dve, s_ch, 0)
                    v = nc.vector
                    v.memset(dsti[:, :], PAD_NODE).then_inc(s_set, 1)
                    v.memset(srcidx[:, :], 0).then_inc(s_set, 1)
                    v.memset(typi[:, :], 0).then_inc(s_set, 1)
                    v.memset(weight[:, :], 0.0).then_inc(s_set, 1)
                    v.memset(previ[:, :], -1).then_inc(s_set, 1)
                    v.memset(nexti[:, :], -1).then_inc(s_set, 1)
                    v.memset(ones[:, :], 1.0).then_inc(s_cl, 1)
                    v.memset(epsc[:, :], EPS).then_inc(s_cl, 1)
                    v.memset(coef[:, :, :], 0.0).then_inc(s_cl, 1)
                    for t in (same, lead, rdeg, mainend, sidend, trail):
                        ch.link(v.memset(t[:, :], 0.0))
                    dve.wait_ge(s_ld, PREP_LOADS)
                    dve.wait_ge(s_cl, 3)
                    dve.wait_ge(s_iota, 8)
                    ch.link(v.memset(amat[:, :, :], 0.0))
                    for k in range(2):
                        for l in range(2):
                            ch.link(v.tensor_scalar(amat[:, k, l * H:(l + 1) * H], heads[:, :], avec[:, 2 * k + l:2 * k + l + 1], None, ALU.mult))
                    for l in range(2):
                        ch.link(v.tensor_copy(amat[:, 2, l * H:l * H + 1], avec[:, 4 + l:5 + l]))
                    dve.sem_inc(s_am, 1)
                    ch.link(v.tensor_copy(d[:, :], dsti[:, 0:EPP]))
                    ch.link(v.tensor_copy(typ[:, :], typi[:, :]))
                    ch.link(v.tensor_copy(prev[:, 1:EPP], dsti[:, 0:EPP - 1]))
                    ch.link(v.tensor_copy(prev[:, 0:1], previ[:, :]))
                    ch.link(v.tensor_copy(nxt[:, 0:EPP - 1], dsti[:, 1:EPP]))
                    ch.link(v.tensor_copy(nxt[:, EPP - 1:EPP], nexti[:, :]))
                    ch.mark(v.tensor_scalar(dg[:, 0, :], ident[:, :], d[:, 0:1], None, ALU.mult))
                    ch.link(v.tensor_scalar(dg[:, 1, :], ident[:, :], d[:, EPP - 1:EPP], None, ALU.mult))
                    dve.sem_inc(s_bc, 1)
                    ch.mark(v.tensor_tensor(same[:, 1:EPP], d[:, 1:EPP], prev[:, 1:EPP], ALU.is_equal))
                    ch.mark(v.tensor_tensor(cont[:, :], d[:, 0:1], prev[:, 0:1], ALU.is_equal))
                    ch.mark(v.tensor_tensor(endm[:, :], d[:, :], nxt[:, :], ALU.not_equal))
                    ch.mark(v.tensor_scalar(lead[:, 0:EPP], d[:, :], d[:, 0:1], None, ALU.is_equal))
                    ch.link(v.tensor_scalar(trail[:, 0:EPP], d[:, :], d[:, EPP - 1:EPP], None, ALU.is_equal))
                    ch.link(v.scalar_tensor_tensor(sidend[:, 0:EPP], endm[:, :], cont[:, 0:1], lead[:, 0:EPP], ALU.mult, ALU.mult))
                    ch.mark(v.tensor_tensor(mainend[:, 0:EPP], endm[:, :], sidend[:, 0:EPP], ALU.subtract))
                    ch.link(v.reduce_max(sideact[:, :], sidend[:, 0:EPP], AX.X))
                    ch.link(v.tensor_scalar(t0[:, :], slotrow[:, :], siderow[:, 0:1], -1.0, ALU.subtract, ALU.mult))
                    ch.link(v.tensor_tensor(t0[:, :], t0[:, :], sidend[:, :], ALU.mult))
                    ch.link(v.tensor_tensor(t0[:, :], t0[:, :], slotrow[:, :], ALU.add))
                    ch.link(v.tensor_copy(endrow[:, :], t0[:, :]))
                    ch.link(v.tensor_scalar(t1[:, 0:EPP], d[:, :], float(OUT_OF_RANGE), None, ALU.subtract))
                    ch.link(v.memset(t2[:, :], float(OUT_OF_RANGE)))
                    ch.link(v.tensor_tensor(t0[:, 0:EPP], t1[:, 0:EPP], endm[:, :], ALU.mult))
                    ch.link(v.tensor_tensor(t2[:, 0:EPP], t2[:, 0:EPP], t0[:, 0:EPP], ALU.add))
                    ch.link(v.tensor_copy(endidx[:, :], t2[:, :]))
                    ch.link(v.memset(t2[:, :], float(OUT_OF_RANGE)))
                    ch.link(v.tensor_tensor(t0[:, 0:EPP], t1[:, 0:EPP], mainend[:, 0:EPP], ALU.mult))
                    ch.link(v.tensor_tensor(t2[:, 0:EPP], t2[:, 0:EPP], t0[:, 0:EPP], ALU.add))
                    ch.link(v.tensor_tensor(t0[:, 0:1], t1[:, 0:1], sideact[:, :], ALU.mult))
                    ch.link(v.tensor_tensor(t2[:, SIDE:SIDE + 1], t2[:, SIDE:SIDE + 1], t0[:, 0:1], ALU.add))
                    ch.link(v.tensor_copy(outidx[:, :], t2[:, :]))
                    ch.link(v.memset(t0[:, :], 0.0))
                    ch.link(v.tensor_scalar(t0[:, 0:EPP], d[:, :], float(N - 1), None, ALU.min))
                    ch.link(v.tensor_scalar(t0[:, SIDE:SIDE + 1], d[:, 0:1], float(N - 1), None, ALU.min))
                    ch.link(v.tensor_copy(ownidx[:, :], t0[:, :]))
                    dve.wait_ge(s_wt, 3)
                    ch.link(v.scalar_tensor_tensor(mleft[:, :], psr[:, 0, :], d[:, EPP - 1:EPP], less[:, :], ALU.is_equal, ALU.mult))
                    ch.link(v.scalar_tensor_tensor(mright[:, :], psr[:, 1, :], d[:, 0:1], more[:, :], ALU.is_equal, ALU.mult))
                    ch.link(v.tensor_scalar(mside[:, :], mright[:, :], sideact[:, 0:1], None, ALU.mult))
                    for link, m in ((linkl, mright), (linkr, mleft)):
                        ch.link(v.tensor_scalar(link[:, :], (psr[:, 1, :] if link is linkl else psr[:, 0, :]), d[:, 0:1] if link is linkl else d[:, EPP - 1:EPP], None, ALU.is_equal))
                        ch.link(v.tensor_tensor(link[:, :], link[:, :], (more if link is linkl else less)[:, :], ALU.mult))
                        ch.link(v.tensor_scalar(link[:, :], link[:, :], 1.0, BIG, ALU.subtract, ALU.mult))
                    for r in range(R):
                        ch.link(v.tensor_scalar(eq[:, r, :], typ[:, :], float(r), None, ALU.is_equal))
                    for r in range(R):
                        ch.mark(v.tensor_tensor_scan(fw[:, r, :], same[:, 0:EPP], eq[:, r, :], 0.0, ALU.mult, ALU.add))
                    ch.link(v.tensor_tensor(goes[:, :], d[:, :], nxt[:, :], ALU.is_equal))
                    for r in range(R):
                        ch.link(v.tensor_tensor_scan(bw[:, r, ::-1], goes[:, ::-1], eq[:, r, ::-1], 0.0, ALU.mult, ALU.add))
                    dve.sem_inc(s_cnt, 1)
                    dve.wait_ge(s_cross, 1)
                    ch.link(v.tensor_copy(crossed[:, :, :], psx[:, :, :]))
                    for r in range(R):
                        ch.mark(v.scalar_tensor_tensor(fw[:, r, :], lead[:, 0:EPP], crossed[:, 0, r:r + 1], fw[:, r, :], ALU.mult, ALU.add))
                        ch.link(v.scalar_tensor_tensor(bw[:, r, :], trail[:, 0:EPP], crossed[:, 1, r:r + 1], bw[:, r, :], ALU.mult, ALU.add))
                    ch.link(v.tensor_tensor(fw[:, :, :], fw[:, :, :], bw[:, :, :], ALU.add))
                    ch.link(v.tensor_tensor(fw[:, :, :], fw[:, :, :], eq[:, :, :], ALU.subtract))
                    ch.link(v.reduce_sum(t0[:, 0:EPP], fw[:, :, :].rearrange("p r t -> p t r"), AX.X))
                    ch.link(v.reciprocal(rdeg[:, 0:EPP], t0[:, 0:EPP]))
                    ch.link(v.tensor_tensor(fw[:, :, :], fw[:, :, :], eq[:, :, :], ALU.mult))
                    ch.link(v.reduce_sum(t0[:, 0:EPP], fw[:, :, :].rearrange("p r t -> p t r"), AX.X))
                    ch.link(v.reciprocal(t1[:, 0:EPP], t0[:, 0:EPP]))
                    for r in range(R):
                        ch.link(v.tensor_tensor(coef[:, 0:EPP, r], eq[:, r, :], t1[:, 0:EPP], ALU.mult))
                    dve.wait_ge(s_wc, R + 10)
                    dve.wait_ge(s_map, 16)
        nc.all_engine_barrier()

        idxr = sb("idxr", [P, 2, 2 * TS], i32)
        ownal = sb("ownal", [P, TP, 2 * H])
        st = sb("st", [P, U, 6])
        lnt = sb("lnt", [P, 4, U])
        var = sb("var", [P, 2, U])
        sd = sb("sd", [P, 2, U])
        rstd = sb("rstd", [P, 2, U])
        nmr = sb("nmr", [P, 2, U])

        def spread(row, tiles):
            return row[:, :].unsqueeze(1).to_broadcast([P, tiles, D])

        def scan_edge(s, k, src, acc, cap, s_sum, s_cap, dve, same=same, lead=lead):
            t, slot, w = s.n * TS + k, s.par * TS + k, acc.shape[2]
            nc.vector.scalar_tensor_tensor(acc[:, slot, :], acc[:, (slot - 1) % (2 * TS), :], same[:, bass.ds(t, 1)],
                                           src, ALU.mult, ALU.add).then_inc(s_sum, 1)
            nc.vector.scalar_tensor_tensor(cap[:, :], src, lead[:, bass.ds(t, 1)], cap[:, :], ALU.mult, ALU.add).then_inc(s_cap, 1)
            dve.wait_ge(s_sum, t + 1)
            dve.wait_ge(s_cap, t + 1)

        def side_sums(acc, cap, psC, s_sum, s_carry, dve):
            w = acc.shape[2]
            dve.wait_ge(s_carry, 1)
            nc.vector.tensor_tensor(acc[:, SIDE % (2 * TS), :], psC, cap[:, :], ALU.add).then_inc(s_sum, 1)
            nc.vector.memset(acc[:, SIDE % (2 * TS) + 1:SIDE % (2 * TS) + TS, :], 0.0).then_inc(s_sum, TS - 1)

        def normalizing(dve, ch, s, k, src, t0, s_var, s_std, s_norm, t1=U, factor=1.0, first=0):
            v = nc.vector
            for j in range(t0, t1):
                at = ch.mark(v.bn_stats(st[:, j, :], src[:, j - first, :]))
            dve.wait_ge(ch.sem, at)
            tt = slice(t0, t1)
            ch.mark(v.tensor_tensor(lnt[:, 0, tt], st[:, tt, 1], st[:, tt, 4], ALU.subtract))
            ch.mark(v.tensor_tensor(lnt[:, 1, tt], st[:, tt, 2], st[:, tt, 5], ALU.add))
            ch.link(v.tensor_tensor(lnt[:, 2, tt], st[:, tt, 1], st[:, tt, 4], ALU.add))
            ch.link(v.scalar_tensor_tensor(lnt[:, 3, tt], lnt[:, 0, tt], 0.25, lnt[:, 0, tt], ALU.mult, ALU.mult))
            v.scalar_tensor_tensor(var[:, k, tt], lnt[:, 1, tt], 1.0 / D, lnt[:, 3, tt], ALU.mult, ALU.add).then_inc(s_var, 1)
            dve.wait_ge(s_std, s.n + 1)
            ch.link(v.reciprocal(rstd[:, k, tt], sd[:, k, tt]))
            if factor != 1.0:
                ch.link(v.tensor_scalar(rstd[:, k, tt], rstd[:, k, tt], factor, None, ALU.mult))
            v.scalar_tensor_tensor(nmr[:, k, tt], lnt[:, 2, tt], -0.5, rstd[:, k, tt], ALU.mult, ALU.mult).then_inc(s_norm, 1)

        LN_LINKS = 5

        def deviate(act, s, k, t0, s_var, s_std, t1=U, factor=1.0):
            act.wait_ge(s_var, s.n + 1)
            nc.scalar.activation(sd[:, k, t0:t1], var[:, k, t0:t1], ACT.Sqrt, bias=epsc[:, 0:1], scale=factor * factor).then_inc(s_std, 1)

        def normalize(act, s, k, src, dst, t0, s_norm, s_done, t1=U):
            act.wait_ge(s_norm, s.n + 1)
            for j in range(t0, t1):
                m = nc.scalar.activation(dst[:, j, :], src[:, j, :], ACT.Identity, bias=nmr[:, k, j:j + 1], scale=rstd[:, k, j:j + 1])
            m.then_inc(s_done, 1)

        s_go = ctx.enter_context(nc.semaphore("row_numbers_seen"))

        def indices(pool, sem, count):
            pool.wait_ge(sem, count)
            pool.sem_inc(s_go, 1)

        def gather(pool, dst, table, index, done, last):
            pool.indirect_dma_start(out=dst, out_offset=None, in_=table, in_offset=bass.IndirectOffsetOnAxis(ap=index, axis=0),
                                    bounds_check=last, oob_is_err=False).then_inc(done, 16)

        def scatter_rows(pool, table, rows_, index, done, last):
            pool.indirect_dma_start(out=table, out_offset=bass.IndirectOffsetOnAxis(ap=index, axis=0), in_=rows_, in_offset=None,
                                    bounds_check=last, oob_is_err=False).then_inc(done, 16)

        def arrived(s):
            return (s.n - s.par) * 8 + 16

        def free(s, each):
            return (s.n - 1) * each

        def first_free(s, each):
            return free(s, each)

        def closing(sems, c):
            nc.all_engine_barrier()
            for x in sems:
                nc.sync.sem_clear(x)
            nc.all_engine_barrier()

        def names(prefix, c, *keys):
            out_ = [c.enter_context(nc.semaphore(prefix + k)) for k in keys]
            return out_

        closing(used, None)
        gath = names("", ctx, *[f"gathered{k}" for k in range(2 * TS)])
        ogath = names("", ctx, *[f"own_gathered{k}" for k in range(2 * TS)])
        s_mv = names("", ctx, "map_moved0", "map_moved1")
        placed = [16 * len(range(k, EPP, 2 * TS)) for k in range(2 * TS)]
        before = [0] * (2 * TS)

        def edge_rows(eng, s, k):
            eng.wait_ge(gath[s.par * TS + k], before[s.par * TS + k] + arrived(s))

        def slots_moved():
            for k in range(2 * TS):
                placed[k] += 8 * STEPS

        def slot_rows_moved(eng, s, k):
            eng.wait_ge(ogath[s.par * TS + k], placed[s.par * TS + k] + arrived(s))

        def slot_rows_free(eng, s, k):
            if not (isinstance(s.n, int) and s.n < 2 and placed[s.par * TS + k] == 0):
                eng.wait_ge(ogath[s.par * TS + k], placed[s.par * TS + k] + (s.n - s.par) * 8)

        def row_numbers_free(pool, s):
            if not (isinstance(s.n, int) and s.n < 2):
                for k in range(TS):
                    slot_rows_free(pool, s, k)

        def edges_gathered():
            for t in range(EPP):
                before[t % (2 * TS)] += 16


        with ExitStack() as c:
            s_ld, s_iota, s_ch, s_hot, s_hist, s_base, s_row, s_tr, s_tc, s_look, s_run, s_cp, s_pos, s_rec, s_set, s_zero = names(
                "sort_", c, "loaded", "iota", "chain", "one_hot", "counted", "bases", "keys_spread", "transposed", "transpose_copied",
                "looked_up", "run_on", "run_copied", "position", "records", "cleared", "zeroed")
            keyi = sb("keyi", [P, EPP], i32, c)
            loi = sb("loi", [P, EPP], i32, c)
            key = sb("key", [P, EPP], fp32, c)
            lo = sb("lo", [P, EPP], fp32, c)
            hi = sb("hi", [P, EPP], fp32, c)
            columns = sb("columns", [P, KH], fp32, c)
            olo = sb("olo", [P, 2, P], fp32, c)
            ohi = sb("ohi", [P, 2, KH], fp32, c)
            oloT = sb("oloT", [P, 2, P], fp32, c)
            diag = sb("diag", [P, 2, P], fp32, c)
            count = sb("count", [P, KH], fp32, c)
            base = sb("base", [P, KH], fp32, c)
            run = sb("run", [P, 2, KH], fp32, c)
            picked = sb("picked", [P, KH], fp32, c)
            twin = sb("twin", [P, P], fp32, c)
            part = sb("part", [P, 2], fp32, c)
            place = sb("place", [P, EPP], fp32, c)
            placei = sb("placei", [P, EPP], i32, c)
            rec = sb("rec", [P, EPP, 4], fp32, c)
            desti = sb("desti", [P, EPP], i32, c)
            less = sb("less_s", [P, P], fp32, c)
            more = sb("more_s", [P, P], fp32, c)
            zeros = sb("zeros", [P, TN, D], fp32, c)
            psH = pb("psH", [P, 512], c)
            psL = [pb(f"psL{i}", [P, 512], c) for i in range(2)]
            psR = [pb(f"psR{i}", [P, 512], c) for i in range(2)]
            psH2 = [psH, pb("psH2", [P, 512], c)]
            psQ = pb("psQ", [P, 512], c)
            psB = pb("psB", [P, 8], c)

            def tiles(eng, part_):
                for t in range(2):
                    part_(t, t)
                with eng.Fori(1, EPP // 2 - 1) as i:
                    part_(i * 2, 0)
                    part_(i * 2 + 1, 1)
                for t in range(EPP - 2, EPP):
                    part_(t, t % 2)

            with nc.Block() as block:
                @block.sync
                def _(sp):
                    sp.wait_ge(s_set, 2)
                    for buf, name in ((keyi, "src"), (desti, "dst")):
                        sp.dma_start(buf[0:P - 1, :], a[name][0:(P - 1) * EPP].rearrange("(p t) -> p t", t=EPP)).then_inc(s_ld, 16)
                        sp.dma_start(buf[P - 1:P, 0:E - (P - 1) * EPP], a[name][(P - 1) * EPP:E].rearrange("(p t) -> p t", p=1)).then_inc(s_ld, 16)
                    sp.wait_ge(s_set, 3)
                    with sp.Fori(0, STEPS) as i:
                        for t in (E1, E2, E3):
                            sp.dma_start(node_rows(t, i), zeros[:, :, :]).then_inc(s_zero, 16)
                    sp.wait_ge(s_zero, 48 * STEPS)

                @block.gpsimd
                def _(pool):
                    last_record = pool.to_reg(P * EPP - 1)
                    nc.gpsimd.iota(columns[:, :], [[1, KH]], base=0, channel_multiplier=0, allow_small_or_imprecise_dtypes=True).then_inc(s_iota, 1)
                    nc.gpsimd.affine_select(out=less[:, :], in_=ones[:, :], compare_op=ALU.is_gt, fill=0.0, base=0, pattern=[[1, P]], channel_multiplier=-1).then_inc(s_iota, 1)
                    nc.gpsimd.affine_select(out=more[:, :], in_=ones[:, :], compare_op=ALU.is_gt, fill=0.0, base=0, pattern=[[-1, P]], channel_multiplier=1).then_inc(s_iota, 1)
                    pool.wait_ge(s_rec, 1)
                    for t in range(EPP):
                        pool.indirect_dma_start(out=records, out_offset=bass.IndirectOffsetOnAxis(ap=placei[:, t:t + 1], axis=0), in_=rec[:, t, :], in_offset=None,
                                                bounds_check=last_record, oob_is_err=False).then_inc(ogath[t % (2 * TS)], 16)
                    for k in range(2 * TS):
                        pool.wait_ge(ogath[k], 16 * len(range(k, EPP, 2 * TS)))

                @block.tensor
                def _(pe):
                    t_ = nc.tensor

                    def count_up(t, par):
                        pe.wait_ge(s_hot, t + 1)
                        t_.matmul(psH[:, 0:KH], olo[:, par, :], ohi[:, par, :], start=isinstance(t, int) and t == 0,
                                  stop=isinstance(t, int) and t == EPP - 1).then_inc(s_hist, 1)

                    tiles(pe, count_up)
                    pe.wait_ge(s_base, 1)
                    t_.matmul(psB[:, 0:1], less[:, :], part[:, 0:1], start=True, stop=True).then_inc(s_row, 1)

                    def look(t, par):
                        pe.wait_ge(s_hot, t + EPP + 1)
                        t_.transpose(psR[par][:, 0:P], olo[:, par, :], ident[:, :]).then_inc(s_tr, 1)
                        t_.matmul(psQ[:, par * P:(par + 1) * P], ones[:, :], diag[:, par, :], start=True, stop=True).then_inc(s_row, 1)
                        t_.matmul(psH2[par][:, 0:KH], olo[:, par, :], ohi[:, par, :], start=True, stop=True).then_inc(s_run, 1)
                        pe.wait_ge(s_tc, t + 1)
                        pe.wait_ge(s_cp, t + 1)
                        t_.matmul(psL[par][:, 0:KH], oloT[:, par, :], run[:, par, :], start=True, stop=True).then_inc(s_look, 1)

                    tiles(pe, look)

                @block.scalar
                def _(act):
                    def copies(t, par):
                        act.wait_ge(s_tr, t + 1)
                        if not (isinstance(t, int) and t < 2):
                            act.wait_ge(s_look, t - 1)
                        nc.scalar.copy(oloT[:, par, :], psR[par][:, 0:P]).then_inc(s_tc, 1)

                    tiles(act, copies)

                @block.vector
                def _(dve):
                    v = nc.vector
                    ch = Chain(dve, s_ch, 0)
                    v.memset(keyi[:, :], PAD_KEY).then_inc(s_set, 1)
                    v.memset(desti[:, :], 0).then_inc(s_set, 1)
                    v.memset(zeros[:, :, :], 0.0).then_inc(s_set, 1)
                    dve.wait_ge(s_ld, 64)
                    dve.wait_ge(s_iota, 3)
                    ch.link(v.tensor_copy(key[:, :], keyi[:, :]))
                    ch.link(v.tensor_scalar(loi[:, :], keyi[:, :], P - 1, None, ALU.bitwise_and))
                    ch.link(v.tensor_copy(lo[:, :], loi[:, :]))
                    ch.link(v.tensor_tensor(hi[:, :], key[:, :], lo[:, :], ALU.subtract))
                    ch.link(v.tensor_scalar(hi[:, :], hi[:, :], 1.0 / P, None, ALU.mult))
                    ch.link(v.memset(rec[:, :, 3], 0.0))
                    ch.link(v.tensor_copy(rec[:, :, 0], keyi[:, :]))
                    ch.link(v.tensor_copy(rec[:, :, 1], desti[:, :]))
                    ch.link(v.tensor_copy(rec[:, :, 2], weight[:, 0:EPP]))

                    def hot(t, par):
                        if isinstance(t, int):
                            wait(dve, s_hist, t - 1)
                        else:
                            dve.wait_ge(s_hist, t - 1)
                        v.tensor_scalar(olo[:, par, :], columns[:, 0:P], lo[:, bass.ds(t, 1)], None, ALU.is_equal)
                        v.tensor_scalar(ohi[:, par, :], columns[:, :], hi[:, bass.ds(t, 1)], None, ALU.is_equal).then_inc(s_hot, 1)

                    tiles(dve, hot)
                    dve.wait_ge(s_hist, EPP)
                    ch.link(v.tensor_copy(count[:, :], psH[:, 0:KH]))
                    ch.link(v.tensor_tensor_scan(base[:, :], ones[:, 0:1].to_broadcast([P, KH]), count[:, :], 0.0, ALU.mult, ALU.add))
                    v.reduce_sum(part[:, 0:1], count[:, :], AX.X).then_inc(s_base, 1)
                    dve.wait_ge(s_row, 1)
                    ch.link(v.tensor_tensor(base[:, :], base[:, :], count[:, :], ALU.subtract))
                    v.tensor_scalar(run[:, 0, :], base[:, :], psB[:, 0:1], None, ALU.add).then_inc(s_cp, 1)

                    def position(t, par):
                        if not (isinstance(t, int) and t < 2):
                            dve.wait_ge(s_look, t - 1)
                        v.tensor_scalar(olo[:, par, :], columns[:, 0:P], lo[:, bass.ds(t, 1)], None, ALU.is_equal)
                        v.tensor_scalar(diag[:, par, :], ident[:, :], key[:, bass.ds(t, 1)], None, ALU.mult)
                        v.tensor_scalar(ohi[:, par, :], columns[:, :], hi[:, bass.ds(t, 1)], None, ALU.is_equal).then_inc(s_hot, 1)
                        dve.wait_ge(s_row, t + 2)
                        v.scalar_tensor_tensor(twin[:, :], psQ[:, par * P:(par + 1) * P], key[:, bass.ds(t, 1)], more[:, :], ALU.is_equal, ALU.mult).then_inc(s_pos, 1)
                        dve.wait_ge(s_pos, t * 5 + 1)
                        v.reduce_sum(part[:, 0:1], twin[:, :], AX.X).then_inc(s_pos, 1)
                        dve.wait_ge(s_run, t + 1)
                        dve.wait_ge(s_cp, t + 1)
                        v.tensor_tensor(run[:, 1 - par, :], run[:, par, :], psH2[par][:, 0:KH], ALU.add).then_inc(s_cp, 1)
                        dve.wait_ge(s_look, t + 1)
                        v.tensor_tensor(picked[:, :], psL[par][:, 0:KH], ohi[:, par, :], ALU.mult).then_inc(s_pos, 1)
                        dve.wait_ge(s_pos, t * 5 + 3)
                        v.reduce_sum(part[:, 1:2], picked[:, :], AX.X).then_inc(s_pos, 1)
                        dve.wait_ge(s_pos, t * 5 + 4)
                        v.tensor_tensor(place[:, bass.ds(t, 1)], part[:, 0:1], part[:, 1:2], ALU.add).then_inc(s_pos, 1)

                    tiles(dve, position)
                    dve.wait_ge(s_pos, 5 * EPP)
                    v.tensor_copy(placei[:, :], place[:, :]).then_inc(s_rec, 1)
            closing([s_ld, s_iota, s_ch, s_hot, s_hist, s_base, s_row, s_tr, s_tc, s_look, s_run, s_cp, s_pos, s_rec, s_set, s_zero], c)

        with ExitStack() as c:
            s_ld, s_set, s_ch, s_iota, s_dg, s_row = names("masks_", c, "loaded", "cleared", "chain", "iota", "diagonal", "row_spread")
            rec = sb("rec_b", [P, EPP, 4], fp32, c)
            before_ = sb("before_", [P, 1], fp32, c)
            after_ = sb("after_", [P, 1], fp32, c)
            prev = sb("prev_b", [P, EPP], fp32, c)
            nxt = sb("nxt_b", [P, EPP], fp32, c)
            endm = sb("endm_b", [P, EPP], fp32, c)
            side = sb("side_b", [P, EPP], fp32, c)
            act_ = sb("sideact_b", [P, 1], fp32, c)
            t0 = sb("t0_b", [P, TP], fp32, c)
            t1 = sb("t1_b", [P, TP], fp32, c)
            cont = sb("cont_b", [P, 1], fp32, c)
            dg = sb("dg_b", [P, P], fp32, c)
            less = sb("less_b", [P, P], fp32, c)
            psr = pb("psr_b", [P, P], c)
            with nc.Block() as block:
                @block.sync
                def _(sp):
                    sp.wait_ge(s_set, 2)
                    sp.dma_start(rec[:, :, :], records.rearrange("(p t) f -> p t f", p=P)).then_inc(s_ld, 16)
                    byrow = records.rearrange("(p t) f -> p t f", p=P)
                    sp.dma_start(before_[1:P, :], byrow[0:P - 1, EPP - 1, 0:1], allow_slow_non_contiguous=True).then_inc(s_ld, 16)
                    sp.dma_start(after_[0:P - 1, :], byrow[1:P, 0, 0:1], allow_slow_non_contiguous=True).then_inc(s_ld, 16)

                @block.gpsimd
                def _(pool):
                    nc.gpsimd.affine_select(out=less[:, :], in_=ones[:, :], compare_op=ALU.is_gt, fill=0.0, base=0, pattern=[[1, P]], channel_multiplier=-1).then_inc(s_iota, 1)

                @block.tensor
                def _(pe):
                    pe.wait_ge(s_dg, 1)
                    nc.tensor.matmul(psr[:, :], ones[:, :], dg[:, :], start=True, stop=True).then_inc(s_row, 1)

                @block.vector
                def _(dve):
                    v = nc.vector
                    ch = Chain(dve, s_ch, 0)
                    A = slice(0, EPP)
                    v.memset(before_[:, :], -1.0).then_inc(s_set, 1)
                    v.memset(after_[:, :], -1.0).then_inc(s_set, 1)
                    for t in (sameb, leadb, weightb, t1):
                        ch.link(v.memset(t[:, :], 0.0))
                    dve.wait_ge(s_ld, 48)
                    dve.wait_ge(s_iota, 1)
                    src_ = rec[:, :, 0]
                    ch.link(v.tensor_copy(prev[:, 1:EPP], rec[:, 0:EPP - 1, 0]))
                    ch.link(v.tensor_copy(prev[:, 0:1], before_[:, :]))
                    ch.link(v.tensor_copy(nxt[:, 0:EPP - 1], rec[:, 1:EPP, 0]))
                    ch.link(v.tensor_copy(nxt[:, EPP - 1:EPP], after_[:, :]))
                    v.tensor_scalar(dg[:, :], ident[:, :], rec[:, 0, 0:1], None, ALU.mult).then_inc(s_dg, 1)
                    ch.link(v.tensor_copy(weightb[:, A], rec[:, :, 2]))
                    ch.link(v.tensor_copy(t1[:, A], rec[:, :, 1]))
                    ch.link(v.tensor_copy(dstb[:, :], t1[:, :]))
                    ch.link(v.tensor_tensor(sameb[:, 1:EPP], rec[:, 1:EPP, 0], prev[:, 1:EPP], ALU.is_equal))
                    ch.link(v.tensor_tensor(cont[:, :], rec[:, 0, 0:1], prev[:, 0:1], ALU.is_equal))
                    ch.link(v.tensor_tensor(endm[:, :], src_, nxt[:, :], ALU.not_equal))
                    ch.link(v.tensor_scalar(leadb[:, A], src_, rec[:, 0, 0:1], None, ALU.is_equal))
                    ch.link(v.scalar_tensor_tensor(side[:, :], endm[:, :], cont[:, 0:1], leadb[:, A], ALU.mult, ALU.mult))
                    ch.link(v.tensor_tensor(endm[:, :], endm[:, :], side[:, :], ALU.subtract))
                    ch.link(v.reduce_max(act_[:, :], side[:, :], AX.X))
                    ch.link(v.memset(t0[:, :], float(OUT_OF_RANGE)))
                    ch.link(v.tensor_scalar(t1[:, A], src_, float(OUT_OF_RANGE), None, ALU.subtract))
                    ch.link(v.tensor_tensor(prev[:, :], t1[:, A], endm[:, :], ALU.mult))
                    ch.link(v.tensor_tensor(t0[:, A], t0[:, A], prev[:, :], ALU.add))
                    ch.link(v.tensor_tensor(prev[:, 0:1], t1[:, 0:1], act_[:, :], ALU.mult))
                    ch.link(v.tensor_tensor(t0[:, SIDE:SIDE + 1], t0[:, SIDE:SIDE + 1], prev[:, 0:1], ALU.add))
                    ch.link(v.tensor_copy(outb[:, :], t0[:, :]))
                    dve.wait_ge(s_row, 1)
                    ch.link(v.scalar_tensor_tensor(mleftb[:, :], psr[:, :], rec[:, EPP - 1, 0:1], less[:, :], ALU.is_equal, ALU.mult))
            closing([s_ld, s_set, s_ch, s_iota, s_dg, s_row], c)

        with ExitStack() as c:
            X = sb("X0", [P, 2 * TS, D], fp32, c)
            acc = sb("acc0", [P, 2 * TS, D], fp32, c)
            cap = sb("cap0", [P, D], fp32, c)
            own = [sb(f"own0_{i}", [P, U, D], fp32, c) for i in range(2)]
            y = [sb(f"y0_{i}", [P, U, D], fp32, c) for i in range(2)]
            z = sb("z0", [P, U, D], fp32, c)
            res = [sb(f"res0_{i}", [P, U, D], fp32, c) for i in range(2)]
            xT = sb("xT0", [P, 3, TS * P], fp32, c)
            eT = sb("eT0", [P, 2, P], fp32, c)
            prod = sb("prod", [P, 2, R, D], fp32, c)
            msg = sb("msg", [P, 2, D], fp32, c)
            mring = sb("mring", [P, 2, 3, TS], i32, c)
            psT = [pb(f"psT{i}", [P, TS * P], c) for i in range(2)]
            psO = [pb(f"psO{i}", [P, TS * P], c) for i in range(2)]
            psY = [pb(f"psY{i}", [P, R * D], c) for i in range(2)]
            loaded = names("r0_", c, "own_loaded0", "own_loaded1")
            stored = names("r0_", c, "stored0", "stored1")
            rest_ = names("r0_", c, "indices_ready", "edge_transposed", "transposed", "edge_evacuated", "evacuated", "relations_done",
                          "relations_weighted", "message_ready", "cap_ready", "sum_ready", "product_ready", "relu_done", "back_chain",
                          "var1", "std1", "norm1", "applied1", "added", "var2", "std2", "norm2", "result_ready", "carry_ready", "cleared",
                          "map_copied")
            (s_idx, s_etr, s_tr, s_eev, s_ev, s_rel, s_relmul, s_msg, s_cap, s_sum, s_out, s_y, s_bch, s_var1, s_std1, s_norm1, s_app1,
             s_added, s_var2, s_std2, s_norm2, s_res, s_carry, s_set, s_mcp) = rest_
            GROUPS = (1, 2, 0)

            with nc.Block() as block:
                @block.sync
                def _(sp):
                    def load(s):
                        wait(sp, s_added, free(s, 1))
                        if isinstance(s.n, int) and (s.n + 1) * TN * P > N:
                            rest = max(0, N - s.n * TN * P) // TN
                            if rest:
                                src = a["x"][s.n * TN * P:N, :].rearrange("(p j) f -> p j f", j=TN)
                                for p0, p1 in ((0, rest // 16 * 16), (rest // 16 * 16, rest)):
                                    sp.dma_start(own[s.par][p0:p1, TS:U, :], src[p0:p1]).then_inc(loaded[s.par], 16)
                            return
                        src = a["x"][bass.ds(s.n * TN * P, TN * P), :].rearrange("(p j) f -> p j f", j=TN)
                        sp.dma_start(own[s.par][:, TS:U, :], src).then_inc(loaded[s.par], 16)

                    def store(s):
                        sp.wait_ge(s_res, s.n + 1)
                        sp.dma_start(node_rows(X1, s.n), res[s.par][:, TS:U, :]).then_inc(stored[s.par], 16)
                        sp.dma_start(slot_rows(X1, s.n), res[s.par][:, 0:TS, :]).then_inc(stored[s.par], 16)

                    pipelined(sp, [(store, 0), (load, 2)])
                    for i in range(2):
                        sp.wait_ge(stored[i], 32 * (STEPS // 2))

                @block.gpsimd
                def _(pool):
                    last_node, last_target = pool.to_reg(N - 1), pool.to_reg(NPAD - 1)
                    def fetch(s):
                        wait(pool, s_etr, free(s, TS))
                        nc.gpsimd.tensor_copy(idxr[:, s.par, 0:TS], srcidx[:, bass.ds(s.n * TS, TS)]).then_inc(s_idx, 1)
                        indices(pool, s_idx, s.n * 2 + 1)
                        for k in range(TS):
                            if not s.last:
                                gather(pool, X[:, s.par * TS + k, :], a["x"], idxr[:, s.par, k:k + 1], gath[s.par * TS + k], last_node)
                        wait(pool, s_added, free(s, 1))
                        nc.gpsimd.tensor_copy(idxr[:, s.par, TS:2 * TS], ownidx[:, bass.ds(s.n * TS, TS)]).then_inc(s_idx, 1)
                        indices(pool, s_idx, s.n * 2 + 2)
                        for k in range(TS):
                            gather(pool, own[s.par][:, k, :], a["x"], idxr[:, s.par, TS + k:TS + k + 1], ogath[s.par * TS + k], last_node)

                    pipelined(pool, [(fetch, 2)])

                    def enter(s):
                        wait(pool, s_mv[s.par], (s.n - s.par) * 8 * TS)
                        nc.gpsimd.tensor_copy(mring[:, s.par, 0, :], endidx[:, bass.ds(s.n * TS, TS)]).then_inc(s_mcp, 1)
                        nc.gpsimd.tensor_copy(mring[:, s.par, 1, :], endrow[:, bass.ds(s.n * TS, TS)]).then_inc(s_mcp, 1)
                        indices(pool, s_mcp, s.n * 2 + 2)
                        for k in range(TS):
                            pool.indirect_dma_start(out=row_of_node, out_offset=bass.IndirectOffsetOnAxis(ap=mring[:, s.par, 0, k:k + 1], axis=0),
                                                    in_=mring[:, s.par, 1, k:k + 1], in_offset=None, bounds_check=last_target, oob_is_err=False).then_inc(s_mv[s.par], 16)

                    def each(part, first, steps):
                        for n in (0, 1):
                            part(Step(first + n, n))
                        with pool.Fori(1, steps // 2) as i:
                            for n in (0, 1):
                                part(Step(i * 2 + first + n, n))

                    each(enter, 0, STEPS)
                    for i in range(2):
                        pool.wait_ge(s_mv[i], 16 * TS * (STEPS // 2))

                    def look_up(s):
                        pool.wait_ge(s_mv[s.par], (s.n - s.par + STEPS) * 8 * TS)
                        if not (isinstance(s.n, int) and s.n < 2):
                            nc.gpsimd.tensor_copy(gidx[:, bass.ds(s.n * TS - 2 * TS, TS)], mring[:, s.par, 2, :]).then_inc(s_mcp, 1)
                        else:
                            nc.gpsimd.tensor_copy(mring[:, s.par, 2, :], mring[:, s.par, 1, :]).then_inc(s_mcp, 1)
                        nc.gpsimd.tensor_copy(mring[:, s.par, 0, :], srcidx[:, bass.ds(s.n * TS, TS)]).then_inc(s_mcp, 1)
                        indices(pool, s_mcp, s.n * 2 + 2 * STEPS + 2)
                        for k in range(TS):
                            gather(pool, mring[:, s.par, 2, k:k + 1], row_of_node, mring[:, s.par, 0, k:k + 1], s_mv[s.par], last_target)

                    each(look_up, 0, STEPS)
                    for i in range(2):
                        pool.wait_ge(s_mv[i], 32 * TS * (STEPS // 2))
                        nc.gpsimd.tensor_copy(gidx[:, (STEPS - 2 + i) * TS:(STEPS - 1 + i) * TS], mring[:, i, 2, :]).then_inc(s_mcp, 1)

                @block.tensor
                def _(pe):
                    t = nc.tensor

                    def relations(s, k):
                        pe.wait_ge(s_eev, s.n * TS + k + 1)
                        wait(pe, s_relmul, s.n * TS + k - 1)
                        for half in range(2):
                            m = t.matmul(psY[k % 2][:, half * 512:(half + 1) * 512], eT[:, k % 2, :],
                                         wrel[:, half * 4:half * 4 + 4, :], start=True, stop=True)
                        m.then_inc(s_rel, 1)

                    def edges(s):
                        if s.last:
                            pe.wait_ge(s_sum, EPP)
                            pe.wait_ge(s_relmul, EPP)
                            t.matmul(psY[0][:, 0:P], mleft[:, :], acc[:, (SIDE - 1) % (2 * TS), :], start=True, stop=True).then_inc(s_carry, 1)
                            return
                        for k in range(TS):
                            edge_rows(pe, s, k)
                            wait(pe, s_eev, s.n * TS + k)
                            t.transpose(psT[0][:, 0:P], X[:, s.par * TS + k, :], ident[:, :]).then_inc(s_etr, 1)
                            relations(s, k)

                    def product(s, q):
                        u = s.n * 3 + q
                        ps = psO[(s.par + q) % 2]
                        pe.wait_ge(s_ev, u + 1)
                        wait(pe, s_y, u - 1)
                        t.matmul(ps[:, :], ones[0:1, :], biases["L0_gnn_b_self"][0:1, :, :], start=True, stop=False)
                        if q == 2:
                            pe.wait_ge(s_sum, s.n * TS + TS)
                        for j in range(TS):
                            if q == 2:
                                t.matmul(ps[:, j * P:(j + 1) * P], ident[:, :], acc[:, s.par * TS + j, :], start=False, stop=False)
                            m = t.matmul(ps[:, j * P:(j + 1) * P], xT[:, q, j * P:(j + 1) * P], wself[:, :], start=False, stop=j == TS - 1)
                        m.then_inc(s_out, 1)

                    def nodes(s):
                        for q, g in enumerate(GROUPS):
                            wait(pe, s_ev, s.n * 3 + q)
                            if g == 0:
                                for k in range(TS):
                                    pe.wait_ge(ogath[s.par * TS + k], placed[s.par * TS + k] + arrived(s))
                            elif g == 1 and not s.last:
                                pe.wait_ge(loaded[s.par], arrived(s) + (16 if isinstance(s.n, int) and s.n == STEPS - 2 else 0))
                            for j in range(TS):
                                m = t.transpose(psT[1][:, j * P:(j + 1) * P], own[s.par][:, g * TS + j, :], ident[:, :])
                            m.then_inc(s_tr, 1)
                            product(s, q)

                    pipelined(pe, [(edges, 1), (nodes, 1)])

                @block.scalar
                def _(act):
                    sc = nc.scalar

                    def edges(s):
                        if s.last:
                            return
                        for k in range(TS):
                            n = s.n * TS + k
                            act.wait_ge(s_etr, n + 1)
                            wait(act, s_rel, n - 1)
                            sc.copy(eT[:, k % 2, :], psT[0][:, 0:P]).then_inc(s_eev, 1)

                    def nodes(s):
                        for q, g in enumerate(GROUPS):
                            u = s.n * 3 + q
                            act.wait_ge(s_tr, u + 1)
                            wait(act, s_out, u - 2)
                            sc.copy(xT[:, q, :], psT[1][:, :]).then_inc(s_ev, 1)
                            act.wait_ge(s_out, u + 1)
                            sc.activation(y[s.par][:, g * TS:(g + 1) * TS, :], psO[(s.par + q) % 2][:, :], ACT.Relu).then_inc(s_y, 1)

                    def first_norm(s):
                        deviate(act, s, 0, 0, s_var1, s_std1)
                        normalize(act, s, 0, y[s.par], z, 0, s_norm1, s_app1)

                    def second_norm(s):
                        deviate(act, s, 1, 0, s_var2, s_std2)
                        wait(act, stored[s.par], (s.n - s.par) * 16)
                        normalize(act, s, 1, z, res[s.par], 0, s_norm2, s_res)

                    pipelined(act, [(edges, 1), (first_norm, 0), (nodes, 1), (second_norm, 0)])

                @block.vector
                def _(dve):
                    v = nc.vector
                    v.memset(acc[:, :, :], 0.0).then_inc(s_set, 1)
                    v.memset(cap[:, :], 0.0).then_inc(s_set, 1)
                    dve.wait_ge(s_set, 2)
                    ch = Chain(dve, s_bch, 2 * (U + LN_LINKS) + 2)

                    def edges(s):
                        wait(dve, s_out, free(s, 3))
                        if s.last:
                            side_sums(acc, cap, psY[0][:, 0:P], s_sum, s_carry, dve)
                            return
                        for k in range(TS):
                            n = s.n * TS + k
                            dve.wait_ge(s_rel, n + 1)
                            w = coef[:, bass.ds(n, 1), :].rearrange("p a r -> p (a r)").unsqueeze(2).to_broadcast([P, R, D])
                            v.tensor_tensor(prod[:, k % 2, :, :], psY[k % 2][:, :].rearrange("p (r f) -> p r f", r=R), w, ALU.mult).then_inc(s_relmul, 1)
                            dve.wait_ge(s_relmul, n + 1)
                            v.reduce_sum(msg[:, k % 2, :], prod[:, k % 2, :, :].rearrange("p r f -> p f r"), AX.X).then_inc(s_msg, 1)
                            dve.wait_ge(s_msg, n + 1)
                            scan_edge(s, k, msg[:, k % 2, :], acc, cap, s_sum, s_cap, dve)

                    def first_norm(s):
                        ch.begin(s)
                        dve.wait_ge(s_y, s.n * 3 + 3)
                        normalizing(dve, ch, s, 0, y[s.par], 0, s_var1, s_std1, s_norm1)

                    def second_norm(s):
                        dve.wait_ge(s_app1, s.n + 1)
                        ch.link(v.tensor_tensor(z[:, :, :], z[:, :, :], spread(rows["L0_gnn_gamma"], U), ALU.mult))
                        ch.link(v.tensor_tensor(z[:, :, :], z[:, :, :], spread(rows["L0_gnn_beta"], U), ALU.add))
                        v.tensor_tensor(z[:, :, :], z[:, :, :], own[s.par][:, :, :], ALU.add).then_inc(s_added, 1)
                        dve.wait_ge(s_added, s.n + 1)
                        normalizing(dve, ch, s, 1, z, 0, s_var2, s_std2, s_norm2)

                    pipelined(dve, [(edges, 1), (first_norm, 0), (second_norm, 0)])
            edges_gathered()
            slots_moved()
            closing([*loaded, *stored, *rest_], c)

        for k_, (src_table, dst_table) in enumerate(((X1, H1), (H1, X2))):
            c = ExitStack()
            with c:
                pre = f"r{k_ + 1}_"
                X = sb(pre + "X", [P, 2 * TS, D], fp32, c)
                acc = sb(pre + "acc", [P, 2 * TS, D], fp32, c)
                cap = sb(pre + "cap", [P, D], fp32, c)
                own = [sb(pre + f"own{i}", [P, U, D], fp32, c) for i in range(2)]
                old = [sb(pre + f"old{i}", [P, U, D], fp32, c) for i in range(2)] if k_ else None
                y = [sb(pre + f"y{i}", [P, U, D], fp32, c) for i in range(2)]
                z = sb(pre + "z", [P, U, D], fp32, c)
                res = [sb(pre + f"res{i}", [P, U, D], fp32, c) for i in range(2)]
                xT = sb(pre + "xT", [P, 4, TS * P], fp32, c)
                psT = [pb(pre + f"psT{i}", [P, TS * P], c) for i in range(2)]
                psO = [pb(pre + f"psO{i}", [P, TS * P], c) for i in range(2)]
                psC = pb(pre + "psC", [P, D], c)
                loaded = names(pre, c, "own_loaded0", "own_loaded1")
                stored = names(pre, c, "stored0", "stored1")
                rest_ = names(pre, c, "indices_ready", "transposed", "evacuated", "edge_weighted", "cap_ready", "sum_ready", "product_ready",
                              "y_ready", "back_chain", "var1", "std1", "norm1", "applied1", "scaled", "var2", "std2", "norm2", "result_ready",
                              "carry_ready", "cleared")
                (s_idx, s_tr, s_ev, s_wtd, s_cap, s_sum, s_out, s_y, s_bch, s_var1, s_std1, s_norm1, s_app1, s_scaled, s_var2, s_std2,
                 s_norm2, s_res, s_carry, s_set) = rest_
                NL = 32 * (1 + k_)
                ORDER = (1, 2, 0)
                TQ = 4

                with nc.Block() as block:
                    @block.sync
                    def _(sp):
                        def load(s):
                            wait(sp, s_tr, free(s, TQ))
                            sp.dma_start(own[s.par][:, TS:U, :], node_rows(src_table, s.n)).then_inc(loaded[s.par], 16)
                            sp.dma_start(own[s.par][:, 0:TS, :], slot_rows(src_table, s.n)).then_inc(loaded[s.par], 16)
                            if k_:
                                wait(sp, s_scaled, free(s, 1))
                                sp.dma_start(old[s.par][:, TS:U, :], node_rows(X1, s.n)).then_inc(loaded[s.par], 16)
                                sp.dma_start(old[s.par][:, 0:TS, :], slot_rows(X1, s.n)).then_inc(loaded[s.par], 16)

                        def store(s):
                            sp.wait_ge(s_res, s.n + 1)
                            sp.dma_start(node_rows(dst_table, s.n), res[s.par][:, TS:U, :]).then_inc(stored[s.par], 16)
                            sp.dma_start(slot_rows(dst_table, s.n), res[s.par][:, 0:TS, :]).then_inc(stored[s.par], 16)

                        pipelined(sp, [(store, 0), (load, 2)])
                        for i in range(2):
                            sp.wait_ge(stored[i], 32 * (STEPS // 2))

                    @block.gpsimd
                    def _(pool):
                        last_row = pool.to_reg(src_table.shape[0] - 1)
                        def fetch(s):
                            if s.last:
                                return
                            wait(pool, s_sum, free(s, TS))
                            wait(pool, s_cap, free(s, TS))
                            nc.gpsimd.tensor_copy(idxr[:, s.par, 0:TS], gidx[:, bass.ds(s.n * TS, TS)]).then_inc(s_idx, 1)
                            indices(pool, s_idx, s.n + 1)
                            for k in range(TS):
                                gather(pool, X[:, s.par * TS + k, :], src_table, idxr[:, s.par, k:k + 1], gath[s.par * TS + k], last_row)

                        pipelined(pool, [(fetch, 2)])

                    @block.tensor
                    def _(pe):
                        t = nc.tensor

                        def nodes(s):
                            for q, g in enumerate(ORDER):
                                wait(pe, s_ev, s.n * TQ + q - 1)
                                if q == 0:
                                    pe.wait_ge(loaded[s.par], (s.n - s.par) * (NL // 2) + NL)
                                for j in range(TS):
                                    m = t.transpose(psT[q % 2][:, j * P:(j + 1) * P], own[s.par][:, g * TS + j, :], ident[:, :])
                                m.then_inc(s_tr, 1)
                            if s.last:
                                pe.wait_ge(s_sum, EPP)
                                t.matmul(psC[:, :], mleft[:, :], acc[:, (SIDE - 1) % (2 * TS), :], start=True, stop=True).then_inc(s_carry, 1)
                            pe.wait_ge(s_sum, s.n * TS + TS)
                            pe.wait_ge(s_ev, s.n * TQ + 2)
                            for j in range(TS):
                                m = t.transpose(psT[1][:, j * P:(j + 1) * P], acc[:, s.par * TS + j, :], ident[:, :])
                            m.then_inc(s_tr, 1)
                            for q, g in enumerate(ORDER):
                                u = s.n * 3 + q
                                ps = psO[(s.par + q) % 2]
                                pe.wait_ge(s_ev, s.n * TQ + (q + 1 if g else TQ))
                                wait(pe, s_y, u - 1)
                                t.matmul(ps[:, :], ones[0:1, :], biases[f"L1_gnn_b_l{k_}"][0:1, :, :], start=True, stop=False)
                                for j in range(TS):
                                    if g == 0:
                                        t.matmul(ps[:, j * P:(j + 1) * P], xT[:, 3, j * P:(j + 1) * P], wsage[:, 2 * k_, :], start=False, stop=False)
                                    m = t.matmul(ps[:, j * P:(j + 1) * P], xT[:, q, j * P:(j + 1) * P], wsage[:, 2 * k_ + 1, :], start=False, stop=j == TS - 1)
                                m.then_inc(s_out, 1)

                        pipelined(pe, [(nodes, 1)])

                    @block.scalar
                    def _(act):
                        sc = nc.scalar

                        def edges(s):
                            if s.last:
                                return
                            for k in range(TS):
                                edge_rows(act, s, k)
                                sc.activation(X[:, s.par * TS + k, :], X[:, s.par * TS + k, :], ACT.Copy, scale=rdeg[:, bass.ds(s.n * TS + k, 1)]).then_inc(s_wtd, 1)

                        def nodes(s):
                            for q in range(TQ):
                                act.wait_ge(s_tr, s.n * TQ + q + 1)
                                wait(act, s_out, s.n * 3 + (q - 2 if q < 3 else 0))
                                sc.copy(xT[:, q, :], psT[q % 2][:, :]).then_inc(s_ev, 1)
                            for q, g in enumerate(ORDER):
                                act.wait_ge(s_out, s.n * 3 + q + 1)
                                sc.copy(y[s.par][:, g * TS:(g + 1) * TS, :], psO[(s.par + q) % 2][:, :]).then_inc(s_y, 1)

                        def first_norm(s):
                            deviate(act, s, 0, 0, s_var1, s_std1)
                            normalize(act, s, 0, y[s.par], z, 0, s_norm1, s_app1)

                        def finish(s):
                            wait(act, stored[s.par], (s.n - s.par) * 16)
                            if k_:
                                deviate(act, s, 1, 0, s_var2, s_std2)
                                normalize(act, s, 1, z, res[s.par], 0, s_norm2, s_res)
                            else:
                                act.wait_ge(s_scaled, s.n + 1)
                                sc.activation(res[s.par][:, :, :], z[:, :, :], ACT.Relu).then_inc(s_res, 1)

                        pipelined(act, [(edges, 1), (first_norm, 0), (nodes, 1), (finish, 0)])

                    @block.vector
                    def _(dve):
                        v = nc.vector
                        v.memset(acc[:, :, :], 0.0).then_inc(s_set, 1)
                        v.memset(cap[:, :], 0.0).then_inc(s_set, 1)
                        dve.wait_ge(s_set, 2)
                        ch = Chain(dve, s_bch, (1 + k_) * (U + LN_LINKS) + 1 + k_)

                        def edges(s):
                            wait(dve, s_tr, free(s, TQ))
                            if s.last:
                                side_sums(acc, cap, psC[:, :], s_sum, s_carry, dve)
                                return
                            for k in range(TS):
                                dve.wait_ge(s_wtd, s.n * TS + k + 1)
                                scan_edge(s, k, X[:, s.par * TS + k, :], acc, cap, s_sum, s_cap, dve)

                        def first_norm(s):
                            ch.begin(s)
                            dve.wait_ge(s_y, s.n * 3 + 3)
                            normalizing(dve, ch, s, 0, y[s.par], 0, s_var1, s_std1, s_norm1)

                        def second_norm(s):
                            dve.wait_ge(s_app1, s.n + 1)
                            ch.link(v.tensor_tensor(z[:, :, :], z[:, :, :], spread(rows[f"L1_gnn_gamma{k_}"], U), ALU.mult))
                            if not k_:
                                v.tensor_tensor(z[:, :, :], z[:, :, :], spread(rows["L1_gnn_beta0"], U), ALU.add).then_inc(s_scaled, 1)
                                return
                            ch.link(v.tensor_tensor(z[:, :, :], z[:, :, :], spread(rows["L1_gnn_beta1"], U), ALU.add))
                            v.scalar_tensor_tensor(z[:, :, :], z[:, :, :], 0.0, old[s.par][:, :, :], ALU.max, ALU.add).then_inc(s_scaled, 1)
                            dve.wait_ge(s_scaled, s.n + 1)
                            normalizing(dve, ch, s, 1, z, 0, s_var2, s_std2, s_norm2)

                        pipelined(dve, [(first_norm, 0), (edges, 1), (second_norm, 0)])
                edges_gathered()
                closing([*loaded, *stored, *rest_], c)

        with ExitStack() as c:
            buf = sb("x2buf", [P, 2 * TS, D], fp32, c)
            loaded = names("x2_", c, "loaded0", "loaded1")
            (s_idx,) = names("x2_", c, "indices_ready")
            with nc.Block() as block:
                @block.sync
                def _(sp):
                    def load(s):
                        if not (isinstance(s.n, int) and s.n < 2):
                            for k in range(TS):
                                slot_rows_free(sp, s, k)
                        sp.dma_start(buf[:, s.par * TS:(s.par + 1) * TS, :], slot_rows(X2, s.n)).then_inc(loaded[s.par], 16)

                    pipelined(sp, [(load, 2)])

                @block.gpsimd
                def _(pool):
                    last_node = pool.to_reg(N - 1)

                    def scatter(s):
                        row_numbers_free(pool, s)
                        nc.gpsimd.tensor_copy(idxr[:, s.par, 0:TS], outidx[:, bass.ds(s.n * TS, TS)]).then_inc(s_idx, 1)
                        pool.wait_ge(loaded[s.par], arrived(s))
                        indices(pool, s_idx, s.n + 1)
                        for k in range(TS):
                            scatter_rows(pool, X2[0:NPAD, :], buf[:, s.par * TS + k, :], idxr[:, s.par, k:k + 1], ogath[s.par * TS + k], last_node)

                    pipelined(pool, [(scatter, 0)])
                    for k in range(2 * TS):
                        pool.wait_ge(ogath[k], placed[k] + 8 * STEPS)
            slots_moved()
            closing([*loaded, s_idx], c)

        for k_, (src_table, sum_table) in enumerate(((X2, E1), (E1, E2), (E2, E3))):
            c = ExitStack()
            with c:
                pre = f"r{k_ + 3}_"
                X = sb(pre + "X", [P, 2 * TS, D], fp32, c)
                acc = sb(pre + "acc", [P, 2 * TS, D], fp32, c)
                cap = sb(pre + "cap", [P, D], fp32, c)
                psC = pb(pre + "psC", [P, D], c)
                rest_ = names(pre, c, "indices_ready", "targets_ready", "edge_weighted", "cap_ready", "sum_ready", "carry_ready", "cleared")
                s_idx, s_out, s_wtd, s_cap, s_sum, s_carry, s_set = rest_

                with nc.Block() as block:
                    @block.gpsimd
                    def _(pool):
                        last_node, last_row = pool.to_reg(N - 1), pool.to_reg(NPAD - 1)

                        def fetch(s):
                            if s.last:
                                return
                            wait(pool, s_cap, free(s, TS))
                            nc.gpsimd.tensor_copy(idxr[:, s.par, 0:TS], dstb[:, bass.ds(s.n * TS, TS)]).then_inc(s_idx, 1)
                            indices(pool, s_idx, s.n + 1)
                            for k in range(TS):
                                gather(pool, X[:, s.par * TS + k, :], src_table[0:NPAD, :], idxr[:, s.par, k:k + 1], gath[s.par * TS + k], last_row)

                        def scatter(s):
                            row_numbers_free(pool, s)
                            nc.gpsimd.tensor_copy(idxr[:, s.par, TS:2 * TS], outb[:, bass.ds(s.n * TS, TS)]).then_inc(s_out, 1)
                            pool.wait_ge(s_sum, s.n * TS + TS)
                            indices(pool, s_out, s.n + 1)
                            for k in range(TS):
                                scatter_rows(pool, sum_table, acc[:, s.par * TS + k, :], idxr[:, s.par, TS + k:TS + k + 1], ogath[s.par * TS + k], last_node)

                        pipelined(pool, [(fetch, 2), (scatter, 0)])
                        for k in range(2 * TS):
                            pool.wait_ge(ogath[k], placed[k] + 8 * STEPS)

                    @block.tensor
                    def _(pe):
                        pe.wait_ge(s_sum, EPP)
                        nc.tensor.matmul(psC[:, :], mleftb[:, :], acc[:, (SIDE - 1) % (2 * TS), :], start=True, stop=True).then_inc(s_carry, 1)

                    @block.scalar
                    def _(act):
                        def edges(s):
                            if s.last:
                                return
                            for k in range(TS):
                                edge_rows(act, s, k)
                                nc.scalar.activation(X[:, s.par * TS + k, :], X[:, s.par * TS + k, :], ACT.Copy, scale=weightb[:, bass.ds(s.n * TS + k, 1)]).then_inc(s_wtd, 1)

                        pipelined(act, [(edges, 0)])

                    @block.vector
                    def _(dve):
                        v = nc.vector
                        v.memset(acc[:, :, :], 0.0).then_inc(s_set, 1)
                        v.memset(cap[:, :], 0.0).then_inc(s_set, 1)
                        dve.wait_ge(s_set, 2)

                        def edges(s):
                            if not (isinstance(s.n, int) and s.n < 2):
                                for k in range(TS):
                                    slot_rows_free(dve, s, k)
                            if s.last:
                                side_sums(acc, cap, psC[:, :], s_sum, s_carry, dve)
                                return
                            for k in range(TS):
                                dve.wait_ge(s_wtd, s.n * TS + k + 1)
                                scan_edge(s, k, X[:, s.par * TS + k, :], acc, cap, s_sum, s_cap, dve, sameb, leadb)

                        pipelined(dve, [(edges, 0)])
                edges_gathered()
                slots_moved()
                closing(rest_, c)

        for k_ in range(3):
            c = ExitStack()
            with c:
                pre = f"n{k_}_"
                node_table, lin_table = ((X2, T1), (T1, T2), (T2, T3))[k_]
                TQ = TN // TS
                W = node_table.shape[1]
                nin = [sb(pre + f"nodes{i}", [P, TN, W], fp32, c) for i in range(2)]
                sums = [sb(pre + f"sums{i}", [P, 3, TN, D], fp32, c) for i in range(2)] if k_ == 0 else None
                z = sb(pre + "z", [P, TN, D], fp32, c) if k_ == 0 else None
                res = [sb(pre + f"res{i}", [P, TN, D], fp32, c) for i in range(2)] if k_ == 0 else None
                tout = [sb(pre + f"tout{i}", [P, TQ * TS, TW], fp32, c) for i in range(2)]
                xT = sb(pre + "xT", [P, TQ, TS * P], fp32, c)
                psT = [pb(pre + f"psT{i}", [P, TS * P], c) for i in range(2)]
                psG = [pb(pre + f"psG{i}", [P, 2, 512], c) for i in range(2)]
                loaded = names(pre, c, "nodes_loaded0", "nodes_loaded1")
                stored_res = names(pre, c, "results_stored0", "results_stored1")
                stored_lin = names(pre, c, "products_stored0", "products_stored1")
                rest_ = names(pre, c, "transposed", "evacuated", "product_ready", "product_evacuated", "chain", "var", "std", "norm",
                              "normalized", "combined")
                s_tr, s_ev, s_out, s_lin, s_bch, s_var, s_std, s_norm, s_res, s_comb = rest_
                NL = 64 if k_ == 0 else 16

                def store_counts(s, each):
                    return (s.n - s.par) * (each // 2)

                with nc.Block() as block:
                    @block.sync
                    def _(sp):
                        def load(s):
                            if k_ == 0:
                                wait(sp, s_comb, free(s, 1))
                            else:
                                wait(sp, s_tr, free(s, TQ))
                            sp.dma_start(nin[s.par][:, :, :], node_rows(node_table, s.n)).then_inc(loaded[s.par], 16)
                            if k_ == 0:
                                for i, t in enumerate((E1, E2, E3)):
                                    sp.dma_start(sums[s.par][:, i, :, :], node_rows(t, s.n)).then_inc(loaded[s.par], 16)

                        def store_results(s):
                            sp.wait_ge(s_res, s.n + 1)
                            sp.dma_start(node_rows(X3, s.n), res[s.par][:, :, :]).then_inc(stored_res[s.par], 16)

                        def store_products(s):
                            sp.wait_ge(s_lin, s.n * TQ + TQ)
                            sp.dma_start(node_rows(lin_table, s.n), tout[s.par][:, 0:TN, :]).then_inc(stored_lin[s.par], 16)

                        if k_ == 0:
                            pipelined(sp, [(load, 2), (store_results, 0), (store_products, -1)])
                        else:
                            pipelined(sp, [(load, 2), (store_products, -1)])
                        for i in range(2):
                            if k_ == 0:
                                sp.wait_ge(stored_res[i], 16 * (STEPS // 2))
                            sp.wait_ge(stored_lin[i], 16 * (STEPS // 2))

                    def evacuate(eng, copy, s, q):
                        eng.wait_ge(s_out, s.n * TQ + q + 1)
                        if q == 0:
                            wait(eng, stored_lin[s.par], store_counts(s, 16))
                        copy(tout[s.par][:, q * TS:(q + 1) * TS, :].rearrange("p (b j) f -> p b (j f)", b=2),
                             psG[(s.par * TQ + q) % 2][:, :, 0:2 * TW]).then_inc(s_lin, 1)

                    @block.tensor
                    def _(pe):
                        t = nc.tensor

                        def nodes(s):
                            for q in range(TQ):
                                u = s.n * TQ + q
                                wait(pe, s_ev, u - 1)
                                if q == 0 and k_:
                                    pe.wait_ge(loaded[s.par], arrived(s))
                                elif q == 0:
                                    pe.wait_ge(s_res, s.n + 1)
                                for j in range(TS):
                                    tile = res[s.par][:, q * TS + j, :] if k_ == 0 else nin[s.par][:, q * TS + j, 0:D]
                                    m = t.transpose(psT[(s.par * TQ + q) % 2][:, j * P:(j + 1) * P], tile, ident[:, :])
                                m.then_inc(s_tr, 1)
                            for q in range(TQ):
                                u = s.n * TQ + q
                                pe.wait_ge(s_ev, u + 1)
                                wait(pe, s_lin, u - 1)
                                for j in range(TS):
                                    m = t.matmul(psG[(s.par * TQ + q) % 2][:, j // 2, j % 2 * TW:(j % 2 + 1) * TW],
                                                 xT[:, q, j * P:(j + 1) * P], wgat[:, k_, :], start=True, stop=True)
                                m.then_inc(s_out, 1)

                        pipelined(pe, [(nodes, 0)])

                    @block.scalar
                    def _(act):
                        sc = nc.scalar

                        def norm(s):
                            deviate(act, s, 0, 0, s_var, s_std, TN, 0.25)
                            wait(act, stored_res[s.par], store_counts(s, 16))
                            wait(act, s_tr, free(s, TQ))
                            normalize(act, s, 0, z, res[s.par], 0, s_norm, s_res, TN)

                        def transposes(s):
                            for q in range(TQ):
                                u = s.n * TQ + q
                                act.wait_ge(s_tr, u + 1)
                                wait(act, s_out, u - TQ + 1)
                                dst, bank = xT[:, q, :], psT[(s.par * TQ + q) % 2]
                                if k_:
                                    sc.activation(dst, bank[:, :], ACT.Relu, bias=gatbias[:, k_ - 1:k_]).then_inc(s_ev, 1)
                                else:
                                    sc.copy(dst, bank[:, :]).then_inc(s_ev, 1)

                        def products(s):
                            for q in range(TQ):
                                evacuate(act, sc.copy, s, q)

                        if k_ == 0:
                            pipelined(act, [(norm, 0), (transposes, 0)])
                        else:
                            pipelined(act, [(transposes, 0), (products, -1)])

                    if k_ == 0:
                        @block.vector
                        def _(dve):
                            v = nc.vector
                            ch = Chain(dve, s_bch, TN + LN_LINKS + 3)

                            def norm(s):
                                ch.begin(s)
                                dve.wait_ge(loaded[s.par], (s.n - s.par) * (NL // 2) + NL)
                                wait(dve, s_res, s.n)
                                ch.link(v.tensor_tensor(z[:, :, :], sums[s.par][:, 0, :, :], sums[s.par][:, 1, :, :], ALU.add))
                                ch.link(v.tensor_tensor(z[:, :, :], z[:, :, :], sums[s.par][:, 2, :, :], ALU.add))
                                v.scalar_tensor_tensor(z[:, :, :], nin[s.par][:, :, :], 5.0, z[:, :, :], ALU.mult, ALU.add).then_inc(s_comb, 1)
                                dve.wait_ge(s_comb, s.n + 1)
                                normalizing(dve, ch, s, 0, z, 0, s_var, s_std, s_norm, TN, 0.25)

                            def products(s):
                                for q in range(TQ):
                                    evacuate(dve, v.tensor_copy, s, q)

                            pipelined(dve, [(norm, 0), (products, -1)])
                closing([*loaded, *stored_res, *stored_lin, *rest_], c)

        with ExitStack() as c:
            rows_t = sb("own_t", [P, 2 * TS, TW], fp32, c)
            rows_x = sb("own_x", [P, 2 * TS, D], fp32, c)
            stored = names("own_", c, "stored0", "stored1")
            s_idx, s_own = names("own_", c, "indices_ready", "scores_kept")
            with nc.Block() as block:
                @block.gpsimd
                def _(pool):
                    last_row = pool.to_reg(NPAD - 1)

                    def fetch(s):
                        wait(pool, stored[s.par], (s.n - s.par) * 16)
                        wait(pool, s_own, free(s, 1))
                        nc.gpsimd.tensor_copy(idxr[:, s.par, 0:TS], ownidx[:, bass.ds(s.n * TS, TS)]).then_inc(s_idx, 1)
                        indices(pool, s_idx, s.n + 1)
                        for k in range(TS):
                            i, at = s.par * TS + k, idxr[:, s.par, k:k + 1]
                            gather(pool, rows_t[:, i, :], T1[0:NPAD, :], at, ogath[i], last_row)
                            gather(pool, rows_x[:, i, :], X3[0:NPAD, :], at, ogath[i], last_row)

                    pipelined(pool, [(fetch, 2)])

                def both_moved(eng, s):
                    for k in range(TS):
                        eng.wait_ge(ogath[s.par * TS + k], placed[s.par * TS + k] + (s.n - s.par) * 16 + 32)

                @block.sync
                def _(sp):
                    def store(s):
                        both_moved(sp, s)
                        sp.dma_start(slot_rows(T1, s.n), rows_t[:, s.par * TS:(s.par + 1) * TS, :]).then_inc(stored[s.par], 16)
                        sp.dma_start(slot_rows(X3, s.n), rows_x[:, s.par * TS:(s.par + 1) * TS, :]).then_inc(stored[s.par], 16)

                    pipelined(sp, [(store, 0)])
                    for i in range(2):
                        sp.wait_ge(stored[i], 32 * (STEPS // 2))

                @block.vector
                def _(dve):
                    def keep(s):
                        both_moved(dve, s)
                        nc.vector.tensor_copy(ownal[:, bass.ds(s.n * TS, TS), :], rows_t[:, s.par * TS:(s.par + 1) * TS, D:TW]).then_inc(s_own, 1)

                    pipelined(dve, [(keep, 0)])
            slots_moved()
            slots_moved()
            closing([*stored, s_idx, s_own], c)

        xrow = sb("xrow", [P, EPP, TW])
        pself = sb("pself", [P, TP, H])
        for k_ in range(3):
            pre = f"r{k_ + 6}_"
            table, next_table = ((T1, T2), (T2, T3), (T3, None))[k_]
            HH = (H, H, 1)[k_]
            CH = D // HH
            W = D + HH
            c = ExitStack()
            with c:
                FIN = k_ == 0
                nin = [sb(f"fin_nodes{i}", [P, TN, TW], fp32, c) for i in range(2)] if FIN else None
                x3in = [sb(f"fin_x3{i}", [P, TN, D], fp32, c) for i in range(2)] if FIN else None
                y = [sb(f"fin_y{i}", [P, TN, D], fp32, c) for i in range(2)] if FIN else None
                z = sb("fin_z", [P, TN, D], fp32, c) if FIN else None
                loaded = names(pre, c, "nodes_loaded0", "nodes_loaded1")
                stored = names(pre, c, "out_stored0", "out_stored1")
                rest_ = names(pre, c, "biased", "chain", "var1", "std1", "norm1", "normalized", "added", "var2", "std2", "norm2", "result_ready")
                s_y, s_bch, s_var1, s_std1, s_norm1, s_app1, s_added, s_var2, s_std2, s_norm2, s_res = rest_

                with nc.Block() as block:
                    @block.gpsimd
                    def _(pool):
                        last_row = pool.to_reg(table.shape[0] - 1)
                        for t in range(EPP):
                            gather(pool, xrow[:, t, :], table, (gidx if k_ else srcidx)[:, t:t + 1], gath[t % (2 * TS)], last_row)
                        for k in range(2 * TS):
                            pool.wait_ge(gath[k], before[k] + 16 * len(range(k, EPP, 2 * TS)))

                    if FIN:
                        @block.sync
                        def _(sp):
                            def load(s):
                                wait(sp, s_y, free(s, 1))
                                sp.dma_start(nin[s.par][:, :, :], node_rows(T3, s.n)).then_inc(loaded[s.par], 16)
                                wait(sp, s_added, free(s, 1))
                                sp.dma_start(x3in[s.par][:, :, :], node_rows(X3, s.n)).then_inc(loaded[s.par], 16)

                            def store(s):
                                sp.wait_ge(s_res, s.n + 1)
                                if isinstance(s.n, int) and (s.n + 1) * TN * P > N:
                                    rest = max(0, N - s.n * TN * P) // TN
                                    if rest:
                                        dst = out[s.n * TN * P:N, :].rearrange("(p j) f -> p j f", j=TN)
                                        for p0, p1 in ((0, rest // 16 * 16), (rest // 16 * 16, rest)):
                                            sp.dma_start(dst[p0:p1], y[s.par][p0:p1, :, :]).then_inc(stored[s.par], 16)
                                    return
                                dst = out[bass.ds(s.n * TN * P, TN * P), :].rearrange("(p j) f -> p j f", j=TN)
                                sp.dma_start(dst, y[s.par][:, :, :]).then_inc(stored[s.par], 16)

                            pipelined(sp, [(store, 0), (load, 2)])
                            full = N // (TN * P)
                            for i in range(2):
                                sp.wait_ge(stored[i], 16 * ((full + 1 - i) // 2) + (32 if full % 2 == i else 0))

                        @block.scalar
                        def _(act):
                            def first_norm(s):
                                deviate(act, s, 0, 0, s_var1, s_std1, TN)
                                normalize(act, s, 0, y[s.par], z, 0, s_norm1, s_app1, TN)

                            def second_norm(s):
                                deviate(act, s, 1, 0, s_var2, s_std2, TN)
                                normalize(act, s, 1, z, y[s.par], 0, s_norm2, s_res, TN)

                            pipelined(act, [(first_norm, 0), (second_norm, 0)])

                        @block.vector
                        def _(dve):
                            v = nc.vector
                            ch = Chain(dve, s_bch, 2 * (TN + LN_LINKS) + 2)

                            def bias(s):
                                dve.wait_ge(loaded[s.par], (s.n - s.par) * 16 + 32)
                                wait(dve, stored[s.par], (s.n - s.par) * 8)
                                v.tensor_tensor(y[s.par][:, :, :], nin[s.par][:, :, 0:D], spread(rows["L3_gnn_b2"], TN), ALU.add).then_inc(s_y, 1)

                            def first_norm(s):
                                ch.begin(s)
                                dve.wait_ge(s_y, s.n + 1)
                                normalizing(dve, ch, s, 0, y[s.par], 0, s_var1, s_std1, s_norm1, TN)

                            def second_norm(s):
                                dve.wait_ge(s_app1, s.n + 1)
                                ch.link(v.tensor_tensor(z[:, :, :], z[:, :, :], spread(rows["L3_gnn_gamma"], TN), ALU.mult))
                                ch.link(v.tensor_tensor(z[:, :, :], z[:, :, :], spread(rows["L3_gnn_beta"], TN), ALU.add))
                                v.tensor_tensor(z[:, :, :], z[:, :, :], x3in[s.par][:, :, :], ALU.add).then_inc(s_added, 1)
                                dve.wait_ge(s_added, s.n + 1)
                                normalizing(dve, ch, s, 1, z, 0, s_var2, s_std2, s_norm2, TN)

                            pipelined(dve, [(first_norm, 0), (bias, 1), (second_norm, 0)])
                edges_gathered()
                closing([*loaded, *stored, *rest_], c)

            c = ExitStack()
            with c:
                bpre = pre + "w_"
                both = sb(bpre + "both", [P, EPP, 2 * HH], fp32, c)
                spreadb = sb(bpre + "spread", [P, EPP, 2 * HH], fp32, c)
                e = sb(bpre + "e", [P, EPP, HH], fp32, c)
                es = sb(bpre + "es", [P, EPP, HH], fp32, c)
                fmax = sb(bpre + "fmax", [P, EPP, HH], fp32, c)
                bmax = sb(bpre + "bmax", [P, EPP, HH], fp32, c)
                pen = sb(bpre + "pen", [P, 4, EPP], fp32, c)
                dg = sb(bpre + "dg", [P, 2 * H, P], fp32, c)
                tmp = sb(bpre + "tmp", [P, 2 * H, P], fp32, c)
                cross = sb(bpre + "cross", [P, 2 * H], fp32, c)
                psX = pb(bpre + "psX", [P, 2 * H], c)
                psM = [pb(bpre + f"psM{i}", [P, H, P], c) for i in range(2)]
                rest_ = names(bpre, c, "chain", "own_crossed", "diagonals", "maxima_crossed", "weights")
                s_ch, s_xo, s_dg, s_mc, s_w = rest_

                with nc.Block() as block:
                    def score(arr, t, side):
                        return arr[:, t, side * H:side * H + HH]

                    @block.tensor
                    def _(pe):
                        for l in range(2):
                            m = nc.tensor.matmul(psX[:, l * HH:(l + 1) * HH], mside[:, :], score(ownal, SIDE, l), start=True, stop=True)
                        m.then_inc(s_xo, 1)
                        pe.wait_ge(s_dg, 1)
                        for l in range(2):
                            for h in range(HH):
                                m = nc.tensor.matmul(psM[l][:, h, :], ones[:, :], dg[:, l * HH + h, :], start=True, stop=True)
                        m.then_inc(s_mc, 1)

                    @block.vector
                    def _(dve):
                        v = nc.vector
                        ch = Chain(dve, s_ch, 0)
                        A = slice(0, EPP)

                        def col(t, n):
                            return t.unsqueeze(2).to_broadcast([P, EPP, n])

                        for l in range(2):
                            bl = slice(l * HH, (l + 1) * HH)
                            ch.link(v.tensor_tensor(both[:, :, bl], score(ownal, A, l), col(mainend[:, A], HH), ALU.mult))
                            ch.link(v.tensor_tensor(spreadb[:, :, bl], col(sidend[:, A], HH), score(ownal, slice(SIDE, SIDE + 1), l).to_broadcast([P, EPP, HH]), ALU.mult))
                        ch.link(v.tensor_tensor(both[:, :, :], both[:, :, :], spreadb[:, :, :], ALU.add))
                        dve.wait_ge(s_xo, 1)
                        ch.link(v.scalar_tensor_tensor(both[:, EPP - 1, :], psX[:, 0:2 * HH], goes[:, EPP - 1:EPP], both[:, EPP - 1, :], ALU.mult, ALU.add))
                        for q in range(2 * HH):
                            at = ch.mark(v.tensor_tensor_scan(spreadb[:, ::-1, q], goes[:, ::-1], both[:, ::-1, q], 0.0, ALU.mult, ALU.add))
                        dve.wait_ge(s_ch, at)
                        ch.link(v.tensor_tensor(e[:, :, :], xrow[:, :, D:D + HH], spreadb[:, :, HH:2 * HH], ALU.add))
                        ch.link(v.scalar_tensor_tensor(e[:, :, :], e[:, :, :], 0.2, e[:, :, :], ALU.mult, ALU.max))
                        ch.link(v.tensor_tensor(es[:, :, :], spreadb[:, :, 0:HH], spreadb[:, :, HH:2 * HH], ALU.add))
                        ch.link(v.scalar_tensor_tensor(es[:, :, :], es[:, :, :], 0.2, es[:, :, :], ALU.mult, ALU.max))
                        for i, m in enumerate((same, goes, lead, trail)):
                            ch.link(v.tensor_scalar(pen[:, i, :], m[:, A], 1.0, BIG, ALU.subtract, ALU.mult))
                        for h in range(HH):
                            ch.mark(v.tensor_tensor_scan(fmax[:, :, h], pen[:, 0, :], e[:, :, h], -BIG, ALU.add, ALU.max))
                            at = ch.mark(v.tensor_tensor_scan(bmax[:, ::-1, h], pen[:, 1, ::-1], e[:, ::-1, h], -BIG, ALU.add, ALU.max))
                        dve.wait_ge(s_ch, at)
                        for h in range(HH):
                            ch.link(v.tensor_scalar(dg[:, h, :], ident[:, :], fmax[:, EPP - 1, h:h + 1], None, ALU.mult))
                            ch.link(v.tensor_scalar(dg[:, HH + h, :], ident[:, :], bmax[:, 0, h:h + 1], None, ALU.mult))
                        dve.sem_inc(s_dg, 1)
                        ch.link(v.tensor_tensor(fmax[:, :, :], fmax[:, :, :], bmax[:, :, :], ALU.max))
                        dve.wait_ge(s_mc, 1)
                        for l, link in enumerate((linkl, linkr)):
                            ch.link(v.tensor_tensor(tmp[:, l * HH:(l + 1) * HH, :], psM[l][:, 0:HH, :], link[:, :].unsqueeze(1).to_broadcast([P, HH, P]), ALU.add))
                        ch.link(v.reduce_max(cross[:, 0:2 * HH], tmp[:, 0:2 * HH, :], AX.X))
                        for h in range(HH):
                            for l in range(2):
                                ch.link(v.scalar_tensor_tensor(fmax[:, :, h], pen[:, 2 + l, :], cross[:, l * HH + h:l * HH + h + 1], fmax[:, :, h], ALU.add, ALU.max))
                        ch.link(v.tensor_tensor(fmax[:, :, :], fmax[:, :, :], es[:, :, :], ALU.max))
                        ch.link(v.tensor_tensor(e[:, :, :], e[:, :, :], fmax[:, :, :], ALU.subtract))
                        ch.link(v.tensor_tensor(es[:, :, :], es[:, :, :], fmax[:, :, :], ALU.subtract))
                        ch.link(v.memset(pself[:, EPP:TP, :], 1.0))
                        dve.sem_inc(s_w, 1)

                    @block.scalar
                    def _(act):
                        act.wait_ge(s_w, 1)
                        nc.scalar.activation(xrow[:, :, D:D + HH], e[:, :, :], ACT.Exp)
                        nc.scalar.activation(pself[:, 0:EPP, 0:HH], es[:, :, :], ACT.Exp)
                        nc.scalar.activation(pself[:, SIDE, 0:HH], es[:, 0, :], ACT.Exp).then_inc(s_w, 1)
                closing(rest_, c)

            c = ExitStack()
            with c:
                cpre = pre + "s_"
                LAST = k_ == 2
                acc = sb(cpre + "acc", [P, 2 * TS, W], fp32, c)
                cap = sb(cpre + "cap", [P, W], fp32, c)
                own = [sb(cpre + f"own{i}", [P, TS, TW], fp32, c) for i in range(2)]
                x3in = [sb(cpre + f"x3_{i}", [P, TS, D], fp32, c) for i in range(2)] if LAST else None
                z = [sb(cpre + f"z{i}", [P, TS, D], fp32, c) for i in range(2)]
                z2 = sb(cpre + "z2", [P, TS, D], fp32, c) if LAST else None
                res = [sb(cpre + f"res{i}", [P, TS, D], fp32, c) for i in range(2)] if LAST else None
                den = sb(cpre + "den", [P, TS, HH], fp32, c)
                xT = sb(cpre + "xT", [P, TS * P], fp32, c)
                tout = [sb(cpre + f"tout{i}", [P, TS, TW], fp32, c) for i in range(2)]
                psT = pb(cpre + "psT", [P, TS * P], c)
                psG = [pb(cpre + f"psG{i}", [P, 2, 512], c) for i in range(2)]
                psC = pb(cpre + "psC", [P, W], c)
                loaded = names(cpre, c, "own_loaded0", "own_loaded1")
                stored = names(cpre, c, "stored0", "stored1")
                rest_ = names(cpre, c, "edge_weighted", "cap_ready", "sum_ready", "self_ready", "averaged", "transposed", "evacuated", "product_ready",
                              "product_evacuated", "own_copied", "chain", "var1", "std1", "norm1", "normalized", "added", "var2", "std2", "norm2",
                              "result_ready", "carry_ready", "cleared", "indices_ready")
                (s_wtd, s_cap, s_sum, s_self, s_avg, s_tr, s_ev, s_out, s_lin, s_own, s_bch, s_var1, s_std1, s_norm1, s_app1, s_added, s_var2, s_std2,
                 s_norm2, s_res, s_carry, s_set, s_idx) = rest_
                NL = 32 if LAST else 16

                with nc.Block() as block:
                    @block.sync
                    def _(sp):
                        def load(s):
                            wait(sp, s_self, free(s, 1))
                            sp.dma_start(own[s.par][:, :, :], slot_rows(table, s.n)).then_inc(loaded[s.par], 16)
                            if LAST:
                                wait(sp, s_added, free(s, 1))
                                sp.dma_start(x3in[s.par][:, :, :], slot_rows(X3, s.n)).then_inc(loaded[s.par], 16)

                        def store(s):
                            sp.wait_ge(s_lin, s.n + 1)
                            sp.dma_start(slot_rows(next_table, s.n), tout[s.par][:, :, :]).then_inc(stored[s.par], 16)

                        if LAST:
                            pipelined(sp, [(load, 2)])
                        else:
                            pipelined(sp, [(load, 2), (store, 0)])
                            for i in range(2):
                                sp.wait_ge(stored[i], 16 * (STEPS // 2))

                    @block.gpsimd
                    def _(pool):
                        last_node = pool.to_reg(N - 1)
                        def weigh(s):
                            if s.last:
                                return
                            tiles = bass.ds(s.n * TS, TS)
                            w = xrow[:, tiles, D:W].unsqueeze(3).to_broadcast([P, TS, HH, CH])
                            x = xrow[:, tiles, 0:D].rearrange("p t (h c) -> p t h c", h=HH)
                            nc.gpsimd.tensor_tensor(x, x, w, ALU.mult).then_inc(s_wtd, 1)

                        def scatter(s):
                            pool.wait_ge(s_res, s.n + 1)
                            row_numbers_free(pool, s)
                            nc.gpsimd.tensor_copy(idxr[:, s.par, 0:TS], outidx[:, bass.ds(s.n * TS, TS)]).then_inc(s_idx, 1)
                            indices(pool, s_idx, s.n + 1)
                            for k in range(TS):
                                pool.indirect_dma_start(out=out, out_offset=bass.IndirectOffsetOnAxis(ap=idxr[:, s.par, k:k + 1], axis=0),
                                                        in_=res[s.par][:, k, :], in_offset=None, bounds_check=last_node, oob_is_err=False).then_inc(ogath[s.par * TS + k], 16)

                        if LAST:
                            pipelined(pool, [(weigh, 1), (scatter, 0)])
                            for k in range(2 * TS):
                                pool.wait_ge(ogath[k], placed[k] + 8 * STEPS)
                        else:
                            pipelined(pool, [(weigh, 1)])

                    @block.tensor
                    def _(pe):
                        t = nc.tensor

                        def carry(s):
                            if s.last:
                                pe.wait_ge(s_sum, EPP)
                                t.matmul(psC[:, :], mleft[:, :], acc[:, (SIDE - 1) % (2 * TS), :], start=True, stop=True).then_inc(s_carry, 1)

                        def product(s):
                            if LAST:
                                return
                            pe.wait_ge(s_avg, s.n + 1)
                            wait(pe, s_ev, s.n)
                            for j in range(TS):
                                m = t.transpose(psT[:, j * P:(j + 1) * P], z[s.par][:, j, :], ident[:, :])
                            m.then_inc(s_tr, 1)
                            pe.wait_ge(s_ev, s.n + 1)
                            wait(pe, s_lin, free(s, 1))
                            for j in range(TS):
                                m = t.matmul(psG[s.par][:, j // 2, j % 2 * TW:(j % 2 + 1) * TW], xT[:, j * P:(j + 1) * P], wgat[:, k_ + 1, :], start=True, stop=True)
                            m.then_inc(s_out, 1)

                        pipelined(pe, [(carry, 1), (product, 0)])

                    @block.scalar
                    def _(act):
                        sc = nc.scalar

                        def product(s):
                            act.wait_ge(s_tr, s.n + 1)
                            wait(act, s_out, s.n)
                            sc.activation(xT[:, :], psT[:, :], ACT.Relu, bias=gatbias[:, k_:k_ + 1]).then_inc(s_ev, 1)
                            act.wait_ge(s_out, s.n + 1)
                            wait(act, stored[s.par], (s.n - s.par) * 8)
                            wait(act, s_own, free(s, 1))
                            sc.copy(tout[s.par][:, :, :].rearrange("p (b j) f -> p b (j f)", b=2), psG[s.par][:, :, 0:2 * TW]).then_inc(s_lin, 1)

                        def first_norm(s):
                            deviate(act, s, 0, 0, s_var1, s_std1, TS)
                            normalize(act, s, 0, z[s.par], z2, 0, s_norm1, s_app1, TS)

                        def second_norm(s):
                            deviate(act, s, 1, 0, s_var2, s_std2, TS)
                            for k in range(TS):
                                slot_rows_free(act, s, k)
                            normalize(act, s, 1, z2, res[s.par], 0, s_norm2, s_res, TS)

                        pipelined(act, [(first_norm, 0), (second_norm, 0)] if LAST else [(product, 0)])

                    @block.vector
                    def _(dve):
                        v = nc.vector
                        v.memset(acc[:, :, :], 0.0).then_inc(s_set, 1)
                        v.memset(cap[:, :], 0.0).then_inc(s_set, 1)
                        dve.wait_ge(s_set, 2)
                        ch = Chain(dve, s_bch, 3 + (2 * (TS + LN_LINKS) + 4 if LAST else 0))

                        def edges(s):
                            if s.last:
                                side_sums(acc, cap, psC[:, :], s_sum, s_carry, dve)
                                return
                            dve.wait_ge(s_wtd, s.n + 1)
                            for k in range(TS):
                                scan_edge(s, k, xrow[:, bass.ds(s.n * TS + k, 1), 0:W].rearrange("p a w -> p (a w)"), acc, cap, s_sum, s_cap, dve)

                        def average(s):
                            ch.begin(s)
                            par, tiles = s.par, bass.ds(s.n * TS, TS)
                            dve.wait_ge(loaded[par], (s.n - par) * (NL // 2) + NL)
                            if not LAST:
                                wait(dve, s_tr, free(s, 1))
                            else:
                                wait(dve, s_app1, free(s, 1))
                            z4 = z[par][:, :, :].rearrange("p t (h c) -> p t h c", h=HH)
                            sums = acc[:, par * TS:(par + 1) * TS, :]
                            v.tensor_tensor(z4, own[par][:, :, 0:D].rearrange("p t (h c) -> p t h c", h=HH),
                                            pself[:, tiles, 0:HH].unsqueeze(3).to_broadcast([P, TS, HH, CH]), ALU.mult).then_inc(s_self, 1)
                            dve.wait_ge(s_self, s.n + 1)
                            ch.mark(v.tensor_tensor(z[par][:, :, :], z[par][:, :, :], sums[:, :, 0:D], ALU.add))
                            ch.link(v.scalar_tensor_tensor(den[:, :, :], sums[:, :, D:W], 1e-16, pself[:, tiles, 0:HH], ALU.add, ALU.add))
                            ch.link(v.reciprocal(den[:, :, :], den[:, :, :]))
                            ins = v.tensor_tensor(z4, z4, den[:, :, :].unsqueeze(3).to_broadcast([P, TS, HH, CH]), ALU.mult)
                            if LAST:
                                ch.link(ins)
                                ch.link(v.tensor_tensor(z[par][:, :, :], z[par][:, :, :], spread(rows["L3_gnn_b2"], TS), ALU.add))
                                normalizing(dve, ch, s, 0, z[par], 0, s_var1, s_std1, s_norm1, TS)
                            else:
                                ins.then_inc(s_avg, 1)

                        def second_norm(s):
                            dve.wait_ge(s_app1, s.n + 1)
                            ch.link(v.tensor_tensor(z2[:, :, :], z2[:, :, :], spread(rows["L3_gnn_gamma"], TS), ALU.mult))
                            ch.link(v.tensor_tensor(z2[:, :, :], z2[:, :, :], spread(rows["L3_gnn_beta"], TS), ALU.add))
                            v.tensor_tensor(z2[:, :, :], z2[:, :, :], x3in[s.par][:, :, :], ALU.add).then_inc(s_added, 1)
                            dve.wait_ge(s_added, s.n + 1)
                            normalizing(dve, ch, s, 1, z2, 0, s_var2, s_std2, s_norm2, TS)

                        def own_scores(s):
                            dve.wait_ge(s_lin, s.n + 1)
                            v.tensor_copy(ownal[:, bass.ds(s.n * TS, TS), :], tout[s.par][:, :, D:TW]).then_inc(s_own, 1)

                        pipelined(dve, [(average, 0), (edges, 1), (second_norm, 0)] if LAST else [(average, 0), (edges, 1), (own_scores, -1)])
                closing([*loaded, *stored, *rest_], c)


PREP_LOADS = 16 * (6 + 2 + 2 + 2 + 4 + 2 + 3 * 3 + 9 + 3 * TS)


_INS = ["x", "src", "dst", "edge_type_8", "edge_weight",
        "L0_gnn_W_self", "L0_gnn_b_self", "L0_gnn_W_rel", "L0_gnn_gamma", "L0_gnn_beta",
        "L1_gnn_W_l0", "L1_gnn_b_l0", "L1_gnn_W_r0", "L1_gnn_gamma0", "L1_gnn_beta0",
        "L1_gnn_W_l1", "L1_gnn_b_l1", "L1_gnn_W_r1", "L1_gnn_gamma1", "L1_gnn_beta1",
        "L3_gnn_W0", "L3_gnn_a_src0", "L3_gnn_a_dst0", "L3_gnn_b0",
        "L3_gnn_W1", "L3_gnn_a_src1", "L3_gnn_a_dst1", "L3_gnn_b1",
        "L3_gnn_W2", "L3_gnn_a_src2", "L3_gnn_a_dst2", "L3_gnn_b2", "L3_gnn_gamma", "L3_gnn_beta"]


def kernel(**inputs):
    import numpy as _np
    import concourse.bacc as _bacc
    from concourse import mybir as _mybir
    from concourse.bass_utils import run_bass_kernel_spmd as _run

    nc = _bacc.Bacc("TRN2", target_bir_lowering=False, num_devices=1)
    arrays, args = {}, {}
    for name in _INS:
        arr = _np.ascontiguousarray(inputs[name])
        arrays[f"in_{name}_dram"] = arr
        args[name] = nc.dram_tensor(f"in_{name}_dram", arr.shape, _mybir.dt.from_np(arr.dtype), kind="ExternalInput").ap()
    out = nc.dram_tensor("out_0_dram", (N, D), _mybir.dt.float32, kind="ExternalOutput").ap()
    gnn_kernel(nc, args, out)
    r = _run(nc, [arrays], core_ids=[0])
    return r.results[0]["out_0_dram"]
```

```python
import concourse.bass as bass
from concourse import mybir
from contextlib import ExitStack

fp32 = mybir.dt.float32
i32 = mybir.dt.int32
ALU = mybir.AluOpType
ACT = mybir.ActivationFunctionType
AX = mybir.AxisListType

P = 128
N, D, E = 50000, 128, 25000
R = 8
EPP = -(-E // P)
TS = 4
TN = 8
U = TS + TN
STEPS = EPP // TS + 1
TP = STEPS * TS
SIDE = EPP
NPAD = STEPS * TN * P
NSLOT = TP * P
PAD_NODE = NPAD - 1
OUT_OF_RANGE = 1 << 20
KH = N // P + 2
PAD_KEY = KH * P - 1
H, C = 4, 32
TW = D + 2 * H
EPS = 1e-5
BIG = 1e30


def wait(eng, sem, value):
    if isinstance(value, int) and value <= 0:
        return
    eng.wait_ge(sem, value)


class Step:

    def __init__(self, n, par):
        self.n, self.par = n, par
        self.last = isinstance(n, int) and n == STEPS - 1


def pipelined(eng, order, steps=STEPS):
    def run(base, par):
        for part, off in order:
            if isinstance(base, int) and not 0 <= base + off < steps:
                continue
            part(Step(base + off, (par + off) % 2))

    for base in range(-2, 4):
        run(base, base % 2)
    with eng.Fori(2, steps // 2 - 2) as i:
        run(i * 2, 0)
        run(i * 2 + 1, 1)
    for base in range(steps - 4, steps + 2):
        run(base, base % 2)


class Chain:

    def __init__(self, eng, sem, per):
        self.eng, self.sem, self.per, self.n, self.base = eng, sem, per, 0, 0

    def begin(self, step=None):
        assert step is None or self.n in (0, self.per), (self.n, self.per)
        self.base = 0 if step is None else step.n * self.per
        if step is not None:
            self.n = 0

    def mark(self, ins):
        ins.then_inc(self.sem, 1)
        self.n += 1
        return self.base + self.n

    def link(self, ins):
        self.eng.wait_ge(self.sem, self.mark(ins))


def gnn_kernel(nc, a, out):
    ctx = ExitStack()
    with ctx:
        def sb(name, shape, dt=fp32, c=ctx):
            return c.enter_context(nc.sbuf_tensor(name, shape, dt))

        def pb(name, shape, c=ctx):
            return c.enter_context(nc.psum_tensor(name, shape, fp32))

        used = []

        def sem(name):
            s = ctx.enter_context(nc.semaphore(name))
            used.append(s)
            return s

        def dram(name, shape, dt=fp32):
            return nc.dram_tensor(name, shape, dt, kind="Internal").ap()

        row_of_node = dram("row_of_node", (NPAD, 1), i32)
        X1 = dram("X1", (NPAD + NSLOT, D))
        H1 = dram("H1", (NPAD + NSLOT, D))
        X2 = dram("X2", (NPAD + NSLOT, D))
        X3 = dram("X3", (NPAD + NSLOT, D))
        E1 = dram("E1", (NPAD, D))
        E2 = dram("E2", (NPAD, D))
        E3 = dram("E3", (NPAD, D))
        records = dram("records", (P * EPP, 4))
        T1 = dram("T1", (NPAD + NSLOT, TW))
        T2 = dram("T2", (NPAD + NSLOT, TW))
        T3 = dram("T3", (NPAD + NSLOT, TW))

        def node_rows(t, n):
            return t[0:NPAD, :].rearrange("(n p j) f -> n p j f", p=P, j=TN)[n]

        def slot_rows(t, n):
            base = t.shape[0] - NSLOT if t.shape[0] > NPAD else 0
            return t[base:base + NSLOT, :].rearrange("(p t) f -> p t f", p=P)[:, bass.ds(n * TS, TS), :]

        ident = sb("ident", [P, P])
        ones = sb("ones", [P, P])
        epsc = sb("epsc", [P, 1])
        wself = sb("wself", [P, D])
        wrel = sb("wrel", [P, R, D])
        wsage = sb("wsage", [P, 4, D])
        gatbias = sb("gatbias", [P, 2])
        wgat = sb("wgat", [P, 3, TW])
        rows = {k: sb("row_" + k, [P, D]) for k in (
            "L0_gnn_gamma", "L0_gnn_beta", "L1_gnn_gamma0", "L1_gnn_beta0", "L1_gnn_gamma1", "L1_gnn_beta1",
            "L3_gnn_b2", "L3_gnn_gamma", "L3_gnn_beta")}
        biases = {k: sb("bias_" + k, [1, TS, D]) for k in ("L0_gnn_b_self", "L1_gnn_b_l0", "L1_gnn_b_l1")}
        same = sb("same", [P, TP])
        lead = sb("lead", [P, TP])
        weight = sb("weight", [P, TP])
        rdeg = sb("rdeg", [P, TP])
        coef = sb("coef", [P, TP, R])
        mleft = sb("mleft", [P, P])
        mright = sb("mright", [P, P])
        mside = sb("mside", [P, P])
        mainend = sb("mainend", [P, TP])
        sidend = sb("sidend", [P, TP])
        trail = sb("trail", [P, TP])
        sameb = sb("sameb", [P, TP])
        leadb = sb("leadb", [P, TP])
        weightb = sb("weightb", [P, TP])
        mleftb = sb("mleftb", [P, P])
        dstb = sb("dstb", [P, TP], i32)
        outb = sb("outb", [P, TP], i32)
        goes = sb("goes", [P, EPP])
        linkl = sb("linkl", [P, P])
        linkr = sb("linkr", [P, P])
        sideact = sb("sideact", [P, 1])
        srcidx = sb("srcidx", [P, TP], i32)
        ownidx = sb("ownidx", [P, TP], i32)
        endidx = sb("endidx", [P, TP], i32)
        endrow = sb("endrow", [P, TP], i32)
        outidx = sb("outidx", [P, TP], i32)
        gidx = sb("gidx", [P, TP], i32)

        with ExitStack() as c:
            s_set, s_ld, s_ch, s_wt, s_wc, s_bc, s_cl, s_cnt, s_cross, s_iota, s_map, s_zero, s_am = (
                sem("prep_" + k) for k in ("set", "loaded", "chain", "weights_transposed", "weights_copied",
                                           "rows_spread", "masks", "scans", "crossed", "iota", "map", "zero_rows", "score_vectors"))
            dsti = sb("dsti", [P, TP], i32, c)
            typi = sb("typi", [P, EPP], i32, c)
            previ = sb("previ", [P, 1], i32, c)
            nexti = sb("nexti", [P, 1], i32, c)
            d = sb("d", [P, EPP], fp32, c)
            prev = sb("prev", [P, EPP], fp32, c)
            nxt = sb("nxt", [P, EPP], fp32, c)
            typ = sb("typ", [P, EPP], fp32, c)
            eq = sb("eq", [P, R, EPP], fp32, c)
            fw = sb("fw", [P, R, EPP], fp32, c)
            bw = sb("bw", [P, R, EPP], fp32, c)
            cont = sb("cont", [P, 1], fp32, c)
            endm = sb("endm", [P, EPP], fp32, c)
            t0 = sb("t0", [P, TP], fp32, c)
            t1 = sb("t1", [P, TP], fp32, c)
            t2 = sb("t2", [P, TP], fp32, c)
            slotrow = sb("slotrow", [P, TP], fp32, c)
            siderow = sb("siderow", [P, 1], fp32, c)
            dg = sb("dg", [P, 2, P], fp32, c)
            crossed = sb("crossed", [P, 2, R], fp32, c)
            less = sb("less", [P, P], fp32, c)
            more = sb("more", [P, P], fp32, c)
            nodeid = sb("nodeid", [P, NPAD // P], i32, c)
            wnat = sb("wnat", [P, R + 8, D], fp32, c)
            wgt = sb("wgt", [P, 3, D], fp32, c)
            heads = sb("heads", [P, H], fp32, c)
            avec = sb("avec", [P, 6], fp32, c)
            amat = sb("amat", [P, 3, 2 * H], fp32, c)
            psw = [pb(f"psw{i}", [P, 512], c) for i in range(4)]
            psa = pb("psa", [P, 3, 2 * H], c)
            psr = pb("psr", [P, 2, P], c)
            psx = pb("psx", [P, 2, R], c)
            LASTN = E - (P - 1) * EPP

            with nc.Block() as block:
                @block.sync
                def _(sp):
                    sp.wait_ge(s_set, 6)
                    n = 0
                    def ld(dst, src, **kw):
                        nonlocal n
                        sp.dma_start(dst, src, **kw).then_inc(s_ld, 16)
                        n += 1
                    for buf, name in ((dsti, "dst"), (srcidx, "src"), (typi, "edge_type_8")):
                        ld(buf[0:P - 1, 0:EPP], a[name][0:(P - 1) * EPP].rearrange("(p t) -> p t", t=EPP))
                        ld(buf[P - 1:P, 0:LASTN], a[name][(P - 1) * EPP:E].rearrange("(p t) -> p t", p=1))
                    ld(weight[0:P - 1, 0:EPP], a["edge_weight"][0:(P - 1) * EPP].rearrange("(p t) -> p t", t=EPP))
                    ld(weight[P - 1:P, 0:LASTN], a["edge_weight"][(P - 1) * EPP:E].rearrange("(p t) -> p t", p=1))
                    ld(previ[1:P, :], a["dst"][EPP - 1:E].rearrange("(p t) -> p t", p=1)[:, 0:1 + EPP * (P - 2):EPP].rearrange("p t -> t p"), allow_slow_non_contiguous=True)
                    ld(nexti[0:P - 1, :], a["dst"][EPP:E].rearrange("(p t) -> p t", p=1)[:, 0:1 + EPP * (P - 2):EPP].rearrange("p t -> t p"), allow_slow_non_contiguous=True)
                    ld(wnat[:, 0, :], a["L0_gnn_W_self"])
                    ld(wnat[:, 1:R + 1, :], a["L0_gnn_W_rel"].rearrange("r o f -> o r f"))
                    for k, name in enumerate(("W_l0", "W_r0", "W_l1", "W_r1")):
                        ld(wnat[:, R + 1 + k, :], a["L1_gnn_" + name])
                    for k in range(2):
                        ld(gatbias[:, k:k + 1], a[f"L3_gnn_b{k}"].unsqueeze(1), allow_slow_non_contiguous=True)
                    for k in range(3):
                        ld(wnat[:, R + 5 + k, :], a[f"L3_gnn_W{k}"])
                        for l, name in enumerate(("a_src", "a_dst")):
                            ld(avec[:, 2 * k + l:2 * k + l + 1], a[f"L3_gnn_{name}{k}"].rearrange("h c -> (h c)").unsqueeze(1), allow_slow_non_contiguous=True)
                    for k, t in rows.items():
                        ld(t[:, :], a[k].partition_broadcast(P))
                    for k, t in biases.items():
                        for j in range(TS):
                            ld(t[0:1, j, :], a[k].rearrange("(a f) -> a f", a=1))
                    assert 16 * n == PREP_LOADS
                    sp.wait_ge(s_iota, 1)
                    sp.dma_start(row_of_node.rearrange("(p t) o -> p (t o)", p=P), nodeid[:, :]).then_inc(s_map, 16)


                @block.gpsimd
                def _(pool):
                    nc.gpsimd.iota(nodeid[:, :], [[1, NPAD // P]], base=0, channel_multiplier=NPAD // P).then_inc(s_iota, 1)
                    nc.gpsimd.iota(slotrow[:, :], [[1, TP]], base=NPAD, channel_multiplier=TP, allow_small_or_imprecise_dtypes=True).then_inc(s_iota, 1)
                    nc.gpsimd.iota(siderow[:, :], [[1, 1]], base=NPAD + SIDE, channel_multiplier=TP, allow_small_or_imprecise_dtypes=True).then_inc(s_iota, 1)
                    pool.wait_ge(s_cl, 3)
                    nc.gpsimd.affine_select(out=ident[:, :], in_=ones[:, :], compare_op=ALU.is_equal, fill=0.0, base=0, pattern=[[-1, P]], channel_multiplier=1).then_inc(s_iota, 1)
                    nc.gpsimd.affine_select(out=less[:, :], in_=ones[:, :], compare_op=ALU.is_gt, fill=0.0, base=0, pattern=[[1, P]], channel_multiplier=-1).then_inc(s_iota, 1)
                    nc.gpsimd.affine_select(out=more[:, :], in_=ones[:, :], compare_op=ALU.is_gt, fill=0.0, base=0, pattern=[[-1, P]], channel_multiplier=1).then_inc(s_iota, 1)

                    nc.gpsimd.affine_select(out=heads[:, :], in_=ones[:, 0:H], compare_op=ALU.is_ge, fill=0.0, base=0, pattern=[[-C, H]], channel_multiplier=1).then_inc(s_iota, 1)
                    pool.wait_ge(s_iota, 7)
                    nc.gpsimd.affine_select(out=heads[:, :], in_=heads[:, :], compare_op=ALU.is_ge, fill=0.0, base=C - 1, pattern=[[C, H]], channel_multiplier=-1).then_inc(s_iota, 1)

                @block.tensor
                def _(pe):
                    pe.wait_ge(s_iota, 4)
                    pe.wait_ge(s_ld, PREP_LOADS)
                    for k in range(R + 8):
                        m = nc.tensor.transpose(psw[k // 4][:, (k % 4) * P:(k % 4 + 1) * P], wnat[:, k, :], ident[:, :])
                    m.then_inc(s_wt, 1)
                    pe.wait_ge(s_am, 1)
                    pe.wait_ge(s_wc, R + 8)
                    for k in range(3):
                        m = nc.tensor.matmul(psa[:, k, :], wgt[:, k, :], amat[:, k, :], start=True, stop=True)
                    m.then_inc(s_wt, 1)
                    pe.wait_ge(s_bc, 1)
                    for k in range(2):
                        m = nc.tensor.matmul(psr[:, k, :], ones[:, :], dg[:, k, :], start=True, stop=True)
                    m.then_inc(s_wt, 1)
                    pe.wait_ge(s_cnt, 1)
                    nc.tensor.matmul(psx[:, 0, :], mleft[:, :], fw[:, :, EPP - 1], start=True, stop=True)
                    nc.tensor.matmul(psx[:, 1, :], mright[:, :], bw[:, :, 0], start=True, stop=True).then_inc(s_cross, 1)

                @block.scalar
                def _(act):
                    act.wait_ge(s_wt, 1)
                    nc.scalar.copy(wself[:, :], psw[0][:, 0:P]).then_inc(s_wc, 1)
                    for k in range(1, R + 1):
                        nc.scalar.copy(wrel[:, k - 1, :], psw[k // 4][:, (k % 4) * P:(k % 4 + 1) * P]).then_inc(s_wc, 1)
                    for k in range(R + 1, R + 8):
                        dst = wsage[:, k - R - 1, :] if k < R + 5 else wgt[:, k - R - 5, :]
                        nc.scalar.copy(dst, psw[k // 4][:, (k % 4) * P:(k % 4 + 1) * P]).then_inc(s_wc, 1)
                    act.wait_ge(s_wt, 2)
                    nc.scalar.copy(wgat[:, :, D:TW], psa[:, :, :]).then_inc(s_wc, 1)
                    nc.scalar.copy(wgat[:, :, 0:D], wnat[:, R + 5:R + 8, :]).then_inc(s_wc, 1)

                @block.vector
                def _(dve):
                    ch = Chain(dve, s_ch, 0)
                    v = nc.vector
                    v.memset(dsti[:, :], PAD_NODE).then_inc(s_set, 1)
                    v.memset(srcidx[:, :], 0).then_inc(s_set, 1)
                    v.memset(typi[:, :], 0).then_inc(s_set, 1)
                    v.memset(weight[:, :], 0.0).then_inc(s_set, 1)
                    v.memset(previ[:, :], -1).then_inc(s_set, 1)
                    v.memset(nexti[:, :], -1).then_inc(s_set, 1)
                    v.memset(ones[:, :], 1.0).then_inc(s_cl, 1)
                    v.memset(epsc[:, :], EPS).then_inc(s_cl, 1)
                    v.memset(coef[:, :, :], 0.0).then_inc(s_cl, 1)
                    for t in (same, lead, rdeg, mainend, sidend, trail):
                        ch.link(v.memset(t[:, :], 0.0))
                    dve.wait_ge(s_ld, PREP_LOADS)
                    dve.wait_ge(s_cl, 3)
                    dve.wait_ge(s_iota, 8)
                    ch.link(v.memset(amat[:, :, :], 0.0))
                    for k in range(2):
                        for l in range(2):
                            ch.link(v.tensor_scalar(amat[:, k, l * H:(l + 1) * H], heads[:, :], avec[:, 2 * k + l:2 * k + l + 1], None, ALU.mult))
                    for l in range(2):
                        ch.link(v.tensor_copy(amat[:, 2, l * H:l * H + 1], avec[:, 4 + l:5 + l]))
                    dve.sem_inc(s_am, 1)
                    ch.link(v.tensor_copy(d[:, :], dsti[:, 0:EPP]))
                    ch.link(v.tensor_copy(typ[:, :], typi[:, :]))
                    ch.link(v.tensor_copy(prev[:, 1:EPP], dsti[:, 0:EPP - 1]))
                    ch.link(v.tensor_copy(prev[:, 0:1], previ[:, :]))
                    ch.link(v.tensor_copy(nxt[:, 0:EPP - 1], dsti[:, 1:EPP]))
                    ch.link(v.tensor_copy(nxt[:, EPP - 1:EPP], nexti[:, :]))
                    ch.mark(v.tensor_scalar(dg[:, 0, :], ident[:, :], d[:, 0:1], None, ALU.mult))
                    ch.link(v.tensor_scalar(dg[:, 1, :], ident[:, :], d[:, EPP - 1:EPP], None, ALU.mult))
                    dve.sem_inc(s_bc, 1)
                    ch.mark(v.tensor_tensor(same[:, 1:EPP], d[:, 1:EPP], prev[:, 1:EPP], ALU.is_equal))
                    ch.mark(v.tensor_tensor(cont[:, :], d[:, 0:1], prev[:, 0:1], ALU.is_equal))
                    ch.mark(v.tensor_tensor(endm[:, :], d[:, :], nxt[:, :], ALU.not_equal))
                    ch.mark(v.tensor_scalar(lead[:, 0:EPP], d[:, :], d[:, 0:1], None, ALU.is_equal))
                    ch.link(v.tensor_scalar(trail[:, 0:EPP], d[:, :], d[:, EPP - 1:EPP], None, ALU.is_equal))
                    ch.link(v.scalar_tensor_tensor(sidend[:, 0:EPP], endm[:, :], cont[:, 0:1], lead[:, 0:EPP], ALU.mult, ALU.mult))
                    ch.mark(v.tensor_tensor(mainend[:, 0:EPP], endm[:, :], sidend[:, 0:EPP], ALU.subtract))
                    ch.link(v.reduce_max(sideact[:, :], sidend[:, 0:EPP], AX.X))
                    ch.link(v.tensor_scalar(t0[:, :], slotrow[:, :], siderow[:, 0:1], -1.0, ALU.subtract, ALU.mult))
                    ch.link(v.tensor_tensor(t0[:, :], t0[:, :], sidend[:, :], ALU.mult))
                    ch.link(v.tensor_tensor(t0[:, :], t0[:, :], slotrow[:, :], ALU.add))
                    ch.link(v.tensor_copy(endrow[:, :], t0[:, :]))
                    ch.link(v.tensor_scalar(t1[:, 0:EPP], d[:, :], float(OUT_OF_RANGE), None, ALU.subtract))
                    ch.link(v.memset(t2[:, :], float(OUT_OF_RANGE)))
                    ch.link(v.tensor_tensor(t0[:, 0:EPP], t1[:, 0:EPP], endm[:, :], ALU.mult))
                    ch.link(v.tensor_tensor(t2[:, 0:EPP], t2[:, 0:EPP], t0[:, 0:EPP], ALU.add))
                    ch.link(v.tensor_copy(endidx[:, :], t2[:, :]))
                    ch.link(v.memset(t2[:, :], float(OUT_OF_RANGE)))
                    ch.link(v.tensor_tensor(t0[:, 0:EPP], t1[:, 0:EPP], mainend[:, 0:EPP], ALU.mult))
                    ch.link(v.tensor_tensor(t2[:, 0:EPP], t2[:, 0:EPP], t0[:, 0:EPP], ALU.add))
                    ch.link(v.tensor_tensor(t0[:, 0:1], t1[:, 0:1], sideact[:, :], ALU.mult))
                    ch.link(v.tensor_tensor(t2[:, SIDE:SIDE + 1], t2[:, SIDE:SIDE + 1], t0[:, 0:1], ALU.add))
                    ch.link(v.tensor_copy(outidx[:, :], t2[:, :]))
                    ch.link(v.memset(t0[:, :], 0.0))
                    ch.link(v.tensor_scalar(t0[:, 0:EPP], d[:, :], float(N - 1), None, ALU.min))
                    ch.link(v.tensor_scalar(t0[:, SIDE:SIDE + 1], d[:, 0:1], float(N - 1), None, ALU.min))
                    ch.link(v.tensor_copy(ownidx[:, :], t0[:, :]))
                    dve.wait_ge(s_wt, 3)
                    ch.link(v.scalar_tensor_tensor(mleft[:, :], psr[:, 0, :], d[:, EPP - 1:EPP], less[:, :], ALU.is_equal, ALU.mult))
                    ch.link(v.scalar_tensor_tensor(mright[:, :], psr[:, 1, :], d[:, 0:1], more[:, :], ALU.is_equal, ALU.mult))
                    ch.link(v.tensor_scalar(mside[:, :], mright[:, :], sideact[:, 0:1], None, ALU.mult))
                    for link, m in ((linkl, mright), (linkr, mleft)):
                        ch.link(v.tensor_scalar(link[:, :], (psr[:, 1, :] if link is linkl else psr[:, 0, :]), d[:, 0:1] if link is linkl else d[:, EPP - 1:EPP], None, ALU.is_equal))
                        ch.link(v.tensor_tensor(link[:, :], link[:, :], (more if link is linkl else less)[:, :], ALU.mult))
                        ch.link(v.tensor_scalar(link[:, :], link[:, :], 1.0, BIG, ALU.subtract, ALU.mult))
                    for r in range(R):
                        ch.link(v.tensor_scalar(eq[:, r, :], typ[:, :], float(r), None, ALU.is_equal))
                    for r in range(R):
                        ch.mark(v.tensor_tensor_scan(fw[:, r, :], same[:, 0:EPP], eq[:, r, :], 0.0, ALU.mult, ALU.add))
                    ch.link(v.tensor_tensor(goes[:, :], d[:, :], nxt[:, :], ALU.is_equal))
                    for r in range(R):
                        ch.link(v.tensor_tensor_scan(bw[:, r, ::-1], goes[:, ::-1], eq[:, r, ::-1], 0.0, ALU.mult, ALU.add))
                    dve.sem_inc(s_cnt, 1)
                    dve.wait_ge(s_cross, 1)
                    ch.link(v.tensor_copy(crossed[:, :, :], psx[:, :, :]))
                    for r in range(R):
                        ch.mark(v.scalar_tensor_tensor(fw[:, r, :], lead[:, 0:EPP], crossed[:, 0, r:r + 1], fw[:, r, :], ALU.mult, ALU.add))
                        ch.link(v.scalar_tensor_tensor(bw[:, r, :], trail[:, 0:EPP], crossed[:, 1, r:r + 1], bw[:, r, :], ALU.mult, ALU.add))
                    ch.link(v.tensor_tensor(fw[:, :, :], fw[:, :, :], bw[:, :, :], ALU.add))
                    ch.link(v.tensor_tensor(fw[:, :, :], fw[:, :, :], eq[:, :, :], ALU.subtract))
                    ch.link(v.reduce_sum(t0[:, 0:EPP], fw[:, :, :].rearrange("p r t -> p t r"), AX.X))
                    ch.link(v.reciprocal(rdeg[:, 0:EPP], t0[:, 0:EPP]))
                    ch.link(v.tensor_tensor(fw[:, :, :], fw[:, :, :], eq[:, :, :], ALU.mult))
                    ch.link(v.reduce_sum(t0[:, 0:EPP], fw[:, :, :].rearrange("p r t -> p t r"), AX.X))
                    ch.link(v.reciprocal(t1[:, 0:EPP], t0[:, 0:EPP]))
                    for r in range(R):
                        ch.link(v.tensor_tensor(coef[:, 0:EPP, r], eq[:, r, :], t1[:, 0:EPP], ALU.mult))
                    dve.wait_ge(s_wc, R + 10)
                    dve.wait_ge(s_map, 16)
        nc.all_engine_barrier()

        idxr = sb("idxr", [P, 2, 2 * TS], i32)
        ownal = sb("ownal", [P, TP, 2 * H])
        st = sb("st", [P, U, 6])
        lnt = sb("lnt", [P, 4, U])
        var = sb("var", [P, 2, U])
        sd = sb("sd", [P, 2, U])
        rstd = sb("rstd", [P, 2, U])
        nmr = sb("nmr", [P, 2, U])

        def spread(row, tiles):
            return row[:, :].unsqueeze(1).to_broadcast([P, tiles, D])

        def scan_edge(s, k, src, acc, cap, s_sum, s_cap, dve, same=same, lead=lead):
            t, slot, w = s.n * TS + k, s.par * TS + k, acc.shape[2]
            nc.vector.scalar_tensor_tensor(acc[:, slot, :], acc[:, (slot - 1) % (2 * TS), :], same[:, bass.ds(t, 1)],
                                           src, ALU.mult, ALU.add).then_inc(s_sum, 1)
            nc.vector.scalar_tensor_tensor(cap[:, :], src, lead[:, bass.ds(t, 1)], cap[:, :], ALU.mult, ALU.add).then_inc(s_cap, 1)
            dve.wait_ge(s_sum, t + 1)
            dve.wait_ge(s_cap, t + 1)

        def side_sums(acc, cap, psC, s_sum, s_carry, dve):
            w = acc.shape[2]
            dve.wait_ge(s_carry, 1)
            nc.vector.tensor_tensor(acc[:, SIDE % (2 * TS), :], psC, cap[:, :], ALU.add).then_inc(s_sum, 1)
            nc.vector.memset(acc[:, SIDE % (2 * TS) + 1:SIDE % (2 * TS) + TS, :], 0.0).then_inc(s_sum, TS - 1)

        def normalizing(dve, ch, s, k, src, t0, s_var, s_std, s_norm, t1=U, factor=1.0, first=0):
            v = nc.vector
            for j in range(t0, t1):
                at = ch.mark(v.bn_stats(st[:, j, :], src[:, j - first, :]))
            dve.wait_ge(ch.sem, at)
            tt = slice(t0, t1)
            ch.mark(v.tensor_tensor(lnt[:, 0, tt], st[:, tt, 1], st[:, tt, 4], ALU.subtract))
            ch.mark(v.tensor_tensor(lnt[:, 1, tt], st[:, tt, 2], st[:, tt, 5], ALU.add))
            ch.link(v.tensor_tensor(lnt[:, 2, tt], st[:, tt, 1], st[:, tt, 4], ALU.add))
            ch.link(v.scalar_tensor_tensor(lnt[:, 3, tt], lnt[:, 0, tt], 0.25, lnt[:, 0, tt], ALU.mult, ALU.mult))
            v.scalar_tensor_tensor(var[:, k, tt], lnt[:, 1, tt], 1.0 / D, lnt[:, 3, tt], ALU.mult, ALU.add).then_inc(s_var, 1)
            dve.wait_ge(s_std, s.n + 1)
            ch.link(v.reciprocal(rstd[:, k, tt], sd[:, k, tt]))
            if factor != 1.0:
                ch.link(v.tensor_scalar(rstd[:, k, tt], rstd[:, k, tt], factor, None, ALU.mult))
            v.scalar_tensor_tensor(nmr[:, k, tt], lnt[:, 2, tt], -0.5, rstd[:, k, tt], ALU.mult, ALU.mult).then_inc(s_norm, 1)

        LN_LINKS = 5

        def deviate(act, s, k, t0, s_var, s_std, t1=U, factor=1.0):
            act.wait_ge(s_var, s.n + 1)
            nc.scalar.activation(sd[:, k, t0:t1], var[:, k, t0:t1], ACT.Sqrt, bias=epsc[:, 0:1], scale=factor * factor).then_inc(s_std, 1)

        def normalize(act, s, k, src, dst, t0, s_norm, s_done, t1=U):
            act.wait_ge(s_norm, s.n + 1)
            for j in range(t0, t1):
                m = nc.scalar.activation(dst[:, j, :], src[:, j, :], ACT.Identity, bias=nmr[:, k, j:j + 1], scale=rstd[:, k, j:j + 1])
            m.then_inc(s_done, 1)

        s_go = ctx.enter_context(nc.semaphore("row_numbers_seen"))

        def indices(pool, sem, count):
            pool.wait_ge(sem, count)
            pool.sem_inc(s_go, 1)

        def gather(pool, dst, table, index, done, last):
            pool.indirect_dma_start(out=dst, out_offset=None, in_=table, in_offset=bass.IndirectOffsetOnAxis(ap=index, axis=0),
                                    bounds_check=last, oob_is_err=False).then_inc(done, 16)

        def scatter_rows(pool, table, rows_, index, done, last):
            pool.indirect_dma_start(out=table, out_offset=bass.IndirectOffsetOnAxis(ap=index, axis=0), in_=rows_, in_offset=None,
                                    bounds_check=last, oob_is_err=False).then_inc(done, 16)

        def arrived(s):
            return (s.n - s.par) * 8 + 16

        def free(s, each):
            return (s.n - 1) * each

        def first_free(s, each):
            return free(s, each)

        def closing(sems, c):
            nc.all_engine_barrier()
            for x in sems:
                nc.sync.sem_clear(x)
            nc.all_engine_barrier()

        def names(prefix, c, *keys):
            out_ = [c.enter_context(nc.semaphore(prefix + k)) for k in keys]
            return out_

        closing(used, None)
        gath = names("", ctx, *[f"gathered{k}" for k in range(2 * TS)])
        ogath = names("", ctx, *[f"own_gathered{k}" for k in range(2 * TS)])
        s_mv = names("", ctx, "map_moved0", "map_moved1")
        placed = [16 * len(range(k, EPP, 2 * TS)) for k in range(2 * TS)]
        before = [0] * (2 * TS)

        def edge_rows(eng, s, k):
            eng.wait_ge(gath[s.par * TS + k], before[s.par * TS + k] + arrived(s))

        def slots_moved():
            for k in range(2 * TS):
                placed[k] += 8 * STEPS

        def slot_rows_moved(eng, s, k):
            eng.wait_ge(ogath[s.par * TS + k], placed[s.par * TS + k] + arrived(s))

        def slot_rows_free(eng, s, k):
            if not (isinstance(s.n, int) and s.n < 2 and placed[s.par * TS + k] == 0):
                eng.wait_ge(ogath[s.par * TS + k], placed[s.par * TS + k] + (s.n - s.par) * 8)

        def row_numbers_free(pool, s):
            if not (isinstance(s.n, int) and s.n < 2):
                for k in range(TS):
                    slot_rows_free(pool, s, k)

        def edges_gathered():
            for t in range(EPP):
                before[t % (2 * TS)] += 16


        with ExitStack() as c:
            s_ld, s_iota, s_ch, s_hot, s_hist, s_base, s_row, s_tr, s_tc, s_look, s_run, s_cp, s_pos, s_rec, s_set, s_zero, s_mcp = names(
                "sort_", c, "loaded", "iota", "chain", "one_hot", "counted", "bases", "keys_spread", "transposed", "transpose_copied",
                "looked_up", "run_on", "run_copied", "position", "records", "cleared", "zeroed", "map_copied")
            keyi = sb("keyi", [P, EPP], i32, c)
            loi = sb("loi", [P, EPP], i32, c)
            key = sb("key", [P, EPP], fp32, c)
            lo = sb("lo", [P, EPP], fp32, c)
            hi = sb("hi", [P, EPP], fp32, c)
            columns = sb("columns", [P, KH], fp32, c)
            olo = sb("olo", [P, 2, P], fp32, c)
            ohi = sb("ohi", [P, 2, KH], fp32, c)
            oloT = sb("oloT", [P, 2, P], fp32, c)
            diag = sb("diag", [P, 2, P], fp32, c)
            count = sb("count", [P, KH], fp32, c)
            base = sb("base", [P, KH], fp32, c)
            run = sb("run", [P, 2, KH], fp32, c)
            picked = sb("picked", [P, KH], fp32, c)
            twin = sb("twin", [P, P], fp32, c)
            part = sb("part", [P, 2], fp32, c)
            place = sb("place", [P, EPP], fp32, c)
            placei = sb("placei", [P, EPP], i32, c)
            rec = sb("rec", [P, EPP, 4], fp32, c)
            desti = sb("desti", [P, EPP], i32, c)
            less = sb("less_s", [P, P], fp32, c)
            more = sb("more_s", [P, P], fp32, c)
            mring = sb("mring", [P, 2, 3, TS], i32, c)
            zeros = sb("zeros", [P, TN, D], fp32, c)
            psH = pb("psH", [P, 512], c)
            psL = [pb(f"psL{i}", [P, 512], c) for i in range(2)]
            psR = [pb(f"psR{i}", [P, 512], c) for i in range(2)]
            psH2 = [psH, pb("psH2", [P, 512], c)]
            psQ = [pb(f"psQ{i}", [P, 512], c) for i in range(2)]

            def tiles(eng, part_):
                for t in range(2):
                    part_(t, t)
                with eng.Fori(1, EPP // 2 - 1) as i:
                    part_(i * 2, 0)
                    part_(i * 2 + 1, 1)
                for t in range(EPP - 2, EPP):
                    part_(t, t % 2)

            with nc.Block() as block:
                @block.sync
                def _(sp):
                    sp.wait_ge(s_set, 2)
                    for buf, name in ((keyi, "src"), (desti, "dst")):
                        sp.dma_start(buf[0:P - 1, :], a[name][0:(P - 1) * EPP].rearrange("(p t) -> p t", t=EPP)).then_inc(s_ld, 16)
                        sp.dma_start(buf[P - 1:P, 0:E - (P - 1) * EPP], a[name][(P - 1) * EPP:E].rearrange("(p t) -> p t", p=1)).then_inc(s_ld, 16)
                    sp.wait_ge(s_set, 3)
                    with sp.Fori(0, STEPS) as i:
                        for t in (E1, E2, E3):
                            sp.dma_start(node_rows(t, i), zeros[:, :, :]).then_inc(s_zero, 16)
                    sp.wait_ge(s_zero, 48 * STEPS)

                @block.gpsimd
                def _(pool):
                    last_record, last_target = pool.to_reg(P * EPP - 1), pool.to_reg(NPAD - 1)
                    nc.gpsimd.iota(columns[:, :], [[1, KH]], base=0, channel_multiplier=0, allow_small_or_imprecise_dtypes=True).then_inc(s_iota, 1)
                    nc.gpsimd.affine_select(out=less[:, :], in_=ones[:, :], compare_op=ALU.is_gt, fill=0.0, base=0, pattern=[[1, P]], channel_multiplier=-1).then_inc(s_iota, 1)
                    nc.gpsimd.affine_select(out=more[:, :], in_=ones[:, :], compare_op=ALU.is_gt, fill=0.0, base=0, pattern=[[-1, P]], channel_multiplier=1).then_inc(s_iota, 1)
                    def enter(s):
                        wait(pool, s_mv[s.par], (s.n - s.par) * 8 * TS)
                        nc.gpsimd.tensor_copy(mring[:, s.par, 0, :], endidx[:, bass.ds(s.n * TS, TS)]).then_inc(s_mcp, 1)
                        nc.gpsimd.tensor_copy(mring[:, s.par, 1, :], endrow[:, bass.ds(s.n * TS, TS)]).then_inc(s_mcp, 1)
                        indices(pool, s_mcp, s.n * 2 + 2)
                        for k in range(TS):
                            pool.indirect_dma_start(out=row_of_node, out_offset=bass.IndirectOffsetOnAxis(ap=mring[:, s.par, 0, k:k + 1], axis=0),
                                                    in_=mring[:, s.par, 1, k:k + 1], in_offset=None, bounds_check=last_target, oob_is_err=False).then_inc(s_mv[s.par], 16)

                    def each(part, first, steps):
                        for n in (0, 1):
                            part(Step(first + n, n))
                        with pool.Fori(1, steps // 2) as i:
                            for n in (0, 1):
                                part(Step(i * 2 + first + n, n))

                    each(enter, 0, STEPS)
                    for i in range(2):
                        pool.wait_ge(s_mv[i], 16 * TS * (STEPS // 2))

                    def look_up(s):
                        pool.wait_ge(s_mv[s.par], (s.n - s.par + STEPS) * 8 * TS)
                        if not (isinstance(s.n, int) and s.n < 2):
                            nc.gpsimd.tensor_copy(gidx[:, bass.ds(s.n * TS - 2 * TS, TS)], mring[:, s.par, 2, :]).then_inc(s_mcp, 1)
                        else:
                            nc.gpsimd.tensor_copy(mring[:, s.par, 2, :], mring[:, s.par, 1, :]).then_inc(s_mcp, 1)
                        nc.gpsimd.tensor_copy(mring[:, s.par, 0, :], srcidx[:, bass.ds(s.n * TS, TS)]).then_inc(s_mcp, 1)
                        indices(pool, s_mcp, s.n * 2 + 2 * STEPS + 2)
                        for k in range(TS):
                            gather(pool, mring[:, s.par, 2, k:k + 1], row_of_node, mring[:, s.par, 0, k:k + 1], s_mv[s.par], last_target)

                    each(look_up, 0, STEPS)
                    for i in range(2):
                        pool.wait_ge(s_mv[i], 32 * TS * (STEPS // 2))
                        nc.gpsimd.tensor_copy(gidx[:, (STEPS - 2 + i) * TS:(STEPS - 1 + i) * TS], mring[:, i, 2, :]).then_inc(s_mcp, 1)

                    pool.wait_ge(s_rec, 1)
                    for t in range(EPP):
                        pool.indirect_dma_start(out=records, out_offset=bass.IndirectOffsetOnAxis(ap=placei[:, t:t + 1], axis=0), in_=rec[:, t, :], in_offset=None,
                                                bounds_check=last_record, oob_is_err=False).then_inc(ogath[t % (2 * TS)], 16)
                    for k in range(2 * TS):
                        pool.wait_ge(ogath[k], 16 * len(range(k, EPP, 2 * TS)))

                @block.tensor
                def _(pe):
                    t_ = nc.tensor

                    def count_up(t, par):
                        pe.wait_ge(s_hot, t + 1)
                        t_.matmul(psH[:, 0:KH], olo[:, par, :], ohi[:, par, :], start=isinstance(t, int) and t == 0,
                                  stop=isinstance(t, int) and t == EPP - 1).then_inc(s_hist, 1)

                    tiles(pe, count_up)
                    pe.wait_ge(s_base, 1)
                    t_.matmul(psQ[0][:, 0:1], less[:, :], part[:, 0:1], start=True, stop=True).then_inc(s_row, 1)

                    def look(t, par):
                        pe.wait_ge(s_hot, t + EPP + 1)
                        t_.transpose(psR[par][:, 0:P], olo[:, par, :], ident[:, :]).then_inc(s_tr, 1)
                        t_.matmul(psQ[par][:, 0:P], ones[:, :], diag[:, par, :], start=True, stop=True).then_inc(s_row, 1)
                        t_.matmul(psH2[par][:, 0:KH], olo[:, par, :], ohi[:, par, :], start=True, stop=True).then_inc(s_run, 1)
                        pe.wait_ge(s_tc, t + 1)
                        pe.wait_ge(s_cp, t + 1)
                        t_.matmul(psL[par][:, 0:KH], oloT[:, par, :], run[:, par, :], start=True, stop=True).then_inc(s_look, 1)

                    tiles(pe, look)

                @block.scalar
                def _(act):
                    def copies(t, par):
                        act.wait_ge(s_tr, t + 1)
                        if not (isinstance(t, int) and t < 2):
                            act.wait_ge(s_look, t - 1)
                        nc.scalar.copy(oloT[:, par, :], psR[par][:, 0:P]).then_inc(s_tc, 1)

                    tiles(act, copies)

                @block.vector
                def _(dve):
                    v = nc.vector
                    ch = Chain(dve, s_ch, 0)
                    v.memset(keyi[:, :], PAD_KEY).then_inc(s_set, 1)
                    v.memset(desti[:, :], 0).then_inc(s_set, 1)
                    v.memset(zeros[:, :, :], 0.0).then_inc(s_set, 1)
                    dve.wait_ge(s_ld, 64)
                    dve.wait_ge(s_iota, 3)
                    ch.link(v.tensor_copy(key[:, :], keyi[:, :]))
                    ch.link(v.tensor_scalar(loi[:, :], keyi[:, :], P - 1, None, ALU.bitwise_and))
                    ch.link(v.tensor_copy(lo[:, :], loi[:, :]))
                    ch.link(v.tensor_tensor(hi[:, :], key[:, :], lo[:, :], ALU.subtract))
                    ch.link(v.tensor_scalar(hi[:, :], hi[:, :], 1.0 / P, None, ALU.mult))
                    ch.link(v.memset(rec[:, :, 3], 0.0))
                    ch.link(v.tensor_copy(rec[:, :, 0], keyi[:, :]))
                    ch.link(v.tensor_copy(rec[:, :, 1], desti[:, :]))
                    ch.link(v.tensor_copy(rec[:, :, 2], weight[:, 0:EPP]))

                    def hot(t, par):
                        if isinstance(t, int):
                            wait(dve, s_hist, t - 1)
                        else:
                            dve.wait_ge(s_hist, t - 1)
                        v.tensor_scalar(olo[:, par, :], columns[:, 0:P], lo[:, bass.ds(t, 1)], None, ALU.is_equal)
                        v.tensor_scalar(ohi[:, par, :], columns[:, :], hi[:, bass.ds(t, 1)], None, ALU.is_equal).then_inc(s_hot, 1)

                    tiles(dve, hot)
                    dve.wait_ge(s_hist, EPP)
                    ch.link(v.tensor_copy(count[:, :], psH[:, 0:KH]))
                    ch.link(v.tensor_tensor_scan(base[:, :], ones[:, 0:1].to_broadcast([P, KH]), count[:, :], 0.0, ALU.mult, ALU.add))
                    v.reduce_sum(part[:, 0:1], count[:, :], AX.X).then_inc(s_base, 1)
                    dve.wait_ge(s_row, 1)
                    ch.link(v.tensor_tensor(base[:, :], base[:, :], count[:, :], ALU.subtract))
                    v.tensor_scalar(run[:, 0, :], base[:, :], psQ[0][:, 0:1], None, ALU.add).then_inc(s_cp, 1)

                    def spread_out(t, par):
                        if not (isinstance(t, int) and t < 2):
                            dve.wait_ge(s_look, t - 1)
                        v.tensor_scalar(olo[:, par, :], columns[:, 0:P], lo[:, bass.ds(t, 1)], None, ALU.is_equal)
                        v.tensor_scalar(diag[:, par, :], ident[:, :], key[:, bass.ds(t, 1)], None, ALU.mult)
                        v.tensor_scalar(ohi[:, par, :], columns[:, :], hi[:, bass.ds(t, 1)], None, ALU.is_equal).then_inc(s_hot, 1)

                    def position(t, par):
                        if not (isinstance(t, int) and t == EPP - 1):
                            spread_out(t + 1, 1 - par)
                        dve.wait_ge(s_run, t + 1)
                        dve.wait_ge(s_cp, t + 1)
                        v.tensor_tensor(run[:, 1 - par, :], run[:, par, :], psH2[par][:, 0:KH], ALU.add).then_inc(s_cp, 1)
                        dve.wait_ge(s_row, t + 2)
                        v.scalar_tensor_tensor(twin[:, :], psQ[par][:, 0:P], key[:, bass.ds(t, 1)], more[:, :], ALU.is_equal, ALU.mult).then_inc(s_pos, 1)
                        dve.wait_ge(s_look, t + 1)
                        v.tensor_tensor(picked[:, :], psL[par][:, 0:KH], ohi[:, par, :], ALU.mult).then_inc(s_pos, 1)
                        dve.wait_ge(s_pos, t * 5 + 1)
                        v.reduce_sum(part[:, 0:1], twin[:, :], AX.X).then_inc(s_pos, 1)
                        dve.wait_ge(s_pos, t * 5 + 2)
                        v.reduce_sum(part[:, 1:2], picked[:, :], AX.X).then_inc(s_pos, 1)
                        dve.wait_ge(s_pos, t * 5 + 4)
                        v.tensor_tensor(place[:, bass.ds(t, 1)], part[:, 0:1], part[:, 1:2], ALU.add).then_inc(s_pos, 1)

                    spread_out(0, 0)
                    tiles(dve, position)
                    dve.wait_ge(s_pos, 5 * EPP)
                    v.tensor_copy(placei[:, :], place[:, :]).then_inc(s_rec, 1)
            closing([s_ld, s_iota, s_ch, s_hot, s_hist, s_base, s_row, s_tr, s_tc, s_look, s_run, s_cp, s_pos, s_rec, s_set, s_zero, s_mcp], c)

        with ExitStack() as c:
            s_ld, s_set, s_ch, s_iota, s_dg, s_row = names("masks_", c, "loaded", "cleared", "chain", "iota", "diagonal", "row_spread")
            rec = sb("rec_b", [P, EPP, 4], fp32, c)
            before_ = sb("before_", [P, 1], fp32, c)
            after_ = sb("after_", [P, 1], fp32, c)
            prev = sb("prev_b", [P, EPP], fp32, c)
            nxt = sb("nxt_b", [P, EPP], fp32, c)
            endm = sb("endm_b", [P, EPP], fp32, c)
            side = sb("side_b", [P, EPP], fp32, c)
            act_ = sb("sideact_b", [P, 1], fp32, c)
            t0 = sb("t0_b", [P, TP], fp32, c)
            t1 = sb("t1_b", [P, TP], fp32, c)
            cont = sb("cont_b", [P, 1], fp32, c)
            dg = sb("dg_b", [P, P], fp32, c)
            less = sb("less_b", [P, P], fp32, c)
            psr = pb("psr_b", [P, P], c)
            with nc.Block() as block:
                @block.sync
                def _(sp):
                    sp.wait_ge(s_set, 2)
                    sp.dma_start(rec[:, :, :], records.rearrange("(p t) f -> p t f", p=P)).then_inc(s_ld, 16)
                    byrow = records.rearrange("(p t) f -> p t f", p=P)
                    sp.dma_start(before_[1:P, :], byrow[0:P - 1, EPP - 1, 0:1], allow_slow_non_contiguous=True).then_inc(s_ld, 16)
                    sp.dma_start(after_[0:P - 1, :], byrow[1:P, 0, 0:1], allow_slow_non_contiguous=True).then_inc(s_ld, 16)

                @block.gpsimd
                def _(pool):
                    nc.gpsimd.affine_select(out=less[:, :], in_=ones[:, :], compare_op=ALU.is_gt, fill=0.0, base=0, pattern=[[1, P]], channel_multiplier=-1).then_inc(s_iota, 1)

                @block.tensor
                def _(pe):
                    pe.wait_ge(s_dg, 1)
                    nc.tensor.matmul(psr[:, :], ones[:, :], dg[:, :], start=True, stop=True).then_inc(s_row, 1)

                @block.vector
                def _(dve):
                    v = nc.vector
                    ch = Chain(dve, s_ch, 0)
                    A = slice(0, EPP)
                    v.memset(before_[:, :], -1.0).then_inc(s_set, 1)
                    v.memset(after_[:, :], -1.0).then_inc(s_set, 1)
                    for t in (sameb, leadb, weightb, t1):
                        ch.link(v.memset(t[:, :], 0.0))
                    dve.wait_ge(s_ld, 48)
                    dve.wait_ge(s_iota, 1)
                    src_ = rec[:, :, 0]
                    ch.link(v.tensor_copy(prev[:, 1:EPP], rec[:, 0:EPP - 1, 0]))
                    ch.link(v.tensor_copy(prev[:, 0:1], before_[:, :]))
                    ch.link(v.tensor_copy(nxt[:, 0:EPP - 1], rec[:, 1:EPP, 0]))
                    ch.link(v.tensor_copy(nxt[:, EPP - 1:EPP], after_[:, :]))
                    v.tensor_scalar(dg[:, :], ident[:, :], rec[:, 0, 0:1], None, ALU.mult).then_inc(s_dg, 1)
                    ch.link(v.tensor_copy(weightb[:, A], rec[:, :, 2]))
                    ch.link(v.tensor_copy(t1[:, A], rec[:, :, 1]))
                    ch.link(v.tensor_copy(dstb[:, :], t1[:, :]))
                    ch.link(v.tensor_tensor(sameb[:, 1:EPP], rec[:, 1:EPP, 0], prev[:, 1:EPP], ALU.is_equal))
                    ch.link(v.tensor_tensor(cont[:, :], rec[:, 0, 0:1], prev[:, 0:1], ALU.is_equal))
                    ch.link(v.tensor_tensor(endm[:, :], src_, nxt[:, :], ALU.not_equal))
                    ch.link(v.tensor_scalar(leadb[:, A], src_, rec[:, 0, 0:1], None, ALU.is_equal))
                    ch.link(v.scalar_tensor_tensor(side[:, :], endm[:, :], cont[:, 0:1], leadb[:, A], ALU.mult, ALU.mult))
                    ch.link(v.tensor_tensor(endm[:, :], endm[:, :], side[:, :], ALU.subtract))
                    ch.link(v.reduce_max(act_[:, :], side[:, :], AX.X))
                    ch.link(v.memset(t0[:, :], float(OUT_OF_RANGE)))
                    ch.link(v.tensor_scalar(t1[:, A], src_, float(OUT_OF_RANGE), None, ALU.subtract))
                    ch.link(v.tensor_tensor(prev[:, :], t1[:, A], endm[:, :], ALU.mult))
                    ch.link(v.tensor_tensor(t0[:, A], t0[:, A], prev[:, :], ALU.add))
                    ch.link(v.tensor_tensor(prev[:, 0:1], t1[:, 0:1], act_[:, :], ALU.mult))
                    ch.link(v.tensor_tensor(t0[:, SIDE:SIDE + 1], t0[:, SIDE:SIDE + 1], prev[:, 0:1], ALU.add))
                    ch.link(v.tensor_copy(outb[:, :], t0[:, :]))
                    dve.wait_ge(s_row, 1)
                    ch.link(v.scalar_tensor_tensor(mleftb[:, :], psr[:, :], rec[:, EPP - 1, 0:1], less[:, :], ALU.is_equal, ALU.mult))
            closing([s_ld, s_set, s_ch, s_iota, s_dg, s_row], c)

        with ExitStack() as c:
            X = sb("X0", [P, 2 * TS, D], fp32, c)
            acc = sb("acc0", [P, 2 * TS, D], fp32, c)
            cap = sb("cap0", [P, D], fp32, c)
            own = [sb(f"own0_{i}", [P, U, D], fp32, c) for i in range(2)]
            y = [sb(f"y0_{i}", [P, U, D], fp32, c) for i in range(2)]
            z = [sb(f"z0_{i}", [P, U, D], fp32, c) for i in range(2)]
            rest = [sb(f"rest0_{i}", [P, U, D], fp32, c) for i in range(2)]
            res = [sb(f"res0_{i}", [P, U, D], fp32, c) for i in range(2)]
            xT = sb("xT0", [P, 3, TS * P], fp32, c)
            eT = sb("eT0", [P, 2, P], fp32, c)
            prod = sb("prod", [P, 2, R, D], fp32, c)
            msg = sb("msg", [P, 2, D], fp32, c)
            psT = [pb(f"psT{i}", [P, TS * P], c) for i in range(2)]
            psO = [pb(f"psO{i}", [P, TS * P], c) for i in range(2)]
            psY = [pb(f"psY{i}", [P, R * D], c) for i in range(2)]
            loaded = names("r0_", c, "own_loaded0", "own_loaded1")
            stored = names("r0_", c, "stored0", "stored1")
            rest_ = names("r0_", c, "indices_ready", "edge_transposed", "transposed", "edge_evacuated", "evacuated", "relations_done",
                          "relations_weighted", "message_ready", "cap_ready", "sum_ready", "product_ready", "relu_done", "chain1", "chain2", "residual_ready",
                          "var1", "std1", "norm1", "applied1", "added", "var2", "std2", "norm2", "result_ready", "carry_ready", "cleared")
            (s_idx, s_etr, s_tr, s_eev, s_ev, s_rel, s_relmul, s_msg, s_cap, s_sum, s_out, s_y, s_ch1, s_ch2, s_rest, s_var1, s_std1, s_norm1, s_app1,
             s_added, s_var2, s_std2, s_norm2, s_res, s_carry, s_set) = rest_
            GROUPS = (1, 2, 0)

            def nodes_loaded(eng, s):
                if not s.last:
                    eng.wait_ge(loaded[s.par], arrived(s) + (16 if isinstance(s.n, int) and s.n == STEPS - 2 else 0))

            with nc.Block() as block:
                @block.sync
                def _(sp):
                    def load(s):
                        wait(sp, s_tr, free(s, 3))
                        wait(sp, s_rest, free(s, 1))
                        if isinstance(s.n, int) and (s.n + 1) * TN * P > N:
                            rest = max(0, N - s.n * TN * P) // TN
                            if rest:
                                src = a["x"][s.n * TN * P:N, :].rearrange("(p j) f -> p j f", j=TN)
                                for p0, p1 in ((0, rest // 16 * 16), (rest // 16 * 16, rest)):
                                    sp.dma_start(own[s.par][p0:p1, TS:U, :], src[p0:p1]).then_inc(loaded[s.par], 16)
                            return
                        src = a["x"][bass.ds(s.n * TN * P, TN * P), :].rearrange("(p j) f -> p j f", j=TN)
                        sp.dma_start(own[s.par][:, TS:U, :], src).then_inc(loaded[s.par], 16)

                    def store(s):
                        sp.wait_ge(s_res, s.n + 1)
                        sp.dma_start(node_rows(X1, s.n), res[s.par][:, TS:U, :]).then_inc(stored[s.par], 16)
                        sp.dma_start(slot_rows(X1, s.n), res[s.par][:, 0:TS, :]).then_inc(stored[s.par], 16)

                    pipelined(sp, [(load, 2), (store, -2)])
                    for i in range(2):
                        sp.wait_ge(stored[i], 32 * (STEPS // 2))

                @block.gpsimd
                def _(pool):
                    last_node = pool.to_reg(N - 1)
                    def fetch(s):
                        wait(pool, s_etr, free(s, TS))
                        nc.gpsimd.tensor_copy(idxr[:, s.par, 0:TS], srcidx[:, bass.ds(s.n * TS, TS)]).then_inc(s_idx, 1)
                        indices(pool, s_idx, s.n * 2 + 1)
                        for k in range(TS):
                            if not s.last:
                                gather(pool, X[:, s.par * TS + k, :], a["x"], idxr[:, s.par, k:k + 1], gath[s.par * TS + k], last_node)
                        wait(pool, s_tr, free(s, 3))
                        nc.gpsimd.tensor_copy(idxr[:, s.par, TS:2 * TS], ownidx[:, bass.ds(s.n * TS, TS)]).then_inc(s_idx, 1)
                        indices(pool, s_idx, s.n * 2 + 2)
                        for k in range(TS):
                            gather(pool, own[s.par][:, k, :], a["x"], idxr[:, s.par, TS + k:TS + k + 1], ogath[s.par * TS + k], last_node)

                    def residual(s):
                        for k in range(TS):
                            slot_rows_moved(pool, s, k)
                        nodes_loaded(pool, s)
                        wait(pool, s_added, free(s, 1))
                        nc.gpsimd.tensor_tensor(rest[s.par][:, :, :], own[s.par][:, :, :], spread(rows["L0_gnn_beta"], U), ALU.add).then_inc(s_rest, 1)

                    pipelined(pool, [(fetch, 2), (residual, 1)])

                @block.tensor
                def _(pe):
                    t = nc.tensor

                    def relations(s, k):
                        pe.wait_ge(s_eev, s.n * TS + k + 1)
                        wait(pe, s_relmul, s.n * TS + k - 1)
                        for half in range(2):
                            m = t.matmul(psY[k % 2][:, half * 512:(half + 1) * 512], eT[:, k % 2, :],
                                         wrel[:, half * 4:half * 4 + 4, :], start=True, stop=True)
                        m.then_inc(s_rel, 1)

                    def edges(s):
                        if s.last:
                            pe.wait_ge(s_sum, EPP)
                            pe.wait_ge(s_relmul, EPP)
                            t.matmul(psY[0][:, 0:P], mleft[:, :], acc[:, (SIDE - 1) % (2 * TS), :], start=True, stop=True).then_inc(s_carry, 1)
                            return
                        for k in range(TS):
                            edge_rows(pe, s, k)
                            wait(pe, s_eev, s.n * TS + k)
                            t.transpose(psT[0][:, 0:P], X[:, s.par * TS + k, :], ident[:, :]).then_inc(s_etr, 1)
                            relations(s, k)

                    def product(s, q):
                        u = s.n * 3 + q
                        ps = psO[(s.par + q) % 2]
                        pe.wait_ge(s_ev, u + 1)
                        wait(pe, s_y, u - 1)
                        t.matmul(ps[:, :], ones[0:1, :], biases["L0_gnn_b_self"][0:1, :, :], start=True, stop=False)
                        if q == 2:
                            pe.wait_ge(s_sum, s.n * TS + TS)
                        for j in range(TS):
                            if q == 2:
                                t.matmul(ps[:, j * P:(j + 1) * P], ident[:, :], acc[:, s.par * TS + j, :], start=False, stop=False)
                            m = t.matmul(ps[:, j * P:(j + 1) * P], xT[:, q, j * P:(j + 1) * P], wself[:, :], start=False, stop=j == TS - 1)
                        m.then_inc(s_out, 1)

                    def nodes(s):
                        for q, g in enumerate(GROUPS):
                            wait(pe, s_ev, s.n * 3 + q)
                            if g == 0:
                                for k in range(TS):
                                    pe.wait_ge(ogath[s.par * TS + k], placed[s.par * TS + k] + arrived(s))
                            elif g == 1:
                                nodes_loaded(pe, s)
                            for j in range(TS):
                                m = t.transpose(psT[1][:, j * P:(j + 1) * P], own[s.par][:, g * TS + j, :], ident[:, :])
                            m.then_inc(s_tr, 1)
                            product(s, q)

                    pipelined(pe, [(edges, 1), (nodes, 1)])

                @block.scalar
                def _(act):
                    sc = nc.scalar

                    def copy_edges(s, ks):
                        if s.last:
                            return
                        for k in ks:
                            n = s.n * TS + k
                            act.wait_ge(s_etr, n + 1)
                            wait(act, s_rel, n - 1)
                            sc.copy(eT[:, k % 2, :], psT[0][:, 0:P]).then_inc(s_eev, 1)

                    def first_edges(s):
                        copy_edges(s, range(0, 2))

                    def last_edges(s):
                        copy_edges(s, range(2, TS))

                    def nodes(s):
                        for q, g in enumerate(GROUPS):
                            u = s.n * 3 + q
                            act.wait_ge(s_tr, u + 1)
                            wait(act, s_out, u - 2)
                            sc.copy(xT[:, q, :], psT[1][:, :]).then_inc(s_ev, 1)
                            act.wait_ge(s_out, u + 1)
                            if q == 0:
                                wait(act, s_app1, free(s, 1))
                            sc.activation(y[s.par][:, g * TS:(g + 1) * TS, :], psO[(s.par + q) % 2][:, :], ACT.Relu).then_inc(s_y, 1)

                    def first_std(s):
                        deviate(act, s, 0, 0, s_var1, s_std1)

                    def first_norm(s):
                        wait(act, s_res, free(s, 1))
                        normalize(act, s, 0, y[s.par], z[s.par], 0, s_norm1, s_app1)

                    def second_std(s):
                        deviate(act, s, 1, 0, s_var2, s_std2)

                    def second_norm(s):
                        wait(act, stored[s.par], (s.n - s.par) * 16)
                        normalize(act, s, 1, z[s.par], res[s.par], 0, s_norm2, s_res)

                    pipelined(act, [(first_edges, 1), (first_std, 0), (second_norm, -2), (last_edges, 1), (first_norm, 0), (nodes, 1), (second_std, -1)])

                @block.vector
                def _(dve):
                    v = nc.vector
                    v.memset(acc[:, :, :], 0.0).then_inc(s_set, 1)
                    v.memset(cap[:, :], 0.0).then_inc(s_set, 1)
                    dve.wait_ge(s_set, 2)
                    ch1, ch2 = Chain(dve, s_ch1, U + LN_LINKS), Chain(dve, s_ch2, U + LN_LINKS + 1)

                    def edges(s):
                        wait(dve, s_out, free(s, 3))
                        if s.last:
                            side_sums(acc, cap, psY[0][:, 0:P], s_sum, s_carry, dve)
                            return
                        for k in range(TS):
                            n = s.n * TS + k
                            dve.wait_ge(s_rel, n + 1)
                            w = coef[:, bass.ds(n, 1), :].rearrange("p a r -> p (a r)").unsqueeze(2).to_broadcast([P, R, D])
                            v.tensor_tensor(prod[:, k % 2, :, :], psY[k % 2][:, :].rearrange("p (r f) -> p r f", r=R), w, ALU.mult).then_inc(s_relmul, 1)
                            dve.wait_ge(s_relmul, n + 1)
                            v.reduce_sum(msg[:, k % 2, :], prod[:, k % 2, :, :].rearrange("p r f -> p f r"), AX.X).then_inc(s_msg, 1)
                            dve.wait_ge(s_msg, n + 1)
                            scan_edge(s, k, msg[:, k % 2, :], acc, cap, s_sum, s_cap, dve)

                    def first_norm(s):
                        ch1.begin(s)
                        dve.wait_ge(s_y, s.n * 3 + 3)
                        normalizing(dve, ch1, s, 0, y[s.par], 0, s_var1, s_std1, s_norm1)

                    def second_norm(s):
                        ch2.begin(s)
                        zs = z[s.par][:, :, :]
                        dve.wait_ge(s_app1, s.n + 1)
                        ch2.link(v.tensor_tensor(zs, zs, spread(rows["L0_gnn_gamma"], U), ALU.mult))
                        dve.wait_ge(s_rest, s.n + 1)
                        v.tensor_tensor(zs, zs, rest[s.par][:, :, :], ALU.add).then_inc(s_added, 1)
                        dve.wait_ge(s_added, s.n + 1)
                        normalizing(dve, ch2, s, 1, z[s.par], 0, s_var2, s_std2, s_norm2)

                    pipelined(dve, [(first_norm, 0), (edges, 1), (second_norm, -1)])
            edges_gathered()
            slots_moved()
            closing([*loaded, *stored, *rest_], c)

        for k_, (src_table, dst_table) in enumerate(((X1, H1), (H1, X2))):
            c = ExitStack()
            with c:
                pre = f"r{k_ + 1}_"
                X = sb(pre + "X", [P, 2 * TS, D], fp32, c)
                acc = sb(pre + "acc", [P, 2 * TS, D], fp32, c)
                cap = sb(pre + "cap", [P, D], fp32, c)
                own = [sb(pre + f"own{i}", [P, U, D], fp32, c) for i in range(2)]
                old = [sb(pre + f"old{i}", [P, U, D], fp32, c) for i in range(2)] if k_ else None
                y = [sb(pre + f"y{i}", [P, U, D], fp32, c) for i in range(2)]
                z = [sb(pre + f"z{i}", [P, U, D], fp32, c) for i in range(2)]
                res = [sb(pre + f"res{i}", [P, U, D], fp32, c) for i in range(2)]
                xT = sb(pre + "xT", [P, 4, TS * P], fp32, c)
                psT = [pb(pre + f"psT{i}", [P, TS * P], c) for i in range(4)]
                psO = [pb(pre + f"psO{i}", [P, TS * P], c) for i in range(2)]
                psC = pb(pre + "psC", [P, D], c)
                loaded = names(pre, c, "own_loaded0", "own_loaded1")
                old_loaded = names(pre, c, "old_loaded0", "old_loaded1")
                stored = names(pre, c, "stored0", "stored1")
                rest_ = names(pre, c, "indices_ready", "transposed", "evacuated", "edge_weighted", "cap_ready", "sum_ready", "product_ready",
                              "y_ready", "chain1", "chain2", "var1", "std1", "norm1", "applied1", "scaled", "var2", "std2", "norm2", "result_ready",
                              "carry_ready", "cleared")
                (s_idx, s_tr, s_ev, s_wtd, s_cap, s_sum, s_out, s_y, s_ch1, s_ch2, s_var1, s_std1, s_norm1, s_app1, s_scaled, s_var2, s_std2,
                 s_norm2, s_res, s_carry, s_set) = rest_
                ORDER = (1, 2, 0)
                TQ = 4

                with nc.Block() as block:
                    @block.sync
                    def _(sp):
                        def load(s):
                            wait(sp, s_tr, free(s, TQ))
                            sp.dma_start(own[s.par][:, TS:U, :], node_rows(src_table, s.n)).then_inc(loaded[s.par], 16)
                            sp.dma_start(own[s.par][:, 0:TS, :], slot_rows(src_table, s.n)).then_inc(loaded[s.par], 16)

                        def load_old(s):
                            wait(sp, s_scaled, free(s, 1))
                            sp.dma_start(old[s.par][:, TS:U, :], node_rows(X1, s.n)).then_inc(old_loaded[s.par], 16)
                            sp.dma_start(old[s.par][:, 0:TS, :], slot_rows(X1, s.n)).then_inc(old_loaded[s.par], 16)

                        def store(s):
                            sp.wait_ge(s_res, s.n + 1)
                            sp.dma_start(node_rows(dst_table, s.n), res[s.par][:, TS:U, :]).then_inc(stored[s.par], 16)
                            sp.dma_start(slot_rows(dst_table, s.n), res[s.par][:, 0:TS, :]).then_inc(stored[s.par], 16)

                        pipelined(sp, [(load, 2), (store, -1), (load_old, 1)] if k_ else [(load, 2), (store, -1)])
                        for i in range(2):
                            sp.wait_ge(stored[i], 32 * (STEPS // 2))

                    @block.gpsimd
                    def _(pool):
                        last_row = pool.to_reg(src_table.shape[0] - 1)
                        def fetch(s):
                            if s.last:
                                return
                            wait(pool, s_sum, free(s, TS))
                            wait(pool, s_cap, free(s, TS))
                            nc.gpsimd.tensor_copy(idxr[:, s.par, 0:TS], gidx[:, bass.ds(s.n * TS, TS)]).then_inc(s_idx, 1)
                            indices(pool, s_idx, s.n + 1)
                            for k in range(TS):
                                gather(pool, X[:, s.par * TS + k, :], src_table, idxr[:, s.par, k:k + 1], gath[s.par * TS + k], last_row)

                        pipelined(pool, [(fetch, 2)])

                    @block.tensor
                    def _(pe):
                        t = nc.tensor

                        def nodes(s):
                            for q, g in enumerate(ORDER):
                                wait(pe, s_ev, (s.n - 1) * TQ + q + 1)
                                if q == 0:
                                    pe.wait_ge(loaded[s.par], (s.n - s.par) * 16 + 32)
                                for j in range(TS):
                                    m = t.transpose(psT[q][:, j * P:(j + 1) * P], own[s.par][:, g * TS + j, :], ident[:, :])
                                m.then_inc(s_tr, 1)
                            if s.last:
                                pe.wait_ge(s_sum, EPP)
                                t.matmul(psC[:, :], mleft[:, :], acc[:, (SIDE - 1) % (2 * TS), :], start=True, stop=True).then_inc(s_carry, 1)
                            pe.wait_ge(s_sum, s.n * TS + TS)
                            wait(pe, s_ev, s.n * TQ)
                            for j in range(TS):
                                m = t.transpose(psT[3][:, j * P:(j + 1) * P], acc[:, s.par * TS + j, :], ident[:, :])
                            m.then_inc(s_tr, 1)
                            for q, g in enumerate(ORDER):
                                u = s.n * 3 + q
                                ps = psO[(s.par + q) % 2]
                                pe.wait_ge(s_ev, s.n * TQ + (q + 1 if g else TQ))
                                wait(pe, s_y, u - 1)
                                t.matmul(ps[:, :], ones[0:1, :], biases[f"L1_gnn_b_l{k_}"][0:1, :, :], start=True, stop=False)
                                for j in range(TS):
                                    if g == 0:
                                        t.matmul(ps[:, j * P:(j + 1) * P], xT[:, 3, j * P:(j + 1) * P], wsage[:, 2 * k_, :], start=False, stop=False)
                                    m = t.matmul(ps[:, j * P:(j + 1) * P], xT[:, q, j * P:(j + 1) * P], wsage[:, 2 * k_ + 1, :], start=False, stop=j == TS - 1)
                                m.then_inc(s_out, 1)

                        pipelined(pe, [(nodes, 1)])

                    @block.scalar
                    def _(act):
                        sc = nc.scalar

                        def edges(s):
                            if s.last:
                                return
                            for k in range(TS):
                                edge_rows(act, s, k)
                                sc.activation(X[:, s.par * TS + k, :], X[:, s.par * TS + k, :], ACT.Copy, scale=rdeg[:, bass.ds(s.n * TS + k, 1)]).then_inc(s_wtd, 1)

                        def transposes(s):
                            for q in range(TQ):
                                act.wait_ge(s_tr, s.n * TQ + q + 1)
                                wait(act, s_out, s.n * 3 + (q - 2 if q < 3 else 0))
                                sc.copy(xT[:, q, :], psT[q][:, :]).then_inc(s_ev, 1)

                        def products(s):
                            for q, g in enumerate(ORDER):
                                act.wait_ge(s_out, s.n * 3 + q + 1)
                                if q == 0:
                                    wait(act, s_app1, free(s, 1))
                                sc.copy(y[s.par][:, g * TS:(g + 1) * TS, :], psO[(s.par + q) % 2][:, :]).then_inc(s_y, 1)

                        def first_std(s):
                            deviate(act, s, 0, 0, s_var1, s_std1)

                        def first_norm(s):
                            wait(act, s_res, free(s, 1))
                            normalize(act, s, 0, y[s.par], z[s.par], 0, s_norm1, s_app1)

                        def second_std(s):
                            if k_:
                                deviate(act, s, 1, 0, s_var2, s_std2)

                        def finish(s):
                            wait(act, stored[s.par], (s.n - s.par) * 16)
                            if k_:
                                normalize(act, s, 1, z[s.par], res[s.par], 0, s_norm2, s_res)
                            else:
                                act.wait_ge(s_scaled, s.n + 1)
                                sc.activation(res[s.par][:, :, :], z[s.par][:, :, :], ACT.Relu).then_inc(s_res, 1)

                        pipelined(act, [(transposes, 1), (first_std, 0), (first_norm, 0), (products, 1), (second_std, -1), (edges, 2), (finish, -1)])

                    @block.vector
                    def _(dve):
                        v = nc.vector
                        v.memset(acc[:, :, :], 0.0).then_inc(s_set, 1)
                        v.memset(cap[:, :], 0.0).then_inc(s_set, 1)
                        dve.wait_ge(s_set, 2)
                        ch1, ch2 = Chain(dve, s_ch1, U + LN_LINKS), Chain(dve, s_ch2, k_ * (U + LN_LINKS) + 1 + k_)

                        def edges(s):
                            wait(dve, s_tr, free(s, TQ))
                            if s.last:
                                side_sums(acc, cap, psC[:, :], s_sum, s_carry, dve)
                                return
                            for k in range(TS):
                                dve.wait_ge(s_wtd, s.n * TS + k + 1)
                                scan_edge(s, k, X[:, s.par * TS + k, :], acc, cap, s_sum, s_cap, dve)

                        def first_norm(s):
                            ch1.begin(s)
                            dve.wait_ge(s_y, s.n * 3 + 3)
                            normalizing(dve, ch1, s, 0, y[s.par], 0, s_var1, s_std1, s_norm1)

                        def second_norm(s):
                            ch2.begin(s)
                            zs = z[s.par][:, :, :]
                            dve.wait_ge(s_app1, s.n + 1)
                            ch2.link(v.tensor_tensor(zs, zs, spread(rows[f"L1_gnn_gamma{k_}"], U), ALU.mult))
                            if not k_:
                                v.tensor_tensor(zs, zs, spread(rows["L1_gnn_beta0"], U), ALU.add).then_inc(s_scaled, 1)
                                return
                            ch2.link(v.tensor_tensor(zs, zs, spread(rows["L1_gnn_beta1"], U), ALU.add))
                            dve.wait_ge(old_loaded[s.par], (s.n - s.par) * 16 + 32)
                            v.scalar_tensor_tensor(zs, zs, 0.0, old[s.par][:, :, :], ALU.max, ALU.add).then_inc(s_scaled, 1)
                            dve.wait_ge(s_scaled, s.n + 1)
                            normalizing(dve, ch2, s, 1, z[s.par], 0, s_var2, s_std2, s_norm2)

                        pipelined(dve, [(edges, 1), (first_norm, 0), (second_norm, -1)])
                edges_gathered()
                closing([*loaded, *old_loaded, *stored, *rest_], c)

        with ExitStack() as c:
            buf = sb("x2buf", [P, 2 * TS, D], fp32, c)
            loaded = names("x2_", c, "loaded0", "loaded1")
            (s_idx,) = names("x2_", c, "indices_ready")
            with nc.Block() as block:
                @block.sync
                def _(sp):
                    def load(s):
                        if not (isinstance(s.n, int) and s.n < 2):
                            for k in range(TS):
                                slot_rows_free(sp, s, k)
                        sp.dma_start(buf[:, s.par * TS:(s.par + 1) * TS, :], slot_rows(X2, s.n)).then_inc(loaded[s.par], 16)

                    pipelined(sp, [(load, 2)])

                @block.gpsimd
                def _(pool):
                    last_node = pool.to_reg(N - 1)

                    def scatter(s):
                        row_numbers_free(pool, s)
                        nc.gpsimd.tensor_copy(idxr[:, s.par, 0:TS], outidx[:, bass.ds(s.n * TS, TS)]).then_inc(s_idx, 1)
                        pool.wait_ge(loaded[s.par], arrived(s))
                        indices(pool, s_idx, s.n + 1)
                        for k in range(TS):
                            scatter_rows(pool, X2[0:NPAD, :], buf[:, s.par * TS + k, :], idxr[:, s.par, k:k + 1], ogath[s.par * TS + k], last_node)

                    pipelined(pool, [(scatter, 0)])
                    for k in range(2 * TS):
                        pool.wait_ge(ogath[k], placed[k] + 8 * STEPS)
            slots_moved()
            closing([*loaded, s_idx], c)

        for k_, (src_table, sum_table) in enumerate(((X2, E1), (E1, E2), (E2, E3))):
            c = ExitStack()
            with c:
                pre = f"r{k_ + 3}_"
                X = sb(pre + "X", [P, 2 * TS, D], fp32, c)
                acc = sb(pre + "acc", [P, 2 * TS, D], fp32, c)
                cap = sb(pre + "cap", [P, D], fp32, c)
                psC = pb(pre + "psC", [P, D], c)
                rest_ = names(pre, c, "indices_ready", "targets_ready", "edge_weighted", "cap_ready", "sum_ready", "carry_ready", "cleared")
                s_idx, s_out, s_wtd, s_cap, s_sum, s_carry, s_set = rest_

                with nc.Block() as block:
                    @block.gpsimd
                    def _(pool):
                        last_node, last_row = pool.to_reg(N - 1), pool.to_reg(NPAD - 1)

                        def fetch(s):
                            if s.last:
                                return
                            wait(pool, s_cap, free(s, TS))
                            nc.gpsimd.tensor_copy(idxr[:, s.par, 0:TS], dstb[:, bass.ds(s.n * TS, TS)]).then_inc(s_idx, 1)
                            indices(pool, s_idx, s.n + 1)
                            for k in range(TS):
                                gather(pool, X[:, s.par * TS + k, :], src_table[0:NPAD, :], idxr[:, s.par, k:k + 1], gath[s.par * TS + k], last_row)

                        def scatter(s):
                            row_numbers_free(pool, s)
                            nc.gpsimd.tensor_copy(idxr[:, s.par, TS:2 * TS], outb[:, bass.ds(s.n * TS, TS)]).then_inc(s_out, 1)
                            pool.wait_ge(s_sum, s.n * TS + TS)
                            indices(pool, s_out, s.n + 1)
                            for k in range(TS):
                                scatter_rows(pool, sum_table, acc[:, s.par * TS + k, :], idxr[:, s.par, TS + k:TS + k + 1], ogath[s.par * TS + k], last_node)

                        pipelined(pool, [(fetch, 2), (scatter, 0)])
                        for k in range(2 * TS):
                            pool.wait_ge(ogath[k], placed[k] + 8 * STEPS)

                    @block.tensor
                    def _(pe):
                        pe.wait_ge(s_sum, EPP)
                        nc.tensor.matmul(psC[:, :], mleftb[:, :], acc[:, (SIDE - 1) % (2 * TS), :], start=True, stop=True).then_inc(s_carry, 1)

                    @block.scalar
                    def _(act):
                        def edges(s):
                            if s.last:
                                return
                            for k in range(TS):
                                edge_rows(act, s, k)
                                nc.scalar.activation(X[:, s.par * TS + k, :], X[:, s.par * TS + k, :], ACT.Copy, scale=weightb[:, bass.ds(s.n * TS + k, 1)]).then_inc(s_wtd, 1)

                        pipelined(act, [(edges, 0)])

                    @block.vector
                    def _(dve):
                        v = nc.vector
                        v.memset(acc[:, :, :], 0.0).then_inc(s_set, 1)
                        v.memset(cap[:, :], 0.0).then_inc(s_set, 1)
                        dve.wait_ge(s_set, 2)

                        def edges(s):
                            if not (isinstance(s.n, int) and s.n < 2):
                                for k in range(TS):
                                    slot_rows_free(dve, s, k)
                            if s.last:
                                side_sums(acc, cap, psC[:, :], s_sum, s_carry, dve)
                                return
                            for k in range(TS):
                                dve.wait_ge(s_wtd, s.n * TS + k + 1)
                                scan_edge(s, k, X[:, s.par * TS + k, :], acc, cap, s_sum, s_cap, dve, sameb, leadb)

                        pipelined(dve, [(edges, 0)])
                edges_gathered()
                slots_moved()
                closing(rest_, c)

        for k_ in range(3):
            c = ExitStack()
            with c:
                pre = f"n{k_}_"
                node_table, lin_table = ((X2, T1), (T1, T2), (T2, T3))[k_]
                TQ = TN // TS
                W = node_table.shape[1]
                nin = [sb(pre + f"nodes{i}", [P, TN, W], fp32, c) for i in range(2)]
                sums = [sb(pre + f"sums{i}", [P, 3, TN, D], fp32, c) for i in range(2)] if k_ == 0 else None
                z = sb(pre + "z", [P, TN, D], fp32, c) if k_ == 0 else None
                res = [sb(pre + f"res{i}", [P, TN, D], fp32, c) for i in range(2)] if k_ == 0 else None
                tout = [sb(pre + f"tout{i}", [P, TQ * TS, TW], fp32, c) for i in range(2)]
                xT = sb(pre + "xT", [P, TQ, TS * P], fp32, c)
                psT = [pb(pre + f"psT{i}", [P, TS * P], c) for i in range(2)]
                psG = [pb(pre + f"psG{i}", [P, 2, 512], c) for i in range(2)]
                loaded = names(pre, c, "nodes_loaded0", "nodes_loaded1")
                stored_res = names(pre, c, "results_stored0", "results_stored1")
                stored_lin = names(pre, c, "products_stored0", "products_stored1")
                rest_ = names(pre, c, "transposed", "evacuated", "product_ready", "product_evacuated", "chain", "var", "std", "norm",
                              "normalized", "combined")
                OWN = k_ == 1
                rows_t = sb(pre + "own_t", [P, 2 * TS, TW], fp32, c) if OWN else None
                rows_x = sb(pre + "own_x", [P, 2 * TS, D], fp32, c) if OWN else None
                moved = names(pre, c, "own_stored0", "own_stored1")
                s_idx, s_own = names(pre, c, "indices_ready", "scores_kept")
                s_tr, s_ev, s_out, s_lin, s_bch, s_var, s_std, s_norm, s_res, s_comb = rest_
                NL = 64 if k_ == 0 else 16

                def store_counts(s, each):
                    return (s.n - s.par) * (each // 2)

                def own_moved(eng, s):
                    for k in range(TS):
                        eng.wait_ge(ogath[s.par * TS + k], placed[s.par * TS + k] + (s.n - s.par) * 16 + 32)

                with nc.Block() as block:
                    if OWN:
                        @block.gpsimd
                        def _(pool):
                            last_row = pool.to_reg(NPAD - 1)

                            def fetch(s):
                                wait(pool, moved[s.par], (s.n - s.par) * 16)
                                wait(pool, s_own, free(s, 1))
                                nc.gpsimd.tensor_copy(idxr[:, s.par, 0:TS], ownidx[:, bass.ds(s.n * TS, TS)]).then_inc(s_idx, 1)
                                indices(pool, s_idx, s.n + 1)
                                for k in range(TS):
                                    i, at = s.par * TS + k, idxr[:, s.par, k:k + 1]
                                    gather(pool, rows_t[:, i, :], T1[0:NPAD, :], at, ogath[i], last_row)
                                    gather(pool, rows_x[:, i, :], X3[0:NPAD, :], at, ogath[i], last_row)

                            pipelined(pool, [(fetch, 2)])

                        @block.vector
                        def _(dve):
                            def keep(s):
                                own_moved(dve, s)
                                nc.vector.tensor_copy(ownal[:, bass.ds(s.n * TS, TS), :], rows_t[:, s.par * TS:(s.par + 1) * TS, D:TW]).then_inc(s_own, 1)

                            pipelined(dve, [(keep, 0)])

                    @block.sync
                    def _(sp):
                        def load(s):
                            if k_ == 0:
                                wait(sp, s_comb, free(s, 1))
                            else:
                                wait(sp, s_tr, free(s, TQ))
                            sp.dma_start(nin[s.par][:, :, :], node_rows(node_table, s.n)).then_inc(loaded[s.par], 16)
                            if k_ == 0:
                                for i, t in enumerate((E1, E2, E3)):
                                    sp.dma_start(sums[s.par][:, i, :, :], node_rows(t, s.n)).then_inc(loaded[s.par], 16)

                        def store_results(s):
                            sp.wait_ge(s_res, s.n + 1)
                            sp.dma_start(node_rows(X3, s.n), res[s.par][:, :, :]).then_inc(stored_res[s.par], 16)

                        def store_own(s):
                            own_moved(sp, s)
                            sp.dma_start(slot_rows(T1, s.n), rows_t[:, s.par * TS:(s.par + 1) * TS, :]).then_inc(moved[s.par], 16)
                            sp.dma_start(slot_rows(X3, s.n), rows_x[:, s.par * TS:(s.par + 1) * TS, :]).then_inc(moved[s.par], 16)

                        def store_products(s):
                            sp.wait_ge(s_lin, s.n * TQ + TQ)
                            sp.dma_start(node_rows(lin_table, s.n), tout[s.par][:, 0:TN, :]).then_inc(stored_lin[s.par], 16)

                        if k_ == 0:
                            pipelined(sp, [(load, 2), (store_results, 0), (store_products, -1)])
                        elif OWN:
                            pipelined(sp, [(load, 2), (store_own, 0), (store_products, -1)])
                        else:
                            pipelined(sp, [(load, 2), (store_products, -1)])
                        for i in range(2):
                            if OWN:
                                sp.wait_ge(moved[i], 32 * (STEPS // 2))
                            if k_ == 0:
                                sp.wait_ge(stored_res[i], 16 * (STEPS // 2))
                            sp.wait_ge(stored_lin[i], 16 * (STEPS // 2))

                    def evacuate(eng, copy, s, q):
                        eng.wait_ge(s_out, s.n * TQ + q + 1)
                        if q == 0:
                            wait(eng, stored_lin[s.par], store_counts(s, 16))
                        copy(tout[s.par][:, q * TS:(q + 1) * TS, :].rearrange("p (b j) f -> p b (j f)", b=2),
                             psG[(s.par * TQ + q) % 2][:, :, 0:2 * TW]).then_inc(s_lin, 1)

                    @block.tensor
                    def _(pe):
                        t = nc.tensor

                        def nodes(s):
                            for q in range(TQ):
                                u = s.n * TQ + q
                                wait(pe, s_ev, u - 1)
                                if q == 0 and k_:
                                    pe.wait_ge(loaded[s.par], arrived(s))
                                elif q == 0:
                                    pe.wait_ge(s_res, s.n + 1)
                                for j in range(TS):
                                    tile = res[s.par][:, q * TS + j, :] if k_ == 0 else nin[s.par][:, q * TS + j, 0:D]
                                    m = t.transpose(psT[(s.par * TQ + q) % 2][:, j * P:(j + 1) * P], tile, ident[:, :])
                                m.then_inc(s_tr, 1)
                            for q in range(TQ):
                                u = s.n * TQ + q
                                pe.wait_ge(s_ev, u + 1)
                                wait(pe, s_lin, u - 1)
                                for j in range(TS):
                                    m = t.matmul(psG[(s.par * TQ + q) % 2][:, j // 2, j % 2 * TW:(j % 2 + 1) * TW],
                                                 xT[:, q, j * P:(j + 1) * P], wgat[:, k_, :], start=True, stop=True)
                                m.then_inc(s_out, 1)

                        pipelined(pe, [(nodes, 0)])

                    @block.scalar
                    def _(act):
                        sc = nc.scalar

                        def norm(s):
                            deviate(act, s, 0, 0, s_var, s_std, TN, 0.25)
                            wait(act, stored_res[s.par], store_counts(s, 16))
                            wait(act, s_tr, free(s, TQ))
                            normalize(act, s, 0, z, res[s.par], 0, s_norm, s_res, TN)

                        def transposes(s):
                            for q in range(TQ):
                                u = s.n * TQ + q
                                act.wait_ge(s_tr, u + 1)
                                wait(act, s_out, u - TQ + 1)
                                dst, bank = xT[:, q, :], psT[(s.par * TQ + q) % 2]
                                if k_:
                                    sc.activation(dst, bank[:, :], ACT.Relu, bias=gatbias[:, k_ - 1:k_]).then_inc(s_ev, 1)
                                else:
                                    sc.copy(dst, bank[:, :]).then_inc(s_ev, 1)

                        def products(s):
                            for q in range(TQ):
                                evacuate(act, sc.copy, s, q)

                        if k_ == 0:
                            pipelined(act, [(norm, 0), (transposes, 0)])
                        else:
                            pipelined(act, [(transposes, 0), (products, -1)])

                    if k_ == 0:
                        @block.vector
                        def _(dve):
                            v = nc.vector
                            ch = Chain(dve, s_bch, TN + LN_LINKS + 3)

                            def norm(s):
                                ch.begin(s)
                                dve.wait_ge(loaded[s.par], (s.n - s.par) * (NL // 2) + NL)
                                wait(dve, s_res, s.n)
                                ch.link(v.tensor_tensor(z[:, :, :], sums[s.par][:, 0, :, :], sums[s.par][:, 1, :, :], ALU.add))
                                ch.link(v.tensor_tensor(z[:, :, :], z[:, :, :], sums[s.par][:, 2, :, :], ALU.add))
                                v.scalar_tensor_tensor(z[:, :, :], nin[s.par][:, :, :], 5.0, z[:, :, :], ALU.mult, ALU.add).then_inc(s_comb, 1)
                                dve.wait_ge(s_comb, s.n + 1)
                                normalizing(dve, ch, s, 0, z, 0, s_var, s_std, s_norm, TN, 0.25)

                            def products(s):
                                for q in range(TQ):
                                    evacuate(dve, v.tensor_copy, s, q)

                            pipelined(dve, [(norm, 0), (products, -1)])
                if OWN:
                    slots_moved()
                    slots_moved()
                closing([*loaded, *stored_res, *stored_lin, *moved, s_idx, s_own, *rest_], c)


        xrow = sb("xrow", [P, EPP, TW])
        pself = sb("pself", [P, TP, H])
        for k_ in range(3):
            pre = f"r{k_ + 6}_"
            table, next_table = ((T1, T2), (T2, T3), (T3, None))[k_]
            HH = (H, H, 1)[k_]
            CH = D // HH
            W = D + HH
            c = ExitStack()
            with c:
                first, count = ((0, 18), (18, 16), (34, 16))[k_]
                nin = [sb(pre + f"fin_nodes{i}", [P, TN, TW], fp32, c) for i in range(2)]
                x3in = [sb(pre + f"fin_x3{i}", [P, TN, D], fp32, c) for i in range(2)]
                y = [sb(pre + f"fin_y{i}", [P, TN, D], fp32, c) for i in range(2)]
                done = [sb(pre + f"fin_out{i}", [P, TN, D], fp32, c) for i in range(2)]
                z = [sb(pre + f"fin_z{i}", [P, TN, D], fp32, c) for i in range(2)]
                loaded = names(pre, c, "nodes_loaded0", "nodes_loaded1")
                x3_loaded = names(pre, c, "x3_loaded0", "x3_loaded1")
                stored = names(pre, c, "out_stored0", "out_stored1")
                rest_ = names(pre, c, "biased", "chain1", "chain2", "bias_read", "var1", "std1", "norm1", "normalized", "added", "var2", "std2", "norm2", "result_ready")
                s_y, s_ch1, s_ch2, s_bias, s_var1, s_std1, s_norm1, s_app1, s_added, s_var2, s_std2, s_norm2, s_res = rest_

                with nc.Block() as block:
                    @block.gpsimd
                    def _(pool):
                        last_row = pool.to_reg(table.shape[0] - 1)
                        for t in range(EPP):
                            gather(pool, xrow[:, t, :], table, (gidx if k_ else srcidx)[:, t:t + 1], gath[t % (2 * TS)], last_row)
                        for k in range(2 * TS):
                            pool.wait_ge(gath[k], before[k] + 16 * len(range(k, EPP, 2 * TS)))

                    @block.sync
                    def _(sp):
                        def load(s):
                            wait(sp, s_y, free(s, 1))
                            sp.dma_start(nin[s.par][:, :, :], node_rows(T3, s.n + first)).then_inc(loaded[s.par], 16)

                        def load_x3(s):
                            wait(sp, s_added, free(s, 1))
                            sp.dma_start(x3in[s.par][:, :, :], node_rows(X3, s.n + first)).then_inc(x3_loaded[s.par], 16)

                        def store(s):
                            sp.wait_ge(s_res, s.n + 1)
                            row = (s.n + first) * TN * P
                            if isinstance(row, int) and row + TN * P > N:
                                rest = max(0, N - row) // TN
                                if rest:
                                    dst = out[row:N, :].rearrange("(p j) f -> p j f", j=TN)
                                    for p0, p1 in ((0, rest // 16 * 16), (rest // 16 * 16, rest)):
                                        sp.dma_start(dst[p0:p1], done[s.par][p0:p1, :, :]).then_inc(stored[s.par], 16)
                                return
                            dst = out[bass.ds(row, TN * P), :].rearrange("(p j) f -> p j f", j=TN)
                            sp.dma_start(dst, done[s.par][:, :, :]).then_inc(stored[s.par], 16)

                        pipelined(sp, [(load, 2), (store, -1), (load_x3, 1)], count)
                        whole = min(count, N // (TN * P) - first)
                        for i in range(2):
                            sp.wait_ge(stored[i], 16 * ((whole + 1 - i) // 2) + (32 if whole < count and whole % 2 == i else 0))

                    @block.scalar
                    def _(act):
                        def first_norm(s):
                            deviate(act, s, 0, 0, s_var1, s_std1, TN)
                            wait(act, s_res, free(s, 1))
                            normalize(act, s, 0, y[s.par], z[s.par], 0, s_norm1, s_app1, TN)

                        def second_norm(s):
                            deviate(act, s, 1, 0, s_var2, s_std2, TN)
                            wait(act, stored[s.par], (s.n - s.par) * 8)
                            normalize(act, s, 1, z[s.par], done[s.par], 0, s_norm2, s_res, TN)

                        pipelined(act, [(first_norm, 0), (second_norm, -1)], count)

                    @block.vector
                    def _(dve):
                        v = nc.vector
                        ch1, ch2 = Chain(dve, s_ch1, TN + LN_LINKS), Chain(dve, s_ch2, TN + LN_LINKS + 2)

                        def bias(s):
                            dve.wait_ge(loaded[s.par], arrived(s))
                            wait(dve, s_app1, free(s, 1))
                            v.tensor_tensor(y[s.par][:, :, :], nin[s.par][:, :, 0:D], spread(rows["L3_gnn_b2"], TN), ALU.add).then_inc(s_y, 1)

                        def first_norm(s):
                            ch1.begin(s)
                            dve.wait_ge(s_y, s.n + 1)
                            normalizing(dve, ch1, s, 0, y[s.par], 0, s_var1, s_std1, s_norm1, TN)

                        def second_norm(s):
                            ch2.begin(s)
                            zs = z[s.par][:, :, :]
                            dve.wait_ge(s_app1, s.n + 1)
                            ch2.link(v.tensor_tensor(zs, zs, spread(rows["L3_gnn_gamma"], TN), ALU.mult))
                            ch2.link(v.tensor_tensor(zs, zs, spread(rows["L3_gnn_beta"], TN), ALU.add))
                            dve.wait_ge(x3_loaded[s.par], arrived(s))
                            v.tensor_tensor(zs, zs, x3in[s.par][:, :, :], ALU.add).then_inc(s_added, 1)
                            dve.wait_ge(s_added, s.n + 1)
                            normalizing(dve, ch2, s, 1, z[s.par], 0, s_var2, s_std2, s_norm2, TN)

                        pipelined(dve, [(bias, 0), (first_norm, 0), (second_norm, -1)], count)
                edges_gathered()
                closing([*loaded, *x3_loaded, *stored, *rest_], c)

            c = ExitStack()
            with c:
                bpre = pre + "w_"
                both = sb(bpre + "both", [P, EPP, 2 * HH], fp32, c)
                spreadb = sb(bpre + "spread", [P, EPP, 2 * HH], fp32, c)
                e = sb(bpre + "e", [P, EPP, HH], fp32, c)
                es = sb(bpre + "es", [P, EPP, HH], fp32, c)
                fmax = sb(bpre + "fmax", [P, EPP, HH], fp32, c)
                bmax = sb(bpre + "bmax", [P, EPP, HH], fp32, c)
                pen = sb(bpre + "pen", [P, 4, EPP], fp32, c)
                dg = sb(bpre + "dg", [P, 2 * H, P], fp32, c)
                tmp = sb(bpre + "tmp", [P, 2 * H, P], fp32, c)
                cross = sb(bpre + "cross", [P, 2 * H], fp32, c)
                psX = pb(bpre + "psX", [P, 2 * H], c)
                psM = [pb(bpre + f"psM{i}", [P, H, P], c) for i in range(2)]
                rest_ = names(bpre, c, "chain", "own_crossed", "diagonals", "maxima_crossed", "weights")
                s_ch, s_xo, s_dg, s_mc, s_w = rest_

                with nc.Block() as block:
                    def score(arr, t, side):
                        return arr[:, t, side * H:side * H + HH]

                    @block.tensor
                    def _(pe):
                        for l in range(2):
                            m = nc.tensor.matmul(psX[:, l * HH:(l + 1) * HH], mside[:, :], score(ownal, SIDE, l), start=True, stop=True)
                        m.then_inc(s_xo, 1)
                        pe.wait_ge(s_dg, 1)
                        for l in range(2):
                            for h in range(HH):
                                m = nc.tensor.matmul(psM[l][:, h, :], ones[:, :], dg[:, l * HH + h, :], start=True, stop=True)
                        m.then_inc(s_mc, 1)

                    @block.vector
                    def _(dve):
                        v = nc.vector
                        ch = Chain(dve, s_ch, 0)
                        A = slice(0, EPP)

                        def col(t, n):
                            return t.unsqueeze(2).to_broadcast([P, EPP, n])

                        for l in range(2):
                            bl = slice(l * HH, (l + 1) * HH)
                            ch.link(v.tensor_tensor(both[:, :, bl], score(ownal, A, l), col(mainend[:, A], HH), ALU.mult))
                            ch.link(v.tensor_tensor(spreadb[:, :, bl], col(sidend[:, A], HH), score(ownal, slice(SIDE, SIDE + 1), l).to_broadcast([P, EPP, HH]), ALU.mult))
                        ch.link(v.tensor_tensor(both[:, :, :], both[:, :, :], spreadb[:, :, :], ALU.add))
                        dve.wait_ge(s_xo, 1)
                        ch.link(v.scalar_tensor_tensor(both[:, EPP - 1, :], psX[:, 0:2 * HH], goes[:, EPP - 1:EPP], both[:, EPP - 1, :], ALU.mult, ALU.add))
                        for q in range(2 * HH):
                            at = ch.mark(v.tensor_tensor_scan(spreadb[:, ::-1, q], goes[:, ::-1], both[:, ::-1, q], 0.0, ALU.mult, ALU.add))
                        dve.wait_ge(s_ch, at)
                        ch.link(v.tensor_tensor(e[:, :, :], xrow[:, :, D:D + HH], spreadb[:, :, HH:2 * HH], ALU.add))
                        ch.link(v.scalar_tensor_tensor(e[:, :, :], e[:, :, :], 0.2, e[:, :, :], ALU.mult, ALU.max))
                        ch.link(v.tensor_tensor(es[:, :, :], spreadb[:, :, 0:HH], spreadb[:, :, HH:2 * HH], ALU.add))
                        ch.link(v.scalar_tensor_tensor(es[:, :, :], es[:, :, :], 0.2, es[:, :, :], ALU.mult, ALU.max))
                        for i, m in enumerate((same, goes, lead, trail)):
                            ch.link(v.tensor_scalar(pen[:, i, :], m[:, A], 1.0, BIG, ALU.subtract, ALU.mult))
                        for h in range(HH):
                            ch.mark(v.tensor_tensor_scan(fmax[:, :, h], pen[:, 0, :], e[:, :, h], -BIG, ALU.add, ALU.max))
                            at = ch.mark(v.tensor_tensor_scan(bmax[:, ::-1, h], pen[:, 1, ::-1], e[:, ::-1, h], -BIG, ALU.add, ALU.max))
                        dve.wait_ge(s_ch, at)
                        for h in range(HH):
                            ch.link(v.tensor_scalar(dg[:, h, :], ident[:, :], fmax[:, EPP - 1, h:h + 1], None, ALU.mult))
                            ch.link(v.tensor_scalar(dg[:, HH + h, :], ident[:, :], bmax[:, 0, h:h + 1], None, ALU.mult))
                        dve.sem_inc(s_dg, 1)
                        ch.link(v.tensor_tensor(fmax[:, :, :], fmax[:, :, :], bmax[:, :, :], ALU.max))
                        dve.wait_ge(s_mc, 1)
                        for l, link in enumerate((linkl, linkr)):
                            ch.link(v.tensor_tensor(tmp[:, l * HH:(l + 1) * HH, :], psM[l][:, 0:HH, :], link[:, :].unsqueeze(1).to_broadcast([P, HH, P]), ALU.add))
                        ch.link(v.reduce_max(cross[:, 0:2 * HH], tmp[:, 0:2 * HH, :], AX.X))
                        for h in range(HH):
                            for l in range(2):
                                ch.link(v.scalar_tensor_tensor(fmax[:, :, h], pen[:, 2 + l, :], cross[:, l * HH + h:l * HH + h + 1], fmax[:, :, h], ALU.add, ALU.max))
                        ch.link(v.tensor_tensor(fmax[:, :, :], fmax[:, :, :], es[:, :, :], ALU.max))
                        ch.link(v.tensor_tensor(e[:, :, :], e[:, :, :], fmax[:, :, :], ALU.subtract))
                        ch.link(v.tensor_tensor(es[:, :, :], es[:, :, :], fmax[:, :, :], ALU.subtract))
                        ch.link(v.memset(pself[:, EPP:TP, :], 1.0))
                        dve.sem_inc(s_w, 1)

                    @block.scalar
                    def _(act):
                        act.wait_ge(s_w, 1)
                        nc.scalar.activation(xrow[:, :, D:D + HH], e[:, :, :], ACT.Exp)
                        nc.scalar.activation(pself[:, 0:EPP, 0:HH], es[:, :, :], ACT.Exp)
                        nc.scalar.activation(pself[:, SIDE, 0:HH], es[:, 0, :], ACT.Exp).then_inc(s_w, 1)
                closing(rest_, c)

            c = ExitStack()
            with c:
                cpre = pre + "s_"
                LAST = k_ == 2
                acc = sb(cpre + "acc", [P, 2 * TS, W], fp32, c)
                cap = sb(cpre + "cap", [P, W], fp32, c)
                own = [sb(cpre + f"own{i}", [P, TS, TW], fp32, c) for i in range(2)]
                x3in = [sb(cpre + f"x3_{i}", [P, TS, D], fp32, c) for i in range(2)] if LAST else None
                z = [sb(cpre + f"z{i}", [P, TS, D], fp32, c) for i in range(2)]
                z2 = [sb(cpre + f"z2_{i}", [P, TS, D], fp32, c) for i in range(2)] if LAST else None
                res = [sb(cpre + f"res{i}", [P, TS, D], fp32, c) for i in range(2)] if LAST else None
                den = sb(cpre + "den", [P, TS, HH], fp32, c)
                xT = sb(cpre + "xT", [P, TS * P], fp32, c)
                tout = [sb(cpre + f"tout{i}", [P, TS, TW], fp32, c) for i in range(2)]
                psT = pb(cpre + "psT", [P, TS * P], c)
                psG = [pb(cpre + f"psG{i}", [P, 2, 512], c) for i in range(2)]
                psC = pb(cpre + "psC", [P, W], c)
                loaded = names(cpre, c, "own_loaded0", "own_loaded1")
                x3_loaded = names(cpre, c, "x3_loaded0", "x3_loaded1")
                stored = names(cpre, c, "stored0", "stored1")
                rest_ = names(cpre, c, "edge_weighted", "cap_ready", "sum_ready", "self_ready", "averaged", "transposed", "evacuated", "product_ready",
                              "product_evacuated", "own_copied", "chain", "chain2", "var1", "std1", "norm1", "normalized", "added", "var2", "std2", "norm2",
                              "result_ready", "carry_ready", "cleared", "indices_ready")
                (s_wtd, s_cap, s_sum, s_self, s_avg, s_tr, s_ev, s_out, s_lin, s_own, s_bch, s_ch2, s_var1, s_std1, s_norm1, s_app1, s_added, s_var2, s_std2,
                 s_norm2, s_res, s_carry, s_set, s_idx) = rest_

                with nc.Block() as block:
                    @block.sync
                    def _(sp):
                        def load(s):
                            wait(sp, s_self, free(s, 1))
                            sp.dma_start(own[s.par][:, :, :], slot_rows(table, s.n)).then_inc(loaded[s.par], 16)

                        def load_x3(s):
                            wait(sp, s_added, free(s, 1))
                            sp.dma_start(x3in[s.par][:, :, :], slot_rows(X3, s.n)).then_inc(x3_loaded[s.par], 16)

                        def store(s):
                            sp.wait_ge(s_lin, s.n + 1)
                            sp.dma_start(slot_rows(next_table, s.n), tout[s.par][:, :, :]).then_inc(stored[s.par], 16)

                        if LAST:
                            pipelined(sp, [(load, 2), (load_x3, 1)])
                        else:
                            pipelined(sp, [(load, 2), (store, 0)])
                            for i in range(2):
                                sp.wait_ge(stored[i], 16 * (STEPS // 2))

                    @block.gpsimd
                    def _(pool):
                        last_node = pool.to_reg(N - 1)
                        def weigh(s):
                            if s.last:
                                return
                            tiles = bass.ds(s.n * TS, TS)
                            w = xrow[:, tiles, D:W].unsqueeze(3).to_broadcast([P, TS, HH, CH])
                            x = xrow[:, tiles, 0:D].rearrange("p t (h c) -> p t h c", h=HH)
                            nc.gpsimd.tensor_tensor(x, x, w, ALU.mult).then_inc(s_wtd, 1)

                        def scatter(s):
                            pool.wait_ge(s_res, s.n + 1)
                            row_numbers_free(pool, s)
                            nc.gpsimd.tensor_copy(idxr[:, s.par, 0:TS], outidx[:, bass.ds(s.n * TS, TS)]).then_inc(s_idx, 1)
                            indices(pool, s_idx, s.n + 1)
                            for k in range(TS):
                                pool.indirect_dma_start(out=out, out_offset=bass.IndirectOffsetOnAxis(ap=idxr[:, s.par, k:k + 1], axis=0),
                                                        in_=res[s.par][:, k, :], in_offset=None, bounds_check=last_node, oob_is_err=False).then_inc(ogath[s.par * TS + k], 16)

                        if LAST:
                            pipelined(pool, [(weigh, 2), (scatter, -1)])
                            for k in range(2 * TS):
                                pool.wait_ge(ogath[k], placed[k] + 8 * STEPS)
                        else:
                            pipelined(pool, [(weigh, 2)])

                    @block.tensor
                    def _(pe):
                        t = nc.tensor

                        def carry(s):
                            if s.last:
                                pe.wait_ge(s_sum, EPP)
                                t.matmul(psC[:, :], mleft[:, :], acc[:, (SIDE - 1) % (2 * TS), :], start=True, stop=True).then_inc(s_carry, 1)

                        def product(s):
                            if LAST:
                                return
                            pe.wait_ge(s_avg, s.n + 1)
                            wait(pe, s_ev, s.n)
                            for j in range(TS):
                                m = t.transpose(psT[:, j * P:(j + 1) * P], z[s.par][:, j, :], ident[:, :])
                            m.then_inc(s_tr, 1)
                            pe.wait_ge(s_ev, s.n + 1)
                            wait(pe, s_lin, free(s, 1))
                            for j in range(TS):
                                m = t.matmul(psG[s.par][:, j // 2, j % 2 * TW:(j % 2 + 1) * TW], xT[:, j * P:(j + 1) * P], wgat[:, k_ + 1, :], start=True, stop=True)
                            m.then_inc(s_out, 1)

                        pipelined(pe, [(carry, 1), (product, 0)])

                    @block.scalar
                    def _(act):
                        sc = nc.scalar

                        def product(s):
                            act.wait_ge(s_tr, s.n + 1)
                            wait(act, s_out, s.n)
                            sc.activation(xT[:, :], psT[:, :], ACT.Relu, bias=gatbias[:, k_:k_ + 1]).then_inc(s_ev, 1)
                            act.wait_ge(s_out, s.n + 1)
                            wait(act, stored[s.par], (s.n - s.par) * 8)
                            wait(act, s_own, free(s, 1))
                            sc.copy(tout[s.par][:, :, :].rearrange("p (b j) f -> p b (j f)", b=2), psG[s.par][:, :, 0:2 * TW]).then_inc(s_lin, 1)

                        def first_norm(s):
                            deviate(act, s, 0, 0, s_var1, s_std1, TS)
                            wait(act, s_res, free(s, 1))
                            normalize(act, s, 0, z[s.par], z2[s.par], 0, s_norm1, s_app1, TS)

                        def second_norm(s):
                            deviate(act, s, 1, 0, s_var2, s_std2, TS)
                            for k in range(TS):
                                slot_rows_free(act, s, k)
                            normalize(act, s, 1, z2[s.par], res[s.par], 0, s_norm2, s_res, TS)

                        pipelined(act, [(first_norm, 0), (second_norm, -1)] if LAST else [(product, 0)])

                    @block.vector
                    def _(dve):
                        v = nc.vector
                        v.memset(acc[:, :, :], 0.0).then_inc(s_set, 1)
                        v.memset(cap[:, :], 0.0).then_inc(s_set, 1)
                        dve.wait_ge(s_set, 2)
                        ch, ch2 = Chain(dve, s_bch, 3 + (TS + LN_LINKS + 2 if LAST else 0)), Chain(dve, s_ch2, TS + LN_LINKS + 2)

                        def edges(s):
                            if s.last:
                                side_sums(acc, cap, psC[:, :], s_sum, s_carry, dve)
                                return
                            dve.wait_ge(s_wtd, s.n + 1)
                            for k in range(TS):
                                scan_edge(s, k, xrow[:, bass.ds(s.n * TS + k, 1), 0:W].rearrange("p a w -> p (a w)"), acc, cap, s_sum, s_cap, dve)

                        def average(s):
                            ch.begin(s)
                            par, tiles = s.par, bass.ds(s.n * TS, TS)
                            dve.wait_ge(loaded[par], arrived(s))
                            if not LAST:
                                wait(dve, s_tr, free(s, 1))
                            else:
                                wait(dve, s_app1, free(s, 1))
                            z4 = z[par][:, :, :].rearrange("p t (h c) -> p t h c", h=HH)
                            sums = acc[:, par * TS:(par + 1) * TS, :]
                            v.tensor_tensor(z4, own[par][:, :, 0:D].rearrange("p t (h c) -> p t h c", h=HH),
                                            pself[:, tiles, 0:HH].unsqueeze(3).to_broadcast([P, TS, HH, CH]), ALU.mult).then_inc(s_self, 1)
                            dve.wait_ge(s_self, s.n + 1)
                            ch.mark(v.tensor_tensor(z[par][:, :, :], z[par][:, :, :], sums[:, :, 0:D], ALU.add))
                            ch.link(v.scalar_tensor_tensor(den[:, :, :], sums[:, :, D:W], 1e-16, pself[:, tiles, 0:HH], ALU.add, ALU.add))
                            ch.link(v.reciprocal(den[:, :, :], den[:, :, :]))
                            ins = v.tensor_tensor(z4, z4, den[:, :, :].unsqueeze(3).to_broadcast([P, TS, HH, CH]), ALU.mult)
                            if LAST:
                                ch.link(ins)
                                ch.link(v.tensor_tensor(z[par][:, :, :], z[par][:, :, :], spread(rows["L3_gnn_b2"], TS), ALU.add))
                                normalizing(dve, ch, s, 0, z[par], 0, s_var1, s_std1, s_norm1, TS)
                            else:
                                ins.then_inc(s_avg, 1)

                        def second_norm(s):
                            ch2.begin(s)
                            zs = z2[s.par][:, :, :]
                            dve.wait_ge(s_app1, s.n + 1)
                            ch2.link(v.tensor_tensor(zs, zs, spread(rows["L3_gnn_gamma"], TS), ALU.mult))
                            ch2.link(v.tensor_tensor(zs, zs, spread(rows["L3_gnn_beta"], TS), ALU.add))
                            dve.wait_ge(x3_loaded[s.par], arrived(s))
                            v.tensor_tensor(zs, zs, x3in[s.par][:, :, :], ALU.add).then_inc(s_added, 1)
                            dve.wait_ge(s_added, s.n + 1)
                            normalizing(dve, ch2, s, 1, z2[s.par], 0, s_var2, s_std2, s_norm2, TS)

                        def own_scores(s):
                            dve.wait_ge(s_lin, s.n + 1)
                            v.tensor_copy(ownal[:, bass.ds(s.n * TS, TS), :], tout[s.par][:, :, D:TW]).then_inc(s_own, 1)

                        pipelined(dve, [(average, 0), (edges, 1), (second_norm, -1)] if LAST else [(average, 0), (edges, 1), (own_scores, -1)])
                closing([*loaded, *x3_loaded, *stored, *rest_], c)


PREP_LOADS = 16 * (6 + 2 + 2 + 2 + 4 + 2 + 3 * 3 + 9 + 3 * TS)


_INS = ["x", "src", "dst", "edge_type_8", "edge_weight",
        "L0_gnn_W_self", "L0_gnn_b_self", "L0_gnn_W_rel", "L0_gnn_gamma", "L0_gnn_beta",
        "L1_gnn_W_l0", "L1_gnn_b_l0", "L1_gnn_W_r0", "L1_gnn_gamma0", "L1_gnn_beta0",
        "L1_gnn_W_l1", "L1_gnn_b_l1", "L1_gnn_W_r1", "L1_gnn_gamma1", "L1_gnn_beta1",
        "L3_gnn_W0", "L3_gnn_a_src0", "L3_gnn_a_dst0", "L3_gnn_b0",
        "L3_gnn_W1", "L3_gnn_a_src1", "L3_gnn_a_dst1", "L3_gnn_b1",
        "L3_gnn_W2", "L3_gnn_a_src2", "L3_gnn_a_dst2", "L3_gnn_b2", "L3_gnn_gamma", "L3_gnn_beta"]


def kernel(**inputs):
    import numpy as _np
    import concourse.bacc as _bacc
    from concourse import mybir as _mybir
    from concourse.bass_utils import run_bass_kernel_spmd as _run

    nc = _bacc.Bacc("TRN2", target_bir_lowering=False, num_devices=1)
    arrays, args = {}, {}
    for name in _INS:
        arr = _np.ascontiguousarray(inputs[name])
        arrays[f"in_{name}_dram"] = arr
        args[name] = nc.dram_tensor(f"in_{name}_dram", arr.shape, _mybir.dt.from_np(arr.dtype), kind="ExternalInput").ap()
    out = nc.dram_tensor("out_0_dram", (N, D), _mybir.dt.float32, kind="ExternalOutput").ap()
    gnn_kernel(nc, args, out)
    r = _run(nc, [arrays], core_ids=[0])
    return r.results[0]["out_0_dram"]
```

```python
import concourse.bass as bass
from concourse import mybir
from contextlib import ExitStack

fp32 = mybir.dt.float32
i32 = mybir.dt.int32
ALU = mybir.AluOpType
ACT = mybir.ActivationFunctionType
AX = mybir.AxisListType

P = 128
N, D, E = 50000, 128, 25000
R = 8
EPP = -(-E // P)
TS = 4
TN = 8
U = TS + TN
STEPS = EPP // TS + 1
TP = STEPS * TS
SIDE = EPP
NPAD = STEPS * TN * P
NSLOT = TP * P
PAD_NODE = NPAD - 1
OUT_OF_RANGE = 1 << 20
KH = N // P + 2
PAD_KEY = KH * P - 1
H, C = 4, 32
TW = D + 2 * H
EPS = 1e-5
BIG = 1e30


def wait(eng, sem, value):
    if isinstance(value, int) and value <= 0:
        return
    eng.wait_ge(sem, value)


class Step:

    def __init__(self, n, par):
        self.n, self.par = n, par
        self.last = isinstance(n, int) and n == STEPS - 1


def pipelined(eng, order, steps=STEPS):
    def run(base, par):
        for part, off in order:
            if isinstance(base, int) and not 0 <= base + off < steps:
                continue
            part(Step(base + off, (par + off) % 2))

    for base in range(-2, 4):
        run(base, base % 2)
    with eng.Fori(2, steps // 2 - 2) as i:
        run(i * 2, 0)
        run(i * 2 + 1, 1)
    for base in range(steps - 4, steps + 2):
        run(base, base % 2)


class Chain:

    def __init__(self, eng, sem, per):
        self.eng, self.sem, self.per, self.n, self.base = eng, sem, per, 0, 0

    def begin(self, step=None):
        assert step is None or self.n in (0, self.per), (self.n, self.per)
        self.base = 0 if step is None else step.n * self.per
        if step is not None:
            self.n = 0

    def mark(self, ins):
        ins.then_inc(self.sem, 1)
        self.n += 1
        return self.base + self.n

    def link(self, ins):
        self.eng.wait_ge(self.sem, self.mark(ins))


def gnn_kernel(nc, a, out):
    ctx = ExitStack()
    with ctx:
        def sb(name, shape, dt=fp32, c=ctx):
            return c.enter_context(nc.sbuf_tensor(name, shape, dt))

        def pb(name, shape, c=ctx):
            return c.enter_context(nc.psum_tensor(name, shape, fp32))

        used = []

        def sem(name):
            s = ctx.enter_context(nc.semaphore(name))
            used.append(s)
            return s

        def dram(name, shape, dt=fp32):
            return nc.dram_tensor(name, shape, dt, kind="Internal").ap()

        row_of_node = dram("row_of_node", (NPAD, 1), i32)
        X1 = dram("X1", (NPAD + NSLOT, D))
        H1 = dram("H1", (NPAD + NSLOT, D))
        X2 = dram("X2", (NPAD + NSLOT, D))
        X3 = dram("X3", (NPAD + NSLOT, D))
        E1 = dram("E1", (NSLOT + P, D))
        E2 = dram("E2", (NSLOT + P, D))
        ES = dram("ES", (NPAD, D))
        slot_of_node = dram("slot_of_node", (NPAD, 1), i32)
        records = dram("records", (P * EPP, 4))
        T1 = dram("T1", (NPAD + NSLOT, TW))
        T2 = dram("T2", (NPAD + NSLOT, TW))
        T3 = dram("T3", (NPAD + NSLOT, TW))

        def node_rows(t, n):
            return t[0:NPAD, :].rearrange("(n p j) f -> n p j f", p=P, j=TN)[n]

        def slot_rows(t, n):
            base = t.shape[0] - NSLOT if t.shape[0] > NPAD else 0
            return t[base:base + NSLOT, :].rearrange("(p t) f -> p t f", p=P)[:, bass.ds(n * TS, TS), :]

        ident = sb("ident", [P, P])
        ones = sb("ones", [P, P])
        epsc = sb("epsc", [P, 1])
        wself = sb("wself", [P, D])
        wrel = sb("wrel", [P, R, D])
        wsage = sb("wsage", [P, 4, D])
        gatbias = sb("gatbias", [P, 2])
        wgat = sb("wgat", [P, 3, TW])
        rows = {k: sb("row_" + k, [P, D]) for k in (
            "L0_gnn_gamma", "L0_gnn_beta", "L1_gnn_gamma0", "L1_gnn_beta0", "L1_gnn_gamma1", "L1_gnn_beta1",
            "L3_gnn_b2", "L3_gnn_gamma", "L3_gnn_beta")}
        biases = {k: sb("bias_" + k, [1, TS, D]) for k in ("L0_gnn_b_self", "L1_gnn_b_l0", "L1_gnn_b_l1")}
        same = sb("same", [P, TP])
        lead = sb("lead", [P, TP])
        weight = sb("weight", [P, TP])
        rdeg = sb("rdeg", [P, TP])
        coef = sb("coef", [P, TP, R])
        mleft = sb("mleft", [P, P])
        mright = sb("mright", [P, P])
        mside = sb("mside", [P, P])
        mainend = sb("mainend", [P, TP])
        sidend = sb("sidend", [P, TP])
        trail = sb("trail", [P, TP])
        sameb = sb("sameb", [P, TP])
        leadb = sb("leadb", [P, TP])
        weightb = sb("weightb", [P, TP])
        mleftb = sb("mleftb", [P, P])
        dstb = sb("dstb", [P, TP], i32)
        outb = sb("outb", [P, TP], i32)
        endb = sb("endb", [P, TP], i32)
        endslot = sb("endslot", [P, TP], i32)
        gidxb = sb("gidxb", [P, TP], i32)
        mring = sb("mring", [P, 2, 3, TS], i32)
        rec = sb("rec", [P, EPP, 4])
        placei = sb("placei", [P, EPP], i32)
        goes = sb("goes", [P, EPP])
        linkl = sb("linkl", [P, P])
        linkr = sb("linkr", [P, P])
        sideact = sb("sideact", [P, 1])
        srcidx = sb("srcidx", [P, TP], i32)
        ownidx = sb("ownidx", [P, TP], i32)
        endidx = sb("endidx", [P, TP], i32)
        endrow = sb("endrow", [P, TP], i32)
        outidx = sb("outidx", [P, TP], i32)
        gidx = sb("gidx", [P, TP], i32)

        with ExitStack() as c:
            s_set, s_ld, s_ch, s_wt, s_wc, s_bc, s_cl, s_cnt, s_cross, s_iota, s_map, s_zero, s_am = (
                sem("prep_" + k) for k in ("set", "loaded", "chain", "weights_transposed", "weights_copied",
                                           "rows_spread", "masks", "scans", "crossed", "iota", "map", "zero_rows", "score_vectors"))
            dsti = sb("dsti", [P, TP], i32, c)
            typi = sb("typi", [P, EPP], i32, c)
            previ = sb("previ", [P, 1], i32, c)
            nexti = sb("nexti", [P, 1], i32, c)
            d = sb("d", [P, EPP], fp32, c)
            prev = sb("prev", [P, EPP], fp32, c)
            nxt = sb("nxt", [P, EPP], fp32, c)
            typ = sb("typ", [P, EPP], fp32, c)
            eq = sb("eq", [P, R, EPP], fp32, c)
            fw = sb("fw", [P, R, EPP], fp32, c)
            bw = sb("bw", [P, R, EPP], fp32, c)
            cont = sb("cont", [P, 1], fp32, c)
            endm = sb("endm", [P, EPP], fp32, c)
            t0 = sb("t0", [P, TP], fp32, c)
            t1 = sb("t1", [P, TP], fp32, c)
            t2 = sb("t2", [P, TP], fp32, c)
            slotrow = sb("slotrow", [P, TP], fp32, c)
            siderow = sb("siderow", [P, 1], fp32, c)
            dg = sb("dg", [P, 2, P], fp32, c)
            crossed = sb("crossed", [P, 2, R], fp32, c)
            less = sb("less", [P, P], fp32, c)
            more = sb("more", [P, P], fp32, c)
            nodeid = sb("nodeid", [P, NPAD // P], i32, c)
            wnat = sb("wnat", [P, R + 8, D], fp32, c)
            wgt = sb("wgt", [P, 3, D], fp32, c)
            heads = sb("heads", [P, H], fp32, c)
            avec = sb("avec", [P, 6], fp32, c)
            amat = sb("amat", [P, 3, 2 * H], fp32, c)
            psw = [pb(f"psw{i}", [P, 512], c) for i in range(4)]
            psa = pb("psa", [P, 3, 2 * H], c)
            psr = pb("psr", [P, 2, P], c)
            psx = pb("psx", [P, 2, R], c)
            LASTN = E - (P - 1) * EPP

            with nc.Block() as block:
                @block.sync
                def _(sp):
                    sp.wait_ge(s_set, 6)
                    n = 0
                    def ld(dst, src, **kw):
                        nonlocal n
                        sp.dma_start(dst, src, **kw).then_inc(s_ld, 16)
                        n += 1
                    for buf, name in ((dsti, "dst"), (srcidx, "src"), (typi, "edge_type_8")):
                        ld(buf[0:P - 1, 0:EPP], a[name][0:(P - 1) * EPP].rearrange("(p t) -> p t", t=EPP))
                        ld(buf[P - 1:P, 0:LASTN], a[name][(P - 1) * EPP:E].rearrange("(p t) -> p t", p=1))
                    ld(weight[0:P - 1, 0:EPP], a["edge_weight"][0:(P - 1) * EPP].rearrange("(p t) -> p t", t=EPP))
                    ld(weight[P - 1:P, 0:LASTN], a["edge_weight"][(P - 1) * EPP:E].rearrange("(p t) -> p t", p=1))
                    ld(previ[1:P, :], a["dst"][EPP - 1:E].rearrange("(p t) -> p t", p=1)[:, 0:1 + EPP * (P - 2):EPP].rearrange("p t -> t p"), allow_slow_non_contiguous=True)
                    ld(nexti[0:P - 1, :], a["dst"][EPP:E].rearrange("(p t) -> p t", p=1)[:, 0:1 + EPP * (P - 2):EPP].rearrange("p t -> t p"), allow_slow_non_contiguous=True)
                    ld(wnat[:, 0, :], a["L0_gnn_W_self"])
                    ld(wnat[:, 1:R + 1, :], a["L0_gnn_W_rel"].rearrange("r o f -> o r f"))
                    for k, name in enumerate(("W_l0", "W_r0", "W_l1", "W_r1")):
                        ld(wnat[:, R + 1 + k, :], a["L1_gnn_" + name])
                    for k in range(2):
                        ld(gatbias[:, k:k + 1], a[f"L3_gnn_b{k}"].unsqueeze(1), allow_slow_non_contiguous=True)
                    for k in range(3):
                        ld(wnat[:, R + 5 + k, :], a[f"L3_gnn_W{k}"])
                        for l, name in enumerate(("a_src", "a_dst")):
                            ld(avec[:, 2 * k + l:2 * k + l + 1], a[f"L3_gnn_{name}{k}"].rearrange("h c -> (h c)").unsqueeze(1), allow_slow_non_contiguous=True)
                    for k, t in rows.items():
                        ld(t[:, :], a[k].partition_broadcast(P))
                    for k, t in biases.items():
                        for j in range(TS):
                            ld(t[0:1, j, :], a[k].rearrange("(a f) -> a f", a=1))
                    assert 16 * n == PREP_LOADS
                    sp.wait_ge(s_iota, 1)
                    sp.dma_start(row_of_node.rearrange("(p t) o -> p (t o)", p=P), nodeid[:, :]).then_inc(s_map, 16)


                @block.gpsimd
                def _(pool):
                    nc.gpsimd.iota(nodeid[:, :], [[1, NPAD // P]], base=0, channel_multiplier=NPAD // P).then_inc(s_iota, 1)
                    nc.gpsimd.iota(slotrow[:, :], [[1, TP]], base=NPAD, channel_multiplier=TP, allow_small_or_imprecise_dtypes=True).then_inc(s_iota, 1)
                    nc.gpsimd.iota(siderow[:, :], [[1, 1]], base=NPAD + SIDE, channel_multiplier=TP, allow_small_or_imprecise_dtypes=True).then_inc(s_iota, 1)
                    pool.wait_ge(s_cl, 3)
                    nc.gpsimd.affine_select(out=ident[:, :], in_=ones[:, :], compare_op=ALU.is_equal, fill=0.0, base=0, pattern=[[-1, P]], channel_multiplier=1).then_inc(s_iota, 1)
                    nc.gpsimd.affine_select(out=less[:, :], in_=ones[:, :], compare_op=ALU.is_gt, fill=0.0, base=0, pattern=[[1, P]], channel_multiplier=-1).then_inc(s_iota, 1)
                    nc.gpsimd.affine_select(out=more[:, :], in_=ones[:, :], compare_op=ALU.is_gt, fill=0.0, base=0, pattern=[[-1, P]], channel_multiplier=1).then_inc(s_iota, 1)

                    nc.gpsimd.affine_select(out=heads[:, :], in_=ones[:, 0:H], compare_op=ALU.is_ge, fill=0.0, base=0, pattern=[[-C, H]], channel_multiplier=1).then_inc(s_iota, 1)
                    pool.wait_ge(s_iota, 7)
                    nc.gpsimd.affine_select(out=heads[:, :], in_=heads[:, :], compare_op=ALU.is_ge, fill=0.0, base=C - 1, pattern=[[C, H]], channel_multiplier=-1).then_inc(s_iota, 1)

                @block.tensor
                def _(pe):
                    pe.wait_ge(s_iota, 4)
                    pe.wait_ge(s_ld, PREP_LOADS)
                    for k in range(R + 8):
                        m = nc.tensor.transpose(psw[k // 4][:, (k % 4) * P:(k % 4 + 1) * P], wnat[:, k, :], ident[:, :])
                    m.then_inc(s_wt, 1)
                    pe.wait_ge(s_am, 1)
                    pe.wait_ge(s_wc, R + 8)
                    for k in range(3):
                        m = nc.tensor.matmul(psa[:, k, :], wgt[:, k, :], amat[:, k, :], start=True, stop=True)
                    m.then_inc(s_wt, 1)
                    pe.wait_ge(s_bc, 1)
                    for k in range(2):
                        m = nc.tensor.matmul(psr[:, k, :], ones[:, :], dg[:, k, :], start=True, stop=True)
                    m.then_inc(s_wt, 1)
                    pe.wait_ge(s_cnt, 1)
                    nc.tensor.matmul(psx[:, 0, :], mleft[:, :], fw[:, :, EPP - 1], start=True, stop=True)
                    nc.tensor.matmul(psx[:, 1, :], mright[:, :], bw[:, :, 0], start=True, stop=True).then_inc(s_cross, 1)

                @block.scalar
                def _(act):
                    act.wait_ge(s_wt, 1)
                    nc.scalar.copy(wself[:, :], psw[0][:, 0:P]).then_inc(s_wc, 1)
                    for k in range(1, R + 1):
                        nc.scalar.copy(wrel[:, k - 1, :], psw[k // 4][:, (k % 4) * P:(k % 4 + 1) * P]).then_inc(s_wc, 1)
                    for k in range(R + 1, R + 8):
                        dst = wsage[:, k - R - 1, :] if k < R + 5 else wgt[:, k - R - 5, :]
                        nc.scalar.copy(dst, psw[k // 4][:, (k % 4) * P:(k % 4 + 1) * P]).then_inc(s_wc, 1)
                    act.wait_ge(s_wt, 2)
                    nc.scalar.copy(wgat[:, :, D:TW], psa[:, :, :]).then_inc(s_wc, 1)
                    nc.scalar.copy(wgat[:, :, 0:D], wnat[:, R + 5:R + 8, :]).then_inc(s_wc, 1)

                @block.vector
                def _(dve):
                    ch = Chain(dve, s_ch, 0)
                    v = nc.vector
                    v.memset(dsti[:, :], PAD_NODE).then_inc(s_set, 1)
                    v.memset(srcidx[:, :], 0).then_inc(s_set, 1)
                    v.memset(typi[:, :], 0).then_inc(s_set, 1)
                    v.memset(weight[:, :], 0.0).then_inc(s_set, 1)
                    v.memset(previ[:, :], -1).then_inc(s_set, 1)
                    v.memset(nexti[:, :], -1).then_inc(s_set, 1)
                    v.memset(ones[:, :], 1.0).then_inc(s_cl, 1)
                    v.memset(epsc[:, :], EPS).then_inc(s_cl, 1)
                    v.memset(coef[:, :, :], 0.0).then_inc(s_cl, 1)
                    for t in (same, lead, rdeg, mainend, sidend, trail):
                        ch.link(v.memset(t[:, :], 0.0))
                    dve.wait_ge(s_ld, PREP_LOADS)
                    dve.wait_ge(s_cl, 3)
                    dve.wait_ge(s_iota, 8)
                    ch.link(v.memset(amat[:, :, :], 0.0))
                    for k in range(2):
                        for l in range(2):
                            ch.link(v.tensor_scalar(amat[:, k, l * H:(l + 1) * H], heads[:, :], avec[:, 2 * k + l:2 * k + l + 1], None, ALU.mult))
                    for l in range(2):
                        ch.link(v.tensor_copy(amat[:, 2, l * H:l * H + 1], avec[:, 4 + l:5 + l]))
                    dve.sem_inc(s_am, 1)
                    ch.link(v.tensor_copy(d[:, :], dsti[:, 0:EPP]))
                    ch.link(v.tensor_copy(typ[:, :], typi[:, :]))
                    ch.link(v.tensor_copy(prev[:, 1:EPP], dsti[:, 0:EPP - 1]))
                    ch.link(v.tensor_copy(prev[:, 0:1], previ[:, :]))
                    ch.link(v.tensor_copy(nxt[:, 0:EPP - 1], dsti[:, 1:EPP]))
                    ch.link(v.tensor_copy(nxt[:, EPP - 1:EPP], nexti[:, :]))
                    ch.mark(v.tensor_scalar(dg[:, 0, :], ident[:, :], d[:, 0:1], None, ALU.mult))
                    ch.link(v.tensor_scalar(dg[:, 1, :], ident[:, :], d[:, EPP - 1:EPP], None, ALU.mult))
                    dve.sem_inc(s_bc, 1)
                    ch.mark(v.tensor_tensor(same[:, 1:EPP], d[:, 1:EPP], prev[:, 1:EPP], ALU.is_equal))
                    ch.mark(v.tensor_tensor(cont[:, :], d[:, 0:1], prev[:, 0:1], ALU.is_equal))
                    ch.mark(v.tensor_tensor(endm[:, :], d[:, :], nxt[:, :], ALU.not_equal))
                    ch.mark(v.tensor_scalar(lead[:, 0:EPP], d[:, :], d[:, 0:1], None, ALU.is_equal))
                    ch.link(v.tensor_scalar(trail[:, 0:EPP], d[:, :], d[:, EPP - 1:EPP], None, ALU.is_equal))
                    ch.link(v.scalar_tensor_tensor(sidend[:, 0:EPP], endm[:, :], cont[:, 0:1], lead[:, 0:EPP], ALU.mult, ALU.mult))
                    ch.mark(v.tensor_tensor(mainend[:, 0:EPP], endm[:, :], sidend[:, 0:EPP], ALU.subtract))
                    ch.link(v.reduce_max(sideact[:, :], sidend[:, 0:EPP], AX.X))
                    ch.link(v.tensor_scalar(t0[:, :], slotrow[:, :], siderow[:, 0:1], -1.0, ALU.subtract, ALU.mult))
                    ch.link(v.tensor_tensor(t0[:, :], t0[:, :], sidend[:, :], ALU.mult))
                    ch.link(v.tensor_tensor(t0[:, :], t0[:, :], slotrow[:, :], ALU.add))
                    ch.link(v.tensor_copy(endrow[:, :], t0[:, :]))
                    ch.link(v.tensor_scalar(t1[:, 0:EPP], d[:, :], float(OUT_OF_RANGE), None, ALU.subtract))
                    ch.link(v.memset(t2[:, :], float(OUT_OF_RANGE)))
                    ch.link(v.tensor_tensor(t0[:, 0:EPP], t1[:, 0:EPP], endm[:, :], ALU.mult))
                    ch.link(v.tensor_tensor(t2[:, 0:EPP], t2[:, 0:EPP], t0[:, 0:EPP], ALU.add))
                    ch.link(v.tensor_copy(endidx[:, :], t2[:, :]))
                    ch.link(v.memset(t2[:, :], float(OUT_OF_RANGE)))
                    ch.link(v.tensor_tensor(t0[:, 0:EPP], t1[:, 0:EPP], mainend[:, 0:EPP], ALU.mult))
                    ch.link(v.tensor_tensor(t2[:, 0:EPP], t2[:, 0:EPP], t0[:, 0:EPP], ALU.add))
                    ch.link(v.tensor_tensor(t0[:, 0:1], t1[:, 0:1], sideact[:, :], ALU.mult))
                    ch.link(v.tensor_tensor(t2[:, SIDE:SIDE + 1], t2[:, SIDE:SIDE + 1], t0[:, 0:1], ALU.add))
                    ch.link(v.tensor_copy(outidx[:, :], t2[:, :]))
                    ch.link(v.memset(t0[:, :], 0.0))
                    ch.link(v.tensor_scalar(t0[:, 0:EPP], d[:, :], float(N - 1), None, ALU.min))
                    ch.link(v.tensor_scalar(t0[:, SIDE:SIDE + 1], d[:, 0:1], float(N - 1), None, ALU.min))
                    ch.link(v.tensor_copy(ownidx[:, :], t0[:, :]))
                    dve.wait_ge(s_wt, 3)
                    ch.link(v.scalar_tensor_tensor(mleft[:, :], psr[:, 0, :], d[:, EPP - 1:EPP], less[:, :], ALU.is_equal, ALU.mult))
                    ch.link(v.scalar_tensor_tensor(mright[:, :], psr[:, 1, :], d[:, 0:1], more[:, :], ALU.is_equal, ALU.mult))
                    ch.link(v.tensor_scalar(mside[:, :], mright[:, :], sideact[:, 0:1], None, ALU.mult))
                    for link, m in ((linkl, mright), (linkr, mleft)):
                        ch.link(v.tensor_scalar(link[:, :], (psr[:, 1, :] if link is linkl else psr[:, 0, :]), d[:, 0:1] if link is linkl else d[:, EPP - 1:EPP], None, ALU.is_equal))
                        ch.link(v.tensor_tensor(link[:, :], link[:, :], (more if link is linkl else less)[:, :], ALU.mult))
                        ch.link(v.tensor_scalar(link[:, :], link[:, :], 1.0, BIG, ALU.subtract, ALU.mult))
                    for r in range(R):
                        ch.link(v.tensor_scalar(eq[:, r, :], typ[:, :], float(r), None, ALU.is_equal))
                    for r in range(R):
                        ch.mark(v.tensor_tensor_scan(fw[:, r, :], same[:, 0:EPP], eq[:, r, :], 0.0, ALU.mult, ALU.add))
                    ch.link(v.tensor_tensor(goes[:, :], d[:, :], nxt[:, :], ALU.is_equal))
                    for r in range(R):
                        ch.link(v.tensor_tensor_scan(bw[:, r, ::-1], goes[:, ::-1], eq[:, r, ::-1], 0.0, ALU.mult, ALU.add))
                    dve.sem_inc(s_cnt, 1)
                    dve.wait_ge(s_cross, 1)
                    ch.link(v.tensor_copy(crossed[:, :, :], psx[:, :, :]))
                    for r in range(R):
                        ch.mark(v.scalar_tensor_tensor(fw[:, r, :], lead[:, 0:EPP], crossed[:, 0, r:r + 1], fw[:, r, :], ALU.mult, ALU.add))
                        ch.link(v.scalar_tensor_tensor(bw[:, r, :], trail[:, 0:EPP], crossed[:, 1, r:r + 1], bw[:, r, :], ALU.mult, ALU.add))
                    ch.link(v.tensor_tensor(fw[:, :, :], fw[:, :, :], bw[:, :, :], ALU.add))
                    ch.link(v.tensor_tensor(fw[:, :, :], fw[:, :, :], eq[:, :, :], ALU.subtract))
                    ch.link(v.reduce_sum(t0[:, 0:EPP], fw[:, :, :].rearrange("p r t -> p t r"), AX.X))
                    ch.link(v.reciprocal(rdeg[:, 0:EPP], t0[:, 0:EPP]))
                    ch.link(v.tensor_tensor(fw[:, :, :], fw[:, :, :], eq[:, :, :], ALU.mult))
                    ch.link(v.reduce_sum(t0[:, 0:EPP], fw[:, :, :].rearrange("p r t -> p t r"), AX.X))
                    ch.link(v.reciprocal(t1[:, 0:EPP], t0[:, 0:EPP]))
                    for r in range(R):
                        ch.link(v.tensor_tensor(coef[:, 0:EPP, r], eq[:, r, :], t1[:, 0:EPP], ALU.mult))
                    dve.wait_ge(s_wc, R + 10)
                    dve.wait_ge(s_map, 16)
        nc.all_engine_barrier()

        idxr = sb("idxr", [P, 2, 2 * TS], i32)
        ownal = sb("ownal", [P, TP, 2 * H])
        st = sb("st", [P, U, 6])
        lnt = sb("lnt", [P, 4, U])
        var = sb("var", [P, 2, U])
        sd = sb("sd", [P, 2, U])
        rstd = sb("rstd", [P, 2, U])
        nmr = sb("nmr", [P, 2, U])

        def spread(row, tiles):
            return row[:, :].unsqueeze(1).to_broadcast([P, tiles, D])

        def scan_edge(s, k, src, acc, cap, s_sum, s_cap, dve, same=same, lead=lead):
            t, slot = s.n * TS + k, s.par * TS + k
            nc.vector.scalar_tensor_tensor(acc[:, slot, :], acc[:, (slot - 1) % (2 * TS), :], same[:, bass.ds(t, 1)],
                                           src, ALU.mult, ALU.add).then_inc(s_sum, 1)
            nc.vector.scalar_tensor_tensor(cap[:, :], src, lead[:, bass.ds(t, 1)], cap[:, :], ALU.mult, ALU.add).then_inc(s_cap, 1)
            dve.wait_ge(s_sum, t + 1)
            dve.wait_ge(s_cap, t + 1)

        def side_sums(acc, cap, psC, s_sum, s_carry, dve):
            dve.wait_ge(s_carry, 1)
            nc.vector.tensor_tensor(acc[:, SIDE % (2 * TS), :], psC, cap[:, :], ALU.add).then_inc(s_sum, 1)
            nc.vector.memset(acc[:, SIDE % (2 * TS) + 1:SIDE % (2 * TS) + TS, :], 0.0).then_inc(s_sum, TS - 1)

        def normalizing(dve, ch, s, k, src, t0, s_var, s_std, s_norm, t1=U, factor=1.0, first=0):
            v = nc.vector
            for j in range(t0, t1):
                at = ch.mark(v.bn_stats(st[:, j, :], src[:, j - first, :]))
            dve.wait_ge(ch.sem, at)
            tt = slice(t0, t1)
            ch.mark(v.tensor_tensor(lnt[:, 0, tt], st[:, tt, 1], st[:, tt, 4], ALU.subtract))
            ch.mark(v.tensor_tensor(lnt[:, 1, tt], st[:, tt, 2], st[:, tt, 5], ALU.add))
            ch.link(v.tensor_tensor(lnt[:, 2, tt], st[:, tt, 1], st[:, tt, 4], ALU.add))
            ch.link(v.scalar_tensor_tensor(lnt[:, 3, tt], lnt[:, 0, tt], 0.25, lnt[:, 0, tt], ALU.mult, ALU.mult))
            v.scalar_tensor_tensor(var[:, k, tt], lnt[:, 1, tt], 1.0 / D, lnt[:, 3, tt], ALU.mult, ALU.add).then_inc(s_var, 1)
            dve.wait_ge(s_std, s.n + 1)
            ch.link(v.reciprocal(rstd[:, k, tt], sd[:, k, tt]))
            if factor != 1.0:
                ch.link(v.tensor_scalar(rstd[:, k, tt], rstd[:, k, tt], factor, None, ALU.mult))
            v.scalar_tensor_tensor(nmr[:, k, tt], lnt[:, 2, tt], -0.5, rstd[:, k, tt], ALU.mult, ALU.mult).then_inc(s_norm, 1)

        LN_LINKS = 5

        def deviate(act, s, k, t0, s_var, s_std, t1=U, factor=1.0):
            act.wait_ge(s_var, s.n + 1)
            nc.scalar.activation(sd[:, k, t0:t1], var[:, k, t0:t1], ACT.Sqrt, bias=epsc[:, 0:1], scale=factor * factor).then_inc(s_std, 1)

        def normalize(act, s, k, src, dst, t0, s_norm, s_done, t1=U):
            act.wait_ge(s_norm, s.n + 1)
            for j in range(t0, t1):
                m = nc.scalar.activation(dst[:, j, :], src[:, j, :], ACT.Identity, bias=nmr[:, k, j:j + 1], scale=rstd[:, k, j:j + 1])
            m.then_inc(s_done, 1)

        s_go = ctx.enter_context(nc.semaphore("row_numbers_seen"))

        def indices(pool, sem, count):
            pool.wait_ge(sem, count)
            pool.sem_inc(s_go, 1)

        def gather(pool, dst, table, index, done, last):
            pool.indirect_dma_start(out=dst, out_offset=None, in_=table, in_offset=bass.IndirectOffsetOnAxis(ap=index, axis=0),
                                    bounds_check=last, oob_is_err=False).then_inc(done, 16)

        def scatter_rows(pool, table, rows_, index, done, last):
            pool.indirect_dma_start(out=table, out_offset=bass.IndirectOffsetOnAxis(ap=index, axis=0), in_=rows_, in_offset=None,
                                    bounds_check=last, oob_is_err=False).then_inc(done, 16)

        def arrived(s):
            return (s.n - s.par) * 8 + 16

        def free(s, each):
            return (s.n - 1) * each

        def closing(sems):
            nc.all_engine_barrier()
            for x in sems:
                nc.sync.sem_clear(x)
            nc.all_engine_barrier()

        def names(prefix, c, *keys):
            return [c.enter_context(nc.semaphore(prefix + k)) for k in keys]

        closing(used)
        gathered = names("", ctx, *[f"gathered{k}" for k in range(2 * TS)])
        own_moves = names("", ctx, *[f"own_gathered{k}" for k in range(2 * TS)])
        map_moved = names("", ctx, "map_moved0", "map_moved1")
        placed = [0] * (2 * TS)
        before = [0] * (2 * TS)

        def edge_rows(eng, s, k):
            eng.wait_ge(gathered[s.par * TS + k], before[s.par * TS + k] + arrived(s))

        def slots_moved():
            for k in range(2 * TS):
                placed[k] += 8 * STEPS

        def slot_rows_moved(eng, s, k):
            eng.wait_ge(own_moves[s.par * TS + k], placed[s.par * TS + k] + arrived(s))

        def slot_rows_free(eng, s, k):
            if not (isinstance(s.n, int) and s.n < 2 and placed[s.par * TS + k] == 0):
                eng.wait_ge(own_moves[s.par * TS + k], placed[s.par * TS + k] + (s.n - s.par) * 8)

        def row_numbers_free(pool, s):
            if not (isinstance(s.n, int) and s.n < 2):
                for k in range(TS):
                    slot_rows_free(pool, s, k)

        def edges_gathered():
            for t in range(EPP):
                before[t % (2 * TS)] += 16

        MAP_MOVES = 2 * 8 * TS * STEPS


        with ExitStack() as c:
            s_ld, s_iota, s_ch, s_hot, s_hist, s_base, s_row, s_tr, s_tc, s_look, s_run, s_cp, s_pos, s_rec, s_set, s_zero, s_mcp = names(
                "sort_", c, "loaded", "iota", "chain", "one_hot", "counted", "bases", "keys_spread", "transposed", "transpose_copied",
                "looked_up", "run_on", "run_copied", "position", "records", "cleared", "zeroed", "map_copied")
            keyi = sb("keyi", [P, EPP], i32, c)
            loi = sb("loi", [P, EPP], i32, c)
            key = sb("key", [P, EPP], fp32, c)
            lo = sb("lo", [P, EPP], fp32, c)
            hi = sb("hi", [P, EPP], fp32, c)
            columns = sb("columns", [P, KH], fp32, c)
            olo = sb("olo", [P, 2, P], fp32, c)
            ohi = sb("ohi", [P, 2, KH], fp32, c)
            oloT = sb("oloT", [P, 2, P], fp32, c)
            diag = sb("diag", [P, 2, P], fp32, c)
            count = sb("count", [P, KH], fp32, c)
            base = sb("base", [P, KH], fp32, c)
            run = sb("run", [P, 2, KH], fp32, c)
            picked = sb("picked", [P, KH], fp32, c)
            twin = sb("twin", [P, P], fp32, c)
            part = sb("part", [P, 2], fp32, c)
            place = sb("place", [P, EPP], fp32, c)
            desti = sb("desti", [P, EPP], i32, c)
            less = sb("less_s", [P, P], fp32, c)
            more = sb("more_s", [P, P], fp32, c)
            noslot = sb("noslot", [P, NPAD // P], i32, c)
            zeros = sb("zeros", [P, TN, D], fp32, c)
            psH = pb("psH", [P, 512], c)
            psL = [pb(f"psL{i}", [P, 512], c) for i in range(2)]
            psR = [pb(f"psR{i}", [P, 512], c) for i in range(2)]
            psH2 = [psH, pb("psH2", [P, 512], c)]
            psQ = [pb(f"psQ{i}", [P, 512], c) for i in range(2)]

            def tiles(eng, part_):
                for t in range(2):
                    part_(t, t)
                with eng.Fori(1, EPP // 2 - 1) as i:
                    part_(i * 2, 0)
                    part_(i * 2 + 1, 1)
                for t in range(EPP - 2, EPP):
                    part_(t, t % 2)

            with nc.Block() as block:
                @block.sync
                def _(sp):
                    sp.wait_ge(s_set, 2)
                    for buf, name in ((keyi, "src"), (desti, "dst")):
                        sp.dma_start(buf[0:P - 1, :], a[name][0:(P - 1) * EPP].rearrange("(p t) -> p t", t=EPP)).then_inc(s_ld, 16)
                        sp.dma_start(buf[P - 1:P, 0:E - (P - 1) * EPP], a[name][(P - 1) * EPP:E].rearrange("(p t) -> p t", p=1)).then_inc(s_ld, 16)
                    sp.wait_ge(s_set, 3)
                    with sp.Fori(0, STEPS) as i:
                        sp.dma_start(node_rows(ES, i), zeros[:, :, :]).then_inc(s_zero, 16)
                    for t in (E1, E2):
                        sp.dma_start(t[NSLOT:NSLOT + P, :], zeros[:, 0, :]).then_inc(s_zero, 16)
                    sp.wait_ge(s_set, 4)
                    sp.dma_start(slot_of_node.rearrange("(p t) o -> p (t o)", p=P), noslot[:, :]).then_inc(s_zero, 16)
                    sp.wait_ge(s_zero, 16 * (STEPS + 3))

                @block.gpsimd
                def _(pool):
                    last_target = pool.to_reg(NPAD - 1)
                    nc.gpsimd.iota(columns[:, :], [[1, KH]], base=0, channel_multiplier=0, allow_small_or_imprecise_dtypes=True).then_inc(s_iota, 1)
                    nc.gpsimd.affine_select(out=less[:, :], in_=ones[:, :], compare_op=ALU.is_gt, fill=0.0, base=0, pattern=[[1, P]], channel_multiplier=-1).then_inc(s_iota, 1)
                    nc.gpsimd.affine_select(out=more[:, :], in_=ones[:, :], compare_op=ALU.is_gt, fill=0.0, base=0, pattern=[[-1, P]], channel_multiplier=1).then_inc(s_iota, 1)
                    def enter(s):
                        wait(pool, map_moved[s.par], (s.n - s.par) * 8 * TS)
                        nc.gpsimd.tensor_copy(mring[:, s.par, 0, :], endidx[:, bass.ds(s.n * TS, TS)]).then_inc(s_mcp, 1)
                        nc.gpsimd.tensor_copy(mring[:, s.par, 1, :], endrow[:, bass.ds(s.n * TS, TS)]).then_inc(s_mcp, 1)
                        indices(pool, s_mcp, s.n * 2 + 2)
                        for k in range(TS):
                            pool.indirect_dma_start(out=row_of_node, out_offset=bass.IndirectOffsetOnAxis(ap=mring[:, s.par, 0, k:k + 1], axis=0),
                                                    in_=mring[:, s.par, 1, k:k + 1], in_offset=None, bounds_check=last_target, oob_is_err=False).then_inc(map_moved[s.par], 16)

                    def each(part, first, steps):
                        for n in (0, 1):
                            part(Step(first + n, n))
                        with pool.Fori(1, steps // 2) as i:
                            for n in (0, 1):
                                part(Step(i * 2 + first + n, n))

                    each(enter, 0, STEPS)
                    for i in range(2):
                        pool.wait_ge(map_moved[i], 16 * TS * (STEPS // 2))

                    def look_up(s):
                        pool.wait_ge(map_moved[s.par], (s.n - s.par + STEPS) * 8 * TS)
                        if not (isinstance(s.n, int) and s.n < 2):
                            nc.gpsimd.tensor_copy(gidx[:, bass.ds(s.n * TS - 2 * TS, TS)], mring[:, s.par, 2, :]).then_inc(s_mcp, 1)
                        else:
                            nc.gpsimd.tensor_copy(mring[:, s.par, 2, :], mring[:, s.par, 1, :]).then_inc(s_mcp, 1)
                        nc.gpsimd.tensor_copy(mring[:, s.par, 0, :], srcidx[:, bass.ds(s.n * TS, TS)]).then_inc(s_mcp, 1)
                        indices(pool, s_mcp, s.n * 2 + 2 * STEPS + 2)
                        for k in range(TS):
                            gather(pool, mring[:, s.par, 2, k:k + 1], row_of_node, mring[:, s.par, 0, k:k + 1], map_moved[s.par], last_target)

                    each(look_up, 0, STEPS)
                    for i in range(2):
                        pool.wait_ge(map_moved[i], 32 * TS * (STEPS // 2))
                        nc.gpsimd.tensor_copy(gidx[:, (STEPS - 2 + i) * TS:(STEPS - 1 + i) * TS], mring[:, i, 2, :]).then_inc(s_mcp, 1)

                @block.tensor
                def _(pe):
                    t_ = nc.tensor

                    def count_up(t, par):
                        pe.wait_ge(s_hot, t + 1)
                        t_.matmul(psH[:, 0:KH], olo[:, par, :], ohi[:, par, :], start=isinstance(t, int) and t == 0,
                                  stop=isinstance(t, int) and t == EPP - 1).then_inc(s_hist, 1)

                    tiles(pe, count_up)
                    pe.wait_ge(s_base, 1)
                    t_.matmul(psQ[0][:, 0:1], less[:, :], part[:, 0:1], start=True, stop=True).then_inc(s_row, 1)

                    def look(t, par):
                        pe.wait_ge(s_hot, t + EPP + 1)
                        t_.transpose(psR[par][:, 0:P], olo[:, par, :], ident[:, :]).then_inc(s_tr, 1)
                        t_.matmul(psQ[par][:, 0:P], ones[:, :], diag[:, par, :], start=True, stop=True).then_inc(s_row, 1)
                        t_.matmul(psH2[par][:, 0:KH], olo[:, par, :], ohi[:, par, :], start=True, stop=True).then_inc(s_run, 1)
                        pe.wait_ge(s_tc, t + 1)
                        pe.wait_ge(s_cp, t + 1)
                        t_.matmul(psL[par][:, 0:KH], oloT[:, par, :], run[:, par, :], start=True, stop=True).then_inc(s_look, 1)

                    tiles(pe, look)

                @block.scalar
                def _(act):
                    def copies(t, par):
                        act.wait_ge(s_tr, t + 1)
                        if not (isinstance(t, int) and t < 2):
                            act.wait_ge(s_look, t - 1)
                        nc.scalar.copy(oloT[:, par, :], psR[par][:, 0:P]).then_inc(s_tc, 1)

                    tiles(act, copies)

                @block.vector
                def _(dve):
                    v = nc.vector
                    ch = Chain(dve, s_ch, 0)
                    v.memset(keyi[:, :], PAD_KEY).then_inc(s_set, 1)
                    v.memset(desti[:, :], 0).then_inc(s_set, 1)
                    v.memset(zeros[:, :, :], 0.0).then_inc(s_set, 1)
                    v.memset(noslot[:, :], NSLOT).then_inc(s_set, 1)
                    dve.wait_ge(s_ld, 64)
                    dve.wait_ge(s_iota, 3)
                    ch.link(v.tensor_copy(key[:, :], keyi[:, :]))
                    ch.link(v.tensor_scalar(loi[:, :], keyi[:, :], P - 1, None, ALU.bitwise_and))
                    ch.link(v.tensor_copy(lo[:, :], loi[:, :]))
                    ch.link(v.tensor_tensor(hi[:, :], key[:, :], lo[:, :], ALU.subtract))
                    ch.link(v.tensor_scalar(hi[:, :], hi[:, :], 1.0 / P, None, ALU.mult))
                    ch.link(v.memset(rec[:, :, 3], 0.0))
                    ch.link(v.tensor_copy(rec[:, :, 0], keyi[:, :]))
                    ch.link(v.tensor_copy(rec[:, :, 1], desti[:, :]))
                    ch.link(v.tensor_copy(rec[:, :, 2], weight[:, 0:EPP]))

                    def hot(t, par):
                        if isinstance(t, int):
                            wait(dve, s_hist, t - 1)
                        else:
                            dve.wait_ge(s_hist, t - 1)
                        v.tensor_scalar(olo[:, par, :], columns[:, 0:P], lo[:, bass.ds(t, 1)], None, ALU.is_equal)
                        v.tensor_scalar(ohi[:, par, :], columns[:, :], hi[:, bass.ds(t, 1)], None, ALU.is_equal).then_inc(s_hot, 1)

                    tiles(dve, hot)
                    dve.wait_ge(s_hist, EPP)
                    ch.link(v.tensor_copy(count[:, :], psH[:, 0:KH]))
                    ch.link(v.tensor_tensor_scan(base[:, :], ones[:, 0:1].to_broadcast([P, KH]), count[:, :], 0.0, ALU.mult, ALU.add))
                    v.reduce_sum(part[:, 0:1], count[:, :], AX.X).then_inc(s_base, 1)
                    dve.wait_ge(s_row, 1)
                    ch.link(v.tensor_tensor(base[:, :], base[:, :], count[:, :], ALU.subtract))
                    v.tensor_scalar(run[:, 0, :], base[:, :], psQ[0][:, 0:1], None, ALU.add).then_inc(s_cp, 1)

                    def spread_out(t, par):
                        if not (isinstance(t, int) and t < 2):
                            dve.wait_ge(s_look, t - 1)
                        v.tensor_scalar(olo[:, par, :], columns[:, 0:P], lo[:, bass.ds(t, 1)], None, ALU.is_equal)
                        v.tensor_scalar(diag[:, par, :], ident[:, :], key[:, bass.ds(t, 1)], None, ALU.mult)
                        v.tensor_scalar(ohi[:, par, :], columns[:, :], hi[:, bass.ds(t, 1)], None, ALU.is_equal).then_inc(s_hot, 1)

                    def position(t, par):
                        if not (isinstance(t, int) and t == EPP - 1):
                            spread_out(t + 1, 1 - par)
                        dve.wait_ge(s_run, t + 1)
                        dve.wait_ge(s_cp, t + 1)
                        v.tensor_tensor(run[:, 1 - par, :], run[:, par, :], psH2[par][:, 0:KH], ALU.add).then_inc(s_cp, 1)
                        dve.wait_ge(s_row, t + 2)
                        v.scalar_tensor_tensor(twin[:, :], psQ[par][:, 0:P], key[:, bass.ds(t, 1)], more[:, :], ALU.is_equal, ALU.mult).then_inc(s_pos, 1)
                        dve.wait_ge(s_look, t + 1)
                        v.tensor_tensor(picked[:, :], psL[par][:, 0:KH], ohi[:, par, :], ALU.mult).then_inc(s_pos, 1)
                        dve.wait_ge(s_pos, t * 5 + 1)
                        v.reduce_sum(part[:, 0:1], twin[:, :], AX.X).then_inc(s_pos, 1)
                        dve.wait_ge(s_pos, t * 5 + 2)
                        v.reduce_sum(part[:, 1:2], picked[:, :], AX.X).then_inc(s_pos, 1)
                        dve.wait_ge(s_pos, t * 5 + 4)
                        v.tensor_tensor(place[:, bass.ds(t, 1)], part[:, 0:1], part[:, 1:2], ALU.add).then_inc(s_pos, 1)

                    spread_out(0, 0)
                    tiles(dve, position)
                    dve.wait_ge(s_pos, 5 * EPP)
                    v.tensor_copy(placei[:, :], place[:, :]).then_inc(s_rec, 1)
            closing([s_ld, s_iota, s_ch, s_hot, s_hist, s_base, s_row, s_tr, s_tc, s_look, s_run, s_cp, s_pos, s_rec, s_set, s_zero, s_mcp])


        with ExitStack() as c:
            X = sb("X0", [P, 2 * TS, D], fp32, c)
            acc = sb("acc0", [P, 2 * TS, D], fp32, c)
            cap = sb("cap0", [P, D], fp32, c)
            own = [sb(f"own0_{i}", [P, U, D], fp32, c) for i in range(2)]
            y = [sb(f"y0_{i}", [P, U, D], fp32, c) for i in range(2)]
            z = [sb(f"z0_{i}", [P, U, D], fp32, c) for i in range(2)]
            rest = [sb(f"rest0_{i}", [P, U, D], fp32, c) for i in range(2)]
            res = [sb(f"res0_{i}", [P, U, D], fp32, c) for i in range(2)]
            xT = sb("xT0", [P, 3, TS * P], fp32, c)
            eT = sb("eT0", [P, 2, P], fp32, c)
            prod = sb("prod", [P, 2, R, D], fp32, c)
            recring = sb("recring", [P, 2 * TS, 4], fp32, c)
            msg = sb("msg", [P, 2, D], fp32, c)
            psT = [pb(f"psT{i}", [P, TS * P], c) for i in range(2)]
            psO = [pb(f"psO{i}", [P, TS * P], c) for i in range(2)]
            psY = [pb(f"psY{i}", [P, R * D], c) for i in range(2)]
            loaded = names("r0_", c, "own_loaded0", "own_loaded1")
            stored = names("r0_", c, "stored0", "stored1")
            counts = names("r0_", c, "indices_ready", "edge_transposed", "transposed", "edge_evacuated", "evacuated", "relations_done",
                          "relations_weighted", "message_ready", "cap_ready", "sum_ready", "product_ready", "relu_done", "chain1", "chain2", "residual_ready",
                          "var1", "std1", "norm1", "applied1", "added", "var2", "std2", "norm2", "result_ready", "carry_ready", "cleared", "records_copied")
            (s_idx, s_etr, s_tr, s_eev, s_ev, s_rel, s_relmul, s_msg, s_cap, s_sum, s_out, s_y, s_ch1, s_ch2, s_rest, s_var1, s_std1, s_norm1, s_app1,
             s_added, s_var2, s_std2, s_norm2, s_res, s_carry, s_set, s_plc) = counts
            GROUPS = (1, 2, 0)

            def nodes_loaded(eng, s):
                if not s.last:
                    eng.wait_ge(loaded[s.par], arrived(s) + (16 if isinstance(s.n, int) and s.n == STEPS - 2 else 0))

            with nc.Block() as block:
                @block.sync
                def _(sp):
                    def load(s):
                        wait(sp, s_tr, free(s, 3))
                        wait(sp, s_rest, free(s, 1))
                        if isinstance(s.n, int) and (s.n + 1) * TN * P > N:
                            rest = max(0, N - s.n * TN * P) // TN
                            if rest:
                                src = a["x"][s.n * TN * P:N, :].rearrange("(p j) f -> p j f", j=TN)
                                for p0, p1 in ((0, rest // 16 * 16), (rest // 16 * 16, rest)):
                                    sp.dma_start(own[s.par][p0:p1, TS:U, :], src[p0:p1]).then_inc(loaded[s.par], 16)
                            return
                        src = a["x"][bass.ds(s.n * TN * P, TN * P), :].rearrange("(p j) f -> p j f", j=TN)
                        sp.dma_start(own[s.par][:, TS:U, :], src).then_inc(loaded[s.par], 16)

                    def store(s):
                        sp.wait_ge(s_res, s.n + 1)
                        sp.dma_start(node_rows(X1, s.n), res[s.par][:, TS:U, :]).then_inc(stored[s.par], 16)
                        sp.dma_start(slot_rows(X1, s.n), res[s.par][:, 0:TS, :]).then_inc(stored[s.par], 16)

                    pipelined(sp, [(load, 2), (store, -2)])
                    for i in range(2):
                        sp.wait_ge(stored[i], 32 * (STEPS // 2))

                @block.gpsimd
                def _(pool):
                    last_node, last_record = pool.to_reg(N - 1), pool.to_reg(P * EPP - 1)
                    def fetch(s):
                        wait(pool, s_etr, free(s, TS))
                        nc.gpsimd.tensor_copy(idxr[:, s.par, 0:TS], srcidx[:, bass.ds(s.n * TS, TS)]).then_inc(s_idx, 1)
                        indices(pool, s_idx, s.n * 2 + 1)
                        for k in range(TS):
                            if not s.last:
                                gather(pool, X[:, s.par * TS + k, :], a["x"], idxr[:, s.par, k:k + 1], gathered[s.par * TS + k], last_node)
                        wait(pool, s_tr, free(s, 3))
                        nc.gpsimd.tensor_copy(idxr[:, s.par, TS:2 * TS], ownidx[:, bass.ds(s.n * TS, TS)]).then_inc(s_idx, 1)
                        indices(pool, s_idx, s.n * 2 + 2)
                        for k in range(TS):
                            gather(pool, own[s.par][:, k, :], a["x"], idxr[:, s.par, TS + k:TS + k + 1], own_moves[s.par * TS + k], last_node)

                    def residual(s):
                        for k in range(TS):
                            slot_rows_moved(pool, s, k)
                        nodes_loaded(pool, s)
                        wait(pool, s_added, free(s, 1))
                        nc.gpsimd.tensor_tensor(rest[s.par][:, :, :], own[s.par][:, :, :], spread(rows["L0_gnn_beta"], U), ALU.add).then_inc(s_rest, 1)

                    def place_records(s):
                        if s.last:
                            return
                        if not (isinstance(s.n, int) and s.n < 2):
                            pool.wait_ge(map_moved[s.par], MAP_MOVES + (s.n - s.par) * 8 * TS)
                        else:
                            pool.wait_ge(map_moved[s.par], MAP_MOVES)
                        nc.gpsimd.tensor_copy(mring[:, s.par, 0, :], placei[:, bass.ds(s.n * TS, TS)]).then_inc(s_plc, 1)
                        nc.gpsimd.tensor_copy(recring[:, s.par * TS:(s.par + 1) * TS, :], rec[:, bass.ds(s.n * TS, TS), :]).then_inc(s_plc, 1)
                        indices(pool, s_plc, s.n * 2 + 2)
                        for k in range(TS):
                            scatter_rows(pool, records, recring[:, s.par * TS + k, :], mring[:, s.par, 0, k:k + 1], map_moved[s.par], last_record)

                    pipelined(pool, [(residual, 0), (fetch, 2), (place_records, 0)])
                    for i in range(2):
                        pool.wait_ge(map_moved[i], MAP_MOVES + 16 * TS * len(range(i, STEPS - 1, 2)))

                @block.tensor
                def _(pe):
                    t = nc.tensor

                    def relations(s, k):
                        pe.wait_ge(s_eev, s.n * TS + k + 1)
                        wait(pe, s_relmul, s.n * TS + k - 1)
                        for half in range(2):
                            m = t.matmul(psY[k % 2][:, half * 512:(half + 1) * 512], eT[:, k % 2, :],
                                         wrel[:, half * 4:half * 4 + 4, :], start=True, stop=True)
                        m.then_inc(s_rel, 1)

                    def edges(s):
                        if s.last:
                            pe.wait_ge(s_sum, EPP)
                            pe.wait_ge(s_relmul, EPP)
                            t.matmul(psY[0][:, 0:P], mleft[:, :], acc[:, (SIDE - 1) % (2 * TS), :], start=True, stop=True).then_inc(s_carry, 1)
                            return
                        for k in range(TS):
                            edge_rows(pe, s, k)
                            wait(pe, s_eev, s.n * TS + k)
                            t.transpose(psT[0][:, 0:P], X[:, s.par * TS + k, :], ident[:, :]).then_inc(s_etr, 1)
                            relations(s, k)

                    def product(s, q):
                        u = s.n * 3 + q
                        ps = psO[(s.par + q) % 2]
                        pe.wait_ge(s_ev, u + 1)
                        wait(pe, s_y, u - 1)
                        t.matmul(ps[:, :], ones[0:1, :], biases["L0_gnn_b_self"][0:1, :, :], start=True, stop=False)
                        if q == 2:
                            pe.wait_ge(s_sum, s.n * TS + TS)
                        for j in range(TS):
                            if q == 2:
                                t.matmul(ps[:, j * P:(j + 1) * P], ident[:, :], acc[:, s.par * TS + j, :], start=False, stop=False)
                            m = t.matmul(ps[:, j * P:(j + 1) * P], xT[:, q, j * P:(j + 1) * P], wself[:, :], start=False, stop=j == TS - 1)
                        m.then_inc(s_out, 1)

                    def nodes(s):
                        for q, g in enumerate(GROUPS):
                            wait(pe, s_ev, s.n * 3 + q)
                            if g == 0:
                                for k in range(TS):
                                    pe.wait_ge(own_moves[s.par * TS + k], placed[s.par * TS + k] + arrived(s))
                            elif g == 1:
                                nodes_loaded(pe, s)
                            for j in range(TS):
                                m = t.transpose(psT[1][:, j * P:(j + 1) * P], own[s.par][:, g * TS + j, :], ident[:, :])
                            m.then_inc(s_tr, 1)
                            product(s, q)

                    pipelined(pe, [(edges, 1), (nodes, 1)])

                @block.scalar
                def _(act):
                    sc = nc.scalar

                    def nodes(s):
                        for q, g in enumerate(GROUPS):
                            u = s.n * 3 + q
                            act.wait_ge(s_tr, u + 1)
                            wait(act, s_out, u - 2)
                            sc.copy(xT[:, q, :], psT[1][:, :]).then_inc(s_ev, 1)
                            act.wait_ge(s_out, u + 1)
                            if q == 0:
                                wait(act, s_app1, free(s, 1))
                            sc.activation(y[s.par][:, g * TS:(g + 1) * TS, :], psO[(s.par + q) % 2][:, :], ACT.Relu).then_inc(s_y, 1)

                    def first_std(s):
                        deviate(act, s, 0, 0, s_var1, s_std1)

                    def first_norm(s):
                        wait(act, s_res, free(s, 1))
                        normalize(act, s, 0, y[s.par], z[s.par], 0, s_norm1, s_app1)

                    def second_std(s):
                        deviate(act, s, 1, 0, s_var2, s_std2)

                    def second_norm(s):
                        wait(act, stored[s.par], (s.n - s.par) * 16)
                        normalize(act, s, 1, z[s.par], res[s.par], 0, s_norm2, s_res)

                    pipelined(act, [(first_std, 0), (second_norm, -2), (first_norm, 0), (nodes, 1), (second_std, -1)])

                @block.vector
                def _(dve):
                    v = nc.vector
                    v.memset(acc[:, :, :], 0.0).then_inc(s_set, 1)
                    v.memset(cap[:, :], 0.0).then_inc(s_set, 1)
                    dve.wait_ge(s_set, 2)
                    ch1, ch2 = Chain(dve, s_ch1, U + LN_LINKS), Chain(dve, s_ch2, U + LN_LINKS + 1)

                    def copy_edge(s, k):
                        n = s.n * TS + k
                        dve.wait_ge(s_etr, n + 1)
                        wait(dve, s_rel, n - 1)
                        v.tensor_copy(eT[:, k % 2, :], psT[0][:, 0:P]).then_inc(s_eev, 1)

                    def first_edges(s):
                        if not s.last:
                            copy_edge(s, 0)
                            copy_edge(s, 1)

                    def edges(s):
                        wait(dve, s_out, free(s, 3))
                        if s.last:
                            side_sums(acc, cap, psY[0][:, 0:P], s_sum, s_carry, dve)
                            return
                        for k in range(TS):
                            n = s.n * TS + k
                            if 0 < k < TS - 1:
                                copy_edge(s, k + 1)
                            dve.wait_ge(s_rel, n + 1)
                            w = coef[:, bass.ds(n, 1), :].rearrange("p a r -> p (a r)").unsqueeze(2).to_broadcast([P, R, D])
                            v.tensor_tensor(prod[:, k % 2, :, :], psY[k % 2][:, :].rearrange("p (r f) -> p r f", r=R), w, ALU.mult).then_inc(s_relmul, 1)
                            dve.wait_ge(s_relmul, n + 1)
                            v.reduce_sum(msg[:, k % 2, :], prod[:, k % 2, :, :].rearrange("p r f -> p f r"), AX.X).then_inc(s_msg, 1)
                            dve.wait_ge(s_msg, n + 1)
                            scan_edge(s, k, msg[:, k % 2, :], acc, cap, s_sum, s_cap, dve)

                    def first_norm(s):
                        ch1.begin(s)
                        dve.wait_ge(s_y, s.n * 3 + 3)
                        normalizing(dve, ch1, s, 0, y[s.par], 0, s_var1, s_std1, s_norm1)

                    def second_norm(s):
                        ch2.begin(s)
                        zs = z[s.par][:, :, :]
                        dve.wait_ge(s_app1, s.n + 1)
                        ch2.link(v.tensor_tensor(zs, zs, spread(rows["L0_gnn_gamma"], U), ALU.mult))
                        dve.wait_ge(s_rest, s.n + 1)
                        v.tensor_tensor(zs, zs, rest[s.par][:, :, :], ALU.add).then_inc(s_added, 1)
                        dve.wait_ge(s_added, s.n + 1)
                        normalizing(dve, ch2, s, 1, z[s.par], 0, s_var2, s_std2, s_norm2)

                    pipelined(dve, [(first_edges, 1), (first_norm, 0), (edges, 1), (second_norm, -1)])
            edges_gathered()
            slots_moved()
            closing([*loaded, *stored, *counts])

        with ExitStack() as c:
            s_ld, s_set, s_ch, s_iota, s_dg, s_row = names("masks_", c, "loaded", "cleared", "chain", "iota", "diagonal", "row_spread")
            recb = sb("recb", [P, EPP, 4], fp32, c)
            slotno = sb("slotno", [P, TP], fp32, c)
            sideno = sb("sideno", [P, 1], fp32, c)
            before_ = sb("before_", [P, 1], fp32, c)
            after_ = sb("after_", [P, 1], fp32, c)
            prev = sb("prev_b", [P, EPP], fp32, c)
            nxt = sb("nxt_b", [P, EPP], fp32, c)
            endm = sb("endm_b", [P, EPP], fp32, c)
            side = sb("side_b", [P, EPP], fp32, c)
            act_ = sb("sideact_b", [P, 1], fp32, c)
            t0 = sb("t0_b", [P, TP], fp32, c)
            t1 = sb("t1_b", [P, TP], fp32, c)
            cont = sb("cont_b", [P, 1], fp32, c)
            dg = sb("dg_b", [P, P], fp32, c)
            less = sb("less_b", [P, P], fp32, c)
            psr = pb("psr_b", [P, P], c)
            with nc.Block() as block:
                @block.sync
                def _(sp):
                    sp.wait_ge(s_set, 2)
                    sp.dma_start(recb[:, :, :], records.rearrange("(p t) f -> p t f", p=P)).then_inc(s_ld, 16)
                    byrow = records.rearrange("(p t) f -> p t f", p=P)
                    sp.dma_start(before_[1:P, :], byrow[0:P - 1, EPP - 1, 0:1], allow_slow_non_contiguous=True).then_inc(s_ld, 16)
                    sp.dma_start(after_[0:P - 1, :], byrow[1:P, 0, 0:1], allow_slow_non_contiguous=True).then_inc(s_ld, 16)

                @block.gpsimd
                def _(pool):
                    nc.gpsimd.affine_select(out=less[:, :], in_=ones[:, :], compare_op=ALU.is_gt, fill=0.0, base=0, pattern=[[1, P]], channel_multiplier=-1).then_inc(s_iota, 1)
                    nc.gpsimd.iota(slotno[:, :], [[1, TP]], base=0, channel_multiplier=TP, allow_small_or_imprecise_dtypes=True).then_inc(s_iota, 1)
                    nc.gpsimd.iota(sideno[:, :], [[1, 1]], base=SIDE, channel_multiplier=TP, allow_small_or_imprecise_dtypes=True).then_inc(s_iota, 1)

                @block.tensor
                def _(pe):
                    pe.wait_ge(s_dg, 1)
                    nc.tensor.matmul(psr[:, :], ones[:, :], dg[:, :], start=True, stop=True).then_inc(s_row, 1)

                @block.vector
                def _(dve):
                    v = nc.vector
                    ch = Chain(dve, s_ch, 0)
                    A = slice(0, EPP)
                    v.memset(before_[:, :], -1.0).then_inc(s_set, 1)
                    v.memset(after_[:, :], -1.0).then_inc(s_set, 1)
                    for t in (sameb, leadb, weightb, t1):
                        ch.link(v.memset(t[:, :], 0.0))
                    dve.wait_ge(s_ld, 48)
                    dve.wait_ge(s_iota, 3)
                    src_ = recb[:, :, 0]
                    ch.link(v.tensor_copy(prev[:, 1:EPP], recb[:, 0:EPP - 1, 0]))
                    ch.link(v.tensor_copy(prev[:, 0:1], before_[:, :]))
                    ch.link(v.tensor_copy(nxt[:, 0:EPP - 1], recb[:, 1:EPP, 0]))
                    ch.link(v.tensor_copy(nxt[:, EPP - 1:EPP], after_[:, :]))
                    v.tensor_scalar(dg[:, :], ident[:, :], recb[:, 0, 0:1], None, ALU.mult).then_inc(s_dg, 1)
                    ch.link(v.tensor_copy(weightb[:, A], recb[:, :, 2]))
                    ch.link(v.tensor_copy(t1[:, A], recb[:, :, 1]))
                    ch.link(v.tensor_copy(dstb[:, :], t1[:, :]))
                    ch.link(v.tensor_tensor(sameb[:, 1:EPP], recb[:, 1:EPP, 0], prev[:, 1:EPP], ALU.is_equal))
                    ch.link(v.tensor_tensor(cont[:, :], recb[:, 0, 0:1], prev[:, 0:1], ALU.is_equal))
                    ch.link(v.tensor_tensor(endm[:, :], src_, nxt[:, :], ALU.not_equal))
                    ch.link(v.tensor_scalar(leadb[:, A], src_, recb[:, 0, 0:1], None, ALU.is_equal))
                    ch.link(v.scalar_tensor_tensor(side[:, :], endm[:, :], cont[:, 0:1], leadb[:, A], ALU.mult, ALU.mult))
                    ch.link(v.tensor_scalar(t0[:, A], slotno[:, A], sideno[:, 0:1], -1.0, ALU.subtract, ALU.mult))
                    ch.link(v.tensor_tensor(t0[:, A], t0[:, A], side[:, :], ALU.mult))
                    ch.link(v.tensor_tensor(slotno[:, A], t0[:, A], slotno[:, A], ALU.add))
                    ch.link(v.tensor_copy(endslot[:, :], slotno[:, :]))
                    ch.link(v.memset(t0[:, :], float(OUT_OF_RANGE)))
                    ch.link(v.tensor_scalar(t1[:, A], src_, float(OUT_OF_RANGE), None, ALU.subtract))
                    ch.link(v.tensor_tensor(prev[:, :], t1[:, A], endm[:, :], ALU.mult))
                    ch.link(v.tensor_tensor(t0[:, A], t0[:, A], prev[:, :], ALU.add))
                    ch.link(v.tensor_copy(endb[:, :], t0[:, :]))
                    ch.link(v.tensor_tensor(endm[:, :], endm[:, :], side[:, :], ALU.subtract))
                    ch.link(v.reduce_max(act_[:, :], side[:, :], AX.X))
                    ch.link(v.memset(t0[:, :], float(OUT_OF_RANGE)))
                    ch.link(v.tensor_scalar(t1[:, A], src_, float(OUT_OF_RANGE), None, ALU.subtract))
                    ch.link(v.tensor_tensor(prev[:, :], t1[:, A], endm[:, :], ALU.mult))
                    ch.link(v.tensor_tensor(t0[:, A], t0[:, A], prev[:, :], ALU.add))
                    ch.link(v.tensor_tensor(prev[:, 0:1], t1[:, 0:1], act_[:, :], ALU.mult))
                    ch.link(v.tensor_tensor(t0[:, SIDE:SIDE + 1], t0[:, SIDE:SIDE + 1], prev[:, 0:1], ALU.add))
                    ch.link(v.tensor_copy(outb[:, :], t0[:, :]))
                    dve.wait_ge(s_row, 1)
                    ch.link(v.scalar_tensor_tensor(mleftb[:, :], psr[:, :], recb[:, EPP - 1, 0:1], less[:, :], ALU.is_equal, ALU.mult))
            closing([s_ld, s_set, s_ch, s_iota, s_dg, s_row])

        for layer, (src_table, dst_table) in enumerate(((X1, H1), (H1, X2))):
            c = ExitStack()
            with c:
                pre = f"r{layer + 1}_"
                X = sb(pre + "X", [P, 2 * TS, D], fp32, c)
                acc = sb(pre + "acc", [P, 2 * TS, D], fp32, c)
                cap = sb(pre + "cap", [P, D], fp32, c)
                own = [sb(pre + f"own{i}", [P, U, D], fp32, c) for i in range(2)]
                old = [sb(pre + f"old{i}", [P, U, D], fp32, c) for i in range(2)] if layer else None
                y = [sb(pre + f"y{i}", [P, U, D], fp32, c) for i in range(2)]
                z = [sb(pre + f"z{i}", [P, U, D], fp32, c) for i in range(2)]
                res = [sb(pre + f"res{i}", [P, U, D], fp32, c) for i in range(2)]
                xT = sb(pre + "xT", [P, 4, TS * P], fp32, c)
                psT = [pb(pre + f"psT{i}", [P, TS * P], c) for i in range(4)]
                psO = [pb(pre + f"psO{i}", [P, TS * P], c) for i in range(2)]
                psC = pb(pre + "psC", [P, D], c)
                loaded = names(pre, c, "own_loaded0", "own_loaded1")
                old_loaded = names(pre, c, "old_loaded0", "old_loaded1")
                stored = names(pre, c, "stored0", "stored1")
                counts = names(pre, c, "indices_ready", "transposed", "evacuated", "edge_weighted", "cap_ready", "sum_ready", "product_ready",
                              "y_ready", "chain1", "chain2", "var1", "std1", "norm1", "applied1", "scaled", "var2", "std2", "norm2", "result_ready",
                              "carry_ready", "cleared", "map_copied")
                (s_idx, s_tr, s_ev, s_wtd, s_cap, s_sum, s_out, s_y, s_ch1, s_ch2, s_var1, s_std1, s_norm1, s_app1, s_scaled, s_var2, s_std2,
                 s_norm2, s_res, s_carry, s_set, s_mcp) = counts
                ORDER = (1, 2, 0)
                TQ = 4

                with nc.Block() as block:
                    @block.sync
                    def _(sp):
                        def load(s):
                            wait(sp, s_tr, free(s, TQ))
                            sp.dma_start(own[s.par][:, TS:U, :], node_rows(src_table, s.n)).then_inc(loaded[s.par], 16)
                            sp.dma_start(own[s.par][:, 0:TS, :], slot_rows(src_table, s.n)).then_inc(loaded[s.par], 16)

                        def load_old(s):
                            wait(sp, s_scaled, free(s, 1))
                            sp.dma_start(old[s.par][:, TS:U, :], node_rows(X1, s.n)).then_inc(old_loaded[s.par], 16)
                            sp.dma_start(old[s.par][:, 0:TS, :], slot_rows(X1, s.n)).then_inc(old_loaded[s.par], 16)

                        def store(s):
                            sp.wait_ge(s_res, s.n + 1)
                            sp.dma_start(node_rows(dst_table, s.n), res[s.par][:, TS:U, :]).then_inc(stored[s.par], 16)
                            sp.dma_start(slot_rows(dst_table, s.n), res[s.par][:, 0:TS, :]).then_inc(stored[s.par], 16)

                        pipelined(sp, [(load, 2), (store, -1), (load_old, 1)] if layer else [(load, 2), (store, -1)])
                        for i in range(2):
                            sp.wait_ge(stored[i], 32 * (STEPS // 2))

                    @block.gpsimd
                    def _(pool):
                        last_row, last_target = pool.to_reg(src_table.shape[0] - 1), pool.to_reg(NPAD - 1)
                        def fetch(s):
                            if s.last:
                                return
                            wait(pool, s_sum, free(s, TS))
                            wait(pool, s_cap, free(s, TS))
                            nc.gpsimd.tensor_copy(idxr[:, s.par, 0:TS], gidx[:, bass.ds(s.n * TS, TS)]).then_inc(s_idx, 1)
                            indices(pool, s_idx, s.n + 1)
                            for k in range(TS):
                                gather(pool, X[:, s.par * TS + k, :], src_table, idxr[:, s.par, k:k + 1], gathered[s.par * TS + k], last_row)

                        moves = [MAP_MOVES + 16 * TS * (len(range(i, STEPS - 1, 2)) + layer * STEPS // 2) for i in range(2)]

                        def enter(s):
                            pool.wait_ge(map_moved[s.par], (s.n - s.par) * 8 * TS + moves[s.par])
                            nc.gpsimd.tensor_copy(mring[:, s.par, 0, :], endb[:, bass.ds(s.n * TS, TS)]).then_inc(s_mcp, 1)
                            nc.gpsimd.tensor_copy(mring[:, s.par, 1, :], endslot[:, bass.ds(s.n * TS, TS)]).then_inc(s_mcp, 1)
                            indices(pool, s_mcp, s.n * 2 + 2)
                            for k in range(TS):
                                scatter_rows(pool, slot_of_node, mring[:, s.par, 1, k:k + 1], mring[:, s.par, 0, k:k + 1], map_moved[s.par], last_target)

                        def look_up(s):
                            pool.wait_ge(map_moved[s.par], (s.n - s.par) * 8 * TS + moves[s.par])
                            if not (isinstance(s.n, int) and s.n < 2):
                                nc.gpsimd.tensor_copy(gidxb[:, bass.ds(s.n * TS - 2 * TS, TS)], mring[:, s.par, 2, :]).then_inc(s_mcp, 1)
                            else:
                                nc.gpsimd.tensor_copy(mring[:, s.par, 2, :], mring[:, s.par, 1, :]).then_inc(s_mcp, 1)
                            nc.gpsimd.tensor_copy(mring[:, s.par, 0, :], dstb[:, bass.ds(s.n * TS, TS)]).then_inc(s_mcp, 1)
                            indices(pool, s_mcp, s.n * 2 + 2)
                            for k in range(TS):
                                gather(pool, mring[:, s.par, 2, k:k + 1], slot_of_node, mring[:, s.par, 0, k:k + 1], map_moved[s.par], last_target)

                        pipelined(pool, [(fetch, 2), (look_up if layer else enter, 0)])
                        for i in range(2):
                            pool.wait_ge(map_moved[i], moves[i] + 8 * TS * STEPS)
                            if layer:
                                nc.gpsimd.tensor_copy(gidxb[:, (STEPS - 2 + i) * TS:(STEPS - 1 + i) * TS], mring[:, i, 2, :]).then_inc(s_mcp, 1)

                    @block.tensor
                    def _(pe):
                        t = nc.tensor

                        def nodes(s):
                            for q, g in enumerate(ORDER):
                                wait(pe, s_ev, (s.n - 1) * TQ + q + 1)
                                if q == 0:
                                    pe.wait_ge(loaded[s.par], (s.n - s.par) * 16 + 32)
                                for j in range(TS):
                                    m = t.transpose(psT[q][:, j * P:(j + 1) * P], own[s.par][:, g * TS + j, :], ident[:, :])
                                m.then_inc(s_tr, 1)
                            if s.last:
                                pe.wait_ge(s_sum, EPP)
                                t.matmul(psC[:, :], mleft[:, :], acc[:, (SIDE - 1) % (2 * TS), :], start=True, stop=True).then_inc(s_carry, 1)
                            pe.wait_ge(s_sum, s.n * TS + TS)
                            wait(pe, s_ev, s.n * TQ)
                            for j in range(TS):
                                m = t.transpose(psT[3][:, j * P:(j + 1) * P], acc[:, s.par * TS + j, :], ident[:, :])
                            m.then_inc(s_tr, 1)
                            for q, g in enumerate(ORDER):
                                u = s.n * 3 + q
                                ps = psO[(s.par + q) % 2]
                                pe.wait_ge(s_ev, s.n * TQ + (q + 1 if g else TQ))
                                wait(pe, s_y, u - 1)
                                t.matmul(ps[:, :], ones[0:1, :], biases[f"L1_gnn_b_l{layer}"][0:1, :, :], start=True, stop=False)
                                for j in range(TS):
                                    if g == 0:
                                        t.matmul(ps[:, j * P:(j + 1) * P], xT[:, 3, j * P:(j + 1) * P], wsage[:, 2 * layer, :], start=False, stop=False)
                                    m = t.matmul(ps[:, j * P:(j + 1) * P], xT[:, q, j * P:(j + 1) * P], wsage[:, 2 * layer + 1, :], start=False, stop=j == TS - 1)
                                m.then_inc(s_out, 1)

                        pipelined(pe, [(nodes, 1)])

                    @block.scalar
                    def _(act):
                        sc = nc.scalar

                        def edges(s):
                            if s.last:
                                return
                            for k in range(TS):
                                edge_rows(act, s, k)
                                sc.activation(X[:, s.par * TS + k, :], X[:, s.par * TS + k, :], ACT.Copy, scale=rdeg[:, bass.ds(s.n * TS + k, 1)]).then_inc(s_wtd, 1)

                        def transposes(s):
                            for q in range(TQ):
                                act.wait_ge(s_tr, s.n * TQ + q + 1)
                                wait(act, s_out, s.n * 3 + (q - 2 if q < 3 else 0))
                                sc.copy(xT[:, q, :], psT[q][:, :]).then_inc(s_ev, 1)

                        def products(s):
                            for q, g in enumerate(ORDER):
                                act.wait_ge(s_out, s.n * 3 + q + 1)
                                if q == 0:
                                    wait(act, s_app1, free(s, 1))
                                sc.copy(y[s.par][:, g * TS:(g + 1) * TS, :], psO[(s.par + q) % 2][:, :]).then_inc(s_y, 1)

                        def first_std(s):
                            deviate(act, s, 0, 0, s_var1, s_std1)

                        def first_norm(s):
                            wait(act, s_res, free(s, 1))
                            normalize(act, s, 0, y[s.par], z[s.par], 0, s_norm1, s_app1)

                        def second_std(s):
                            if layer:
                                deviate(act, s, 1, 0, s_var2, s_std2)

                        def finish(s):
                            wait(act, stored[s.par], (s.n - s.par) * 16)
                            if layer:
                                normalize(act, s, 1, z[s.par], res[s.par], 0, s_norm2, s_res)
                            else:
                                act.wait_ge(s_scaled, s.n + 1)
                                sc.activation(res[s.par][:, :, :], z[s.par][:, :, :], ACT.Relu).then_inc(s_res, 1)

                        if layer:
                            pipelined(act, [(transposes, 1), (first_std, 0), (first_norm, 0), (products, 1), (second_std, -1), (edges, 2), (finish, -1)])
                        else:
                            pipelined(act, [(transposes, 1), (first_std, 0), (first_norm, 0), (edges, 2), (products, 1), (finish, -1)])

                    @block.vector
                    def _(dve):
                        v = nc.vector
                        v.memset(acc[:, :, :], 0.0).then_inc(s_set, 1)
                        v.memset(cap[:, :], 0.0).then_inc(s_set, 1)
                        dve.wait_ge(s_set, 2)
                        ch1, ch2 = Chain(dve, s_ch1, U + LN_LINKS), Chain(dve, s_ch2, layer * (U + LN_LINKS) + 1 + layer)

                        def edges(s):
                            wait(dve, s_tr, free(s, TQ))
                            if s.last:
                                side_sums(acc, cap, psC[:, :], s_sum, s_carry, dve)
                                return
                            for k in range(TS):
                                dve.wait_ge(s_wtd, s.n * TS + k + 1)
                                scan_edge(s, k, X[:, s.par * TS + k, :], acc, cap, s_sum, s_cap, dve)

                        def first_norm(s):
                            ch1.begin(s)
                            dve.wait_ge(s_y, s.n * 3 + 3)
                            normalizing(dve, ch1, s, 0, y[s.par], 0, s_var1, s_std1, s_norm1)

                        def second_norm(s):
                            ch2.begin(s)
                            zs = z[s.par][:, :, :]
                            dve.wait_ge(s_app1, s.n + 1)
                            ch2.link(v.tensor_tensor(zs, zs, spread(rows[f"L1_gnn_gamma{layer}"], U), ALU.mult))
                            if not layer:
                                v.tensor_tensor(zs, zs, spread(rows["L1_gnn_beta0"], U), ALU.add).then_inc(s_scaled, 1)
                                return
                            ch2.link(v.tensor_tensor(zs, zs, spread(rows["L1_gnn_beta1"], U), ALU.add))
                            dve.wait_ge(old_loaded[s.par], (s.n - s.par) * 16 + 32)
                            v.scalar_tensor_tensor(zs, zs, 0.0, old[s.par][:, :, :], ALU.max, ALU.add).then_inc(s_scaled, 1)
                            dve.wait_ge(s_scaled, s.n + 1)
                            normalizing(dve, ch2, s, 1, z[s.par], 0, s_var2, s_std2, s_norm2)

                        pipelined(dve, [(edges, 1), (first_norm, 0), (second_norm, -1)])
                edges_gathered()
                closing([*loaded, *old_loaded, *stored, *counts])

        with ExitStack() as c:
            buf = sb("x2buf", [P, 2 * TS, D], fp32, c)
            loaded = names("x2_", c, "loaded0", "loaded1")
            (s_idx,) = names("x2_", c, "indices_ready")
            with nc.Block() as block:
                @block.sync
                def _(sp):
                    def load(s):
                        if not (isinstance(s.n, int) and s.n < 2):
                            for k in range(TS):
                                slot_rows_free(sp, s, k)
                        sp.dma_start(buf[:, s.par * TS:(s.par + 1) * TS, :], slot_rows(X2, s.n)).then_inc(loaded[s.par], 16)

                    pipelined(sp, [(load, 2)])

                @block.gpsimd
                def _(pool):
                    last_node = pool.to_reg(N - 1)

                    def scatter(s):
                        row_numbers_free(pool, s)
                        nc.gpsimd.tensor_copy(idxr[:, s.par, 0:TS], outidx[:, bass.ds(s.n * TS, TS)]).then_inc(s_idx, 1)
                        pool.wait_ge(loaded[s.par], arrived(s))
                        indices(pool, s_idx, s.n + 1)
                        for k in range(TS):
                            scatter_rows(pool, X2[0:NPAD, :], buf[:, s.par * TS + k, :], idxr[:, s.par, k:k + 1], own_moves[s.par * TS + k], last_node)

                    pipelined(pool, [(scatter, 0)])
                    for k in range(2 * TS):
                        pool.wait_ge(own_moves[k], placed[k] + 8 * STEPS)
            slots_moved()
            closing([*loaded, s_idx])

        for layer, (src_table, index, sum_table) in enumerate(((X2[0:NPAD, :], dstb, E1), (E1, gidxb, E2), (E2, gidxb, ES))):
            c = ExitStack()
            with c:
                pre = f"r{layer + 3}_"
                LAST = layer == 2
                X = sb(pre + "X", [P, 2 * TS, D], fp32, c)
                acc = sb(pre + "acc", [P, 2 * TS, D], fp32, c)
                cap = sb(pre + "cap", [P, D], fp32, c)
                sums = [sb(pre + f"sums{i}", [P, 2, TS, D], fp32, c) for i in range(2)] if LAST else None
                psC = pb(pre + "psC", [P, D], c)
                loaded = names(pre, c, "sums_loaded0", "sums_loaded1")
                stored = names(pre, c, "stored0", "stored1")
                counts = names(pre, c, "indices_ready", "targets_ready", "edge_weighted", "cap_ready", "sum_ready", "carry_ready", "cleared", "two_added", "all_added")
                s_idx, s_out, s_wtd, s_cap, s_sum, s_carry, s_set, s_two, s_all = counts

                with nc.Block() as block:
                    @block.sync
                    def _(sp):
                        def store(s):
                            sp.wait_ge(s_sum, s.n * TS + TS)
                            sp.dma_start(slot_rows(sum_table, s.n), acc[:, s.par * TS:(s.par + 1) * TS, :]).then_inc(stored[s.par], 16)

                        def load(s):
                            if not (isinstance(s.n, int) and s.n < 2):
                                for k in range(TS):
                                    slot_rows_free(sp, s, k)
                            for i, t in enumerate((E1, E2)):
                                sp.dma_start(sums[s.par][:, i, :, :], slot_rows(t, s.n)).then_inc(loaded[s.par], 16)

                        if LAST:
                            pipelined(sp, [(load, 1)])
                        else:
                            pipelined(sp, [(store, 0)])
                            for i in range(2):
                                sp.wait_ge(stored[i], 8 * STEPS)

                    @block.gpsimd
                    def _(pool):
                        last_node, last_row = pool.to_reg(N - 1), pool.to_reg(src_table.shape[0] - 1)

                        def fetch(s):
                            if s.last:
                                return
                            wait(pool, s_cap, free(s, TS))
                            nc.gpsimd.tensor_copy(idxr[:, s.par, 0:TS], index[:, bass.ds(s.n * TS, TS)]).then_inc(s_idx, 1)
                            indices(pool, s_idx, s.n + 1)
                            for k in range(TS):
                                gather(pool, X[:, s.par * TS + k, :], src_table, idxr[:, s.par, k:k + 1], gathered[s.par * TS + k], last_row)

                        def scatter(s):
                            row_numbers_free(pool, s)
                            nc.gpsimd.tensor_copy(idxr[:, s.par, TS:2 * TS], outb[:, bass.ds(s.n * TS, TS)]).then_inc(s_out, 1)
                            pool.wait_ge(s_all, s.n + 1)
                            indices(pool, s_out, s.n + 1)
                            for k in range(TS):
                                scatter_rows(pool, ES, sums[s.par][:, 0, k, :], idxr[:, s.par, TS + k:TS + k + 1], own_moves[s.par * TS + k], last_node)

                        if LAST:
                            pipelined(pool, [(fetch, 2), (scatter, 0)])
                            for k in range(2 * TS):
                                pool.wait_ge(own_moves[k], placed[k] + 8 * STEPS)
                        else:
                            pipelined(pool, [(fetch, 2)])

                    @block.tensor
                    def _(pe):
                        pe.wait_ge(s_sum, EPP)
                        nc.tensor.matmul(psC[:, :], mleftb[:, :], acc[:, (SIDE - 1) % (2 * TS), :], start=True, stop=True).then_inc(s_carry, 1)

                    @block.scalar
                    def _(act):
                        def edges(s):
                            if s.last:
                                return
                            for k in range(TS):
                                edge_rows(act, s, k)
                                nc.scalar.activation(X[:, s.par * TS + k, :], X[:, s.par * TS + k, :], ACT.Copy, scale=weightb[:, bass.ds(s.n * TS + k, 1)]).then_inc(s_wtd, 1)

                        pipelined(act, [(edges, 0)])

                    @block.vector
                    def _(dve):
                        v = nc.vector
                        v.memset(acc[:, :, :], 0.0).then_inc(s_set, 1)
                        v.memset(cap[:, :], 0.0).then_inc(s_set, 1)
                        dve.wait_ge(s_set, 2)

                        def edges(s):
                            if LAST:
                                wait(dve, s_all, free(s, 1))
                            else:
                                wait(dve, stored[s.par], (s.n - s.par) * 8)
                            if s.last:
                                side_sums(acc, cap, psC[:, :], s_sum, s_carry, dve)
                                return
                            for k in range(TS):
                                dve.wait_ge(s_wtd, s.n * TS + k + 1)
                                scan_edge(s, k, X[:, s.par * TS + k, :], acc, cap, s_sum, s_cap, dve, sameb, leadb)

                        def add(s):
                            dve.wait_ge(loaded[s.par], (s.n - s.par) * 16 + 32)
                            two = sums[s.par][:, 0, :, :]
                            v.tensor_tensor(two, two, sums[s.par][:, 1, :, :], ALU.add).then_inc(s_two, 1)
                            dve.wait_ge(s_two, s.n + 1)
                            dve.wait_ge(s_sum, s.n * TS + TS)
                            v.tensor_tensor(two, two, acc[:, s.par * TS:(s.par + 1) * TS, :], ALU.add).then_inc(s_all, 1)

                        pipelined(dve, [(edges, 0), (add, 0)] if LAST else [(edges, 0)])
                edges_gathered()
                if LAST:
                    slots_moved()
                closing([*loaded, *stored, *counts])

        for layer in range(3):
            c = ExitStack()
            with c:
                pre = f"n{layer}_"
                node_table, lin_table = ((X2, T1), (T1, T2), (T2, T3))[layer]
                TQ = TN // TS
                W = node_table.shape[1]
                nin = [sb(pre + f"nodes{i}", [P, TN, W], fp32, c) for i in range(2)]
                sums = [sb(pre + f"sums{i}", [P, TN, D], fp32, c) for i in range(2)] if layer == 0 else None
                z = sb(pre + "z", [P, TN, D], fp32, c) if layer == 0 else None
                res = [sb(pre + f"res{i}", [P, TN, D], fp32, c) for i in range(2)] if layer == 0 else None
                tout = [sb(pre + f"tout{i}", [P, TQ * TS, TW], fp32, c) for i in range(2)]
                xT = sb(pre + "xT", [P, TQ, TS * P], fp32, c)
                psT = [pb(pre + f"psT{i}", [P, TS * P], c) for i in range(2)]
                psG = [pb(pre + f"psG{i}", [P, 2, 512], c) for i in range(2)]
                loaded = names(pre, c, "nodes_loaded0", "nodes_loaded1")
                stored_res = names(pre, c, "results_stored0", "results_stored1")
                stored_lin = names(pre, c, "products_stored0", "products_stored1")
                counts = names(pre, c, "transposed", "evacuated", "product_ready", "product_evacuated", "chain", "var", "std", "norm",
                              "normalized", "combined")
                OWN = layer == 1
                rows_t = sb(pre + "own_t", [P, 2 * TS, TW], fp32, c) if OWN else None
                moved = names(pre, c, "own_stored0", "own_stored1")
                s_idx, s_own = names(pre, c, "indices_ready", "scores_kept")
                s_tr, s_ev, s_out, s_lin, s_bch, s_var, s_std, s_norm, s_res, s_comb = counts
                NL = 32 if layer == 0 else 16

                def store_counts(s, each):
                    return (s.n - s.par) * (each // 2)

                def own_moved(eng, s):
                    for k in range(TS):
                        slot_rows_moved(eng, s, k)

                with nc.Block() as block:
                    if OWN:
                        @block.gpsimd
                        def _(pool):
                            last_row = pool.to_reg(NPAD - 1)

                            def fetch(s):
                                wait(pool, moved[s.par], (s.n - s.par) * 8)
                                wait(pool, s_own, free(s, 1))
                                nc.gpsimd.tensor_copy(idxr[:, s.par, 0:TS], ownidx[:, bass.ds(s.n * TS, TS)]).then_inc(s_idx, 1)
                                indices(pool, s_idx, s.n + 1)
                                for k in range(TS):
                                    i, at = s.par * TS + k, idxr[:, s.par, k:k + 1]
                                    gather(pool, rows_t[:, i, :], T1[0:NPAD, :], at, own_moves[i], last_row)

                            pipelined(pool, [(fetch, 2)])

                        @block.vector
                        def _(dve):
                            def keep(s):
                                own_moved(dve, s)
                                nc.vector.tensor_copy(ownal[:, bass.ds(s.n * TS, TS), :], rows_t[:, s.par * TS:(s.par + 1) * TS, D:TW]).then_inc(s_own, 1)

                            pipelined(dve, [(keep, 0)])

                    @block.sync
                    def _(sp):
                        def load(s):
                            if layer == 0:
                                wait(sp, s_comb, free(s, 1))
                            else:
                                wait(sp, s_tr, free(s, TQ))
                            sp.dma_start(nin[s.par][:, :, :], node_rows(node_table, s.n)).then_inc(loaded[s.par], 16)
                            if layer == 0:
                                sp.dma_start(sums[s.par][:, :, :], node_rows(ES, s.n)).then_inc(loaded[s.par], 16)

                        def store_results(s):
                            sp.wait_ge(s_res, s.n + 1)
                            sp.dma_start(node_rows(X3, s.n), res[s.par][:, :, :]).then_inc(stored_res[s.par], 16)

                        def store_own(s):
                            own_moved(sp, s)
                            sp.dma_start(slot_rows(T1, s.n), rows_t[:, s.par * TS:(s.par + 1) * TS, :]).then_inc(moved[s.par], 16)

                        def store_products(s):
                            sp.wait_ge(s_lin, s.n * TQ + TQ)
                            sp.dma_start(node_rows(lin_table, s.n), tout[s.par][:, 0:TN, :]).then_inc(stored_lin[s.par], 16)

                        if layer == 0:
                            pipelined(sp, [(load, 2), (store_results, 0), (store_products, -1)])
                        elif OWN:
                            pipelined(sp, [(load, 2), (store_own, 0), (store_products, -1)])
                        else:
                            pipelined(sp, [(load, 2), (store_products, -1)])
                        for i in range(2):
                            if OWN:
                                sp.wait_ge(moved[i], 16 * (STEPS // 2))
                            if layer == 0:
                                sp.wait_ge(stored_res[i], 16 * (STEPS // 2))
                            sp.wait_ge(stored_lin[i], 16 * (STEPS // 2))

                    def evacuate(eng, copy, s, q):
                        eng.wait_ge(s_out, s.n * TQ + q + 1)
                        if q == 0:
                            wait(eng, stored_lin[s.par], store_counts(s, 16))
                        copy(tout[s.par][:, q * TS:(q + 1) * TS, :].rearrange("p (b j) f -> p b (j f)", b=2),
                             psG[(s.par * TQ + q) % 2][:, :, 0:2 * TW]).then_inc(s_lin, 1)

                    @block.tensor
                    def _(pe):
                        t = nc.tensor

                        def nodes(s):
                            for q in range(TQ):
                                u = s.n * TQ + q
                                wait(pe, s_ev, u - 1)
                                if q == 0 and layer:
                                    pe.wait_ge(loaded[s.par], arrived(s))
                                elif q == 0:
                                    pe.wait_ge(s_res, s.n + 1)
                                for j in range(TS):
                                    tile = res[s.par][:, q * TS + j, :] if layer == 0 else nin[s.par][:, q * TS + j, 0:D]
                                    m = t.transpose(psT[(s.par * TQ + q) % 2][:, j * P:(j + 1) * P], tile, ident[:, :])
                                m.then_inc(s_tr, 1)
                            for q in range(TQ):
                                u = s.n * TQ + q
                                pe.wait_ge(s_ev, u + 1)
                                wait(pe, s_lin, u - 1)
                                for j in range(TS):
                                    m = t.matmul(psG[(s.par * TQ + q) % 2][:, j // 2, j % 2 * TW:(j % 2 + 1) * TW],
                                                 xT[:, q, j * P:(j + 1) * P], wgat[:, layer, :], start=True, stop=True)
                                m.then_inc(s_out, 1)

                        pipelined(pe, [(nodes, 0)])

                    @block.scalar
                    def _(act):
                        sc = nc.scalar

                        def norm(s):
                            deviate(act, s, 0, 0, s_var, s_std, TN, 0.25)
                            wait(act, stored_res[s.par], store_counts(s, 16))
                            wait(act, s_tr, free(s, TQ))
                            normalize(act, s, 0, z, res[s.par], 0, s_norm, s_res, TN)

                        def transposes(s):
                            for q in range(TQ):
                                u = s.n * TQ + q
                                act.wait_ge(s_tr, u + 1)
                                wait(act, s_out, u - TQ + 1)
                                dst, bank = xT[:, q, :], psT[(s.par * TQ + q) % 2]
                                if layer:
                                    sc.activation(dst, bank[:, :], ACT.Relu, bias=gatbias[:, layer - 1:layer]).then_inc(s_ev, 1)
                                else:
                                    sc.copy(dst, bank[:, :]).then_inc(s_ev, 1)

                        def products(s):
                            for q in range(TQ):
                                evacuate(act, sc.copy, s, q)

                        if layer == 0:
                            pipelined(act, [(norm, 0), (transposes, 0)])
                        else:
                            pipelined(act, [(transposes, 0), (products, -1)])

                    if layer == 0:
                        @block.vector
                        def _(dve):
                            v = nc.vector
                            ch = Chain(dve, s_bch, TN + LN_LINKS + 1)

                            def norm(s):
                                ch.begin(s)
                                dve.wait_ge(loaded[s.par], (s.n - s.par) * (NL // 2) + NL)
                                wait(dve, s_res, s.n)
                                v.scalar_tensor_tensor(z[:, :, :], nin[s.par][:, :, :], 5.0, sums[s.par][:, :, :], ALU.mult, ALU.add).then_inc(s_comb, 1)
                                dve.wait_ge(s_comb, s.n + 1)
                                normalizing(dve, ch, s, 0, z, 0, s_var, s_std, s_norm, TN, 0.25)

                            def products(s):
                                for q in range(TQ):
                                    evacuate(dve, v.tensor_copy, s, q)

                            pipelined(dve, [(norm, 0), (products, -1)])
                if OWN:
                    slots_moved()
                closing([*loaded, *stored_res, *stored_lin, *moved, s_idx, s_own, *counts])


        xrow = sb("xrow", [P, EPP, TW])
        pself = sb("pself", [P, TP, H])
        for layer in range(3):
            pre = f"r{layer + 6}_"
            table, next_table = ((T1, T2), (T2, T3), (T3, None))[layer]
            HH = (H, H, 1)[layer]
            CH = D // HH
            W = D + HH
            c = ExitStack()
            with c:
                first, count = ((0, 18), (18, 16), (34, 16))[layer]
                nin = [sb(pre + f"fin_nodes{i}", [P, TN, TW], fp32, c) for i in range(2)]
                x3in = [sb(pre + f"fin_x3{i}", [P, TN, D], fp32, c) for i in range(2)]
                y = [sb(pre + f"fin_y{i}", [P, TN, D], fp32, c) for i in range(2)]
                done = [sb(pre + f"fin_out{i}", [P, TN, D], fp32, c) for i in range(2)]
                z = [sb(pre + f"fin_z{i}", [P, TN, D], fp32, c) for i in range(2)]
                loaded = names(pre, c, "nodes_loaded0", "nodes_loaded1")
                x3_loaded = names(pre, c, "x3_loaded0", "x3_loaded1")
                stored = names(pre, c, "out_stored0", "out_stored1")
                counts = names(pre, c, "biased", "chain1", "chain2", "bias_read", "var1", "std1", "norm1", "normalized", "added", "var2", "std2", "norm2", "result_ready")
                s_y, s_ch1, s_ch2, s_bias, s_var1, s_std1, s_norm1, s_app1, s_added, s_var2, s_std2, s_norm2, s_res = counts

                with nc.Block() as block:
                    @block.gpsimd
                    def _(pool):
                        last_row = pool.to_reg(table.shape[0] - 1)
                        for t in range(EPP):
                            gather(pool, xrow[:, t, :], table, (gidx if layer else srcidx)[:, t:t + 1], gathered[t % (2 * TS)], last_row)
                        for k in range(2 * TS):
                            pool.wait_ge(gathered[k], before[k] + 16 * len(range(k, EPP, 2 * TS)))

                    @block.sync
                    def _(sp):
                        def load(s):
                            wait(sp, s_y, free(s, 1))
                            sp.dma_start(nin[s.par][:, :, :], node_rows(T3, s.n + first)).then_inc(loaded[s.par], 16)

                        def load_x3(s):
                            wait(sp, s_added, free(s, 1))
                            sp.dma_start(x3in[s.par][:, :, :], node_rows(X3, s.n + first)).then_inc(x3_loaded[s.par], 16)

                        def store(s):
                            sp.wait_ge(s_res, s.n + 1)
                            row = (s.n + first) * TN * P
                            if isinstance(row, int) and row + TN * P > N:
                                rest = max(0, N - row) // TN
                                if rest:
                                    dst = out[row:N, :].rearrange("(p j) f -> p j f", j=TN)
                                    for p0, p1 in ((0, rest // 16 * 16), (rest // 16 * 16, rest)):
                                        sp.dma_start(dst[p0:p1], done[s.par][p0:p1, :, :]).then_inc(stored[s.par], 16)
                                return
                            dst = out[bass.ds(row, TN * P), :].rearrange("(p j) f -> p j f", j=TN)
                            sp.dma_start(dst, done[s.par][:, :, :]).then_inc(stored[s.par], 16)

                        pipelined(sp, [(load, 2), (store, -1), (load_x3, 1)], count)
                        whole = min(count, N // (TN * P) - first)
                        for i in range(2):
                            sp.wait_ge(stored[i], 16 * ((whole + 1 - i) // 2) + (32 if whole < count and whole % 2 == i else 0))

                    @block.scalar
                    def _(act):
                        def first_norm(s):
                            deviate(act, s, 0, 0, s_var1, s_std1, TN)
                            wait(act, s_res, free(s, 1))
                            normalize(act, s, 0, y[s.par], z[s.par], 0, s_norm1, s_app1, TN)

                        def second_norm(s):
                            deviate(act, s, 1, 0, s_var2, s_std2, TN)
                            wait(act, stored[s.par], (s.n - s.par) * 8)
                            normalize(act, s, 1, z[s.par], done[s.par], 0, s_norm2, s_res, TN)

                        pipelined(act, [(first_norm, 0), (second_norm, -1)], count)

                    @block.vector
                    def _(dve):
                        v = nc.vector
                        ch1, ch2 = Chain(dve, s_ch1, TN + LN_LINKS), Chain(dve, s_ch2, TN + LN_LINKS + 2)

                        def bias(s):
                            dve.wait_ge(loaded[s.par], arrived(s))
                            wait(dve, s_app1, free(s, 1))
                            v.tensor_tensor(y[s.par][:, :, :], nin[s.par][:, :, 0:D], spread(rows["L3_gnn_b2"], TN), ALU.add).then_inc(s_y, 1)

                        def first_norm(s):
                            ch1.begin(s)
                            dve.wait_ge(s_y, s.n + 1)
                            normalizing(dve, ch1, s, 0, y[s.par], 0, s_var1, s_std1, s_norm1, TN)

                        def second_norm(s):
                            ch2.begin(s)
                            zs = z[s.par][:, :, :]
                            dve.wait_ge(s_app1, s.n + 1)
                            ch2.link(v.tensor_tensor(zs, zs, spread(rows["L3_gnn_gamma"], TN), ALU.mult))
                            ch2.link(v.tensor_tensor(zs, zs, spread(rows["L3_gnn_beta"], TN), ALU.add))
                            dve.wait_ge(x3_loaded[s.par], arrived(s))
                            v.tensor_tensor(zs, zs, x3in[s.par][:, :, :], ALU.add).then_inc(s_added, 1)
                            dve.wait_ge(s_added, s.n + 1)
                            normalizing(dve, ch2, s, 1, z[s.par], 0, s_var2, s_std2, s_norm2, TN)

                        pipelined(dve, [(bias, 0), (first_norm, 0), (second_norm, -1)], count)
                edges_gathered()
                closing([*loaded, *x3_loaded, *stored, *counts])

            c = ExitStack()
            with c:
                bpre = pre + "w_"
                both = sb(bpre + "both", [P, EPP, 2 * HH], fp32, c)
                spreadb = sb(bpre + "spread", [P, EPP, 2 * HH], fp32, c)
                e = sb(bpre + "e", [P, EPP, HH], fp32, c)
                es = sb(bpre + "es", [P, EPP, HH], fp32, c)
                fmax = sb(bpre + "fmax", [P, EPP, HH], fp32, c)
                bmax = sb(bpre + "bmax", [P, EPP, HH], fp32, c)
                pen = sb(bpre + "pen", [P, 4, EPP], fp32, c)
                dg = sb(bpre + "dg", [P, 2 * H, P], fp32, c)
                tmp = sb(bpre + "tmp", [P, 2 * H, P], fp32, c)
                cross = sb(bpre + "cross", [P, 2 * H], fp32, c)
                psX = pb(bpre + "psX", [P, 2 * H], c)
                psM = [pb(bpre + f"psM{i}", [P, H, P], c) for i in range(2)]
                counts = names(bpre, c, "chain", "own_crossed", "diagonals", "maxima_crossed", "weights")
                s_ch, s_xo, s_dg, s_mc, s_w = counts

                with nc.Block() as block:
                    def score(arr, t, side):
                        return arr[:, t, side * H:side * H + HH]

                    @block.tensor
                    def _(pe):
                        for l in range(2):
                            m = nc.tensor.matmul(psX[:, l * HH:(l + 1) * HH], mside[:, :], score(ownal, SIDE, l), start=True, stop=True)
                        m.then_inc(s_xo, 1)
                        pe.wait_ge(s_dg, 1)
                        for l in range(2):
                            for h in range(HH):
                                m = nc.tensor.matmul(psM[l][:, h, :], ones[:, :], dg[:, l * HH + h, :], start=True, stop=True)
                        m.then_inc(s_mc, 1)

                    @block.vector
                    def _(dve):
                        v = nc.vector
                        ch = Chain(dve, s_ch, 0)
                        A = slice(0, EPP)

                        def col(t, n):
                            return t.unsqueeze(2).to_broadcast([P, EPP, n])

                        for l in range(2):
                            bl = slice(l * HH, (l + 1) * HH)
                            ch.link(v.tensor_tensor(both[:, :, bl], score(ownal, A, l), col(mainend[:, A], HH), ALU.mult))
                            ch.link(v.tensor_tensor(spreadb[:, :, bl], col(sidend[:, A], HH), score(ownal, slice(SIDE, SIDE + 1), l).to_broadcast([P, EPP, HH]), ALU.mult))
                        ch.link(v.tensor_tensor(both[:, :, :], both[:, :, :], spreadb[:, :, :], ALU.add))
                        dve.wait_ge(s_xo, 1)
                        ch.link(v.scalar_tensor_tensor(both[:, EPP - 1, :], psX[:, 0:2 * HH], goes[:, EPP - 1:EPP], both[:, EPP - 1, :], ALU.mult, ALU.add))
                        for q in range(2 * HH):
                            at = ch.mark(v.tensor_tensor_scan(spreadb[:, ::-1, q], goes[:, ::-1], both[:, ::-1, q], 0.0, ALU.mult, ALU.add))
                        dve.wait_ge(s_ch, at)
                        ch.link(v.tensor_tensor(e[:, :, :], xrow[:, :, D:D + HH], spreadb[:, :, HH:2 * HH], ALU.add))
                        ch.link(v.scalar_tensor_tensor(e[:, :, :], e[:, :, :], 0.2, e[:, :, :], ALU.mult, ALU.max))
                        ch.link(v.tensor_tensor(es[:, :, :], spreadb[:, :, 0:HH], spreadb[:, :, HH:2 * HH], ALU.add))
                        ch.link(v.scalar_tensor_tensor(es[:, :, :], es[:, :, :], 0.2, es[:, :, :], ALU.mult, ALU.max))
                        for i, m in enumerate((same, goes, lead, trail)):
                            ch.link(v.tensor_scalar(pen[:, i, :], m[:, A], 1.0, BIG, ALU.subtract, ALU.mult))
                        for h in range(HH):
                            ch.mark(v.tensor_tensor_scan(fmax[:, :, h], pen[:, 0, :], e[:, :, h], -BIG, ALU.add, ALU.max))
                            at = ch.mark(v.tensor_tensor_scan(bmax[:, ::-1, h], pen[:, 1, ::-1], e[:, ::-1, h], -BIG, ALU.add, ALU.max))
                        dve.wait_ge(s_ch, at)
                        for h in range(HH):
                            ch.link(v.tensor_scalar(dg[:, h, :], ident[:, :], fmax[:, EPP - 1, h:h + 1], None, ALU.mult))
                            ch.link(v.tensor_scalar(dg[:, HH + h, :], ident[:, :], bmax[:, 0, h:h + 1], None, ALU.mult))
                        dve.sem_inc(s_dg, 1)
                        ch.link(v.tensor_tensor(fmax[:, :, :], fmax[:, :, :], bmax[:, :, :], ALU.max))
                        dve.wait_ge(s_mc, 1)
                        for l, link in enumerate((linkl, linkr)):
                            ch.link(v.tensor_tensor(tmp[:, l * HH:(l + 1) * HH, :], psM[l][:, 0:HH, :], link[:, :].unsqueeze(1).to_broadcast([P, HH, P]), ALU.add))
                        ch.link(v.reduce_max(cross[:, 0:2 * HH], tmp[:, 0:2 * HH, :], AX.X))
                        for h in range(HH):
                            for l in range(2):
                                ch.link(v.scalar_tensor_tensor(fmax[:, :, h], pen[:, 2 + l, :], cross[:, l * HH + h:l * HH + h + 1], fmax[:, :, h], ALU.add, ALU.max))
                        ch.link(v.tensor_tensor(fmax[:, :, :], fmax[:, :, :], es[:, :, :], ALU.max))
                        ch.link(v.tensor_tensor(e[:, :, :], e[:, :, :], fmax[:, :, :], ALU.subtract))
                        ch.link(v.tensor_tensor(es[:, :, :], es[:, :, :], fmax[:, :, :], ALU.subtract))
                        ch.link(v.memset(pself[:, EPP:TP, :], 1.0))
                        dve.sem_inc(s_w, 1)

                    @block.scalar
                    def _(act):
                        act.wait_ge(s_w, 1)
                        nc.scalar.activation(xrow[:, :, D:D + HH], e[:, :, :], ACT.Exp)
                        nc.scalar.activation(pself[:, 0:EPP, 0:HH], es[:, :, :], ACT.Exp)
                        nc.scalar.activation(pself[:, SIDE, 0:HH], es[:, 0, :], ACT.Exp).then_inc(s_w, 1)
                closing(counts)

            c = ExitStack()
            with c:
                cpre = pre + "s_"
                LAST = layer == 2
                acc = sb(cpre + "acc", [P, 2 * TS, W], fp32, c)
                cap = sb(cpre + "cap", [P, W], fp32, c)
                own = [sb(cpre + f"own{i}", [P, TS, TW], fp32, c) for i in range(2)]
                x3in = [sb(cpre + f"x3_{i}", [P, TS, D], fp32, c) for i in range(2)] if LAST else None
                z = [sb(cpre + f"z{i}", [P, TS, D], fp32, c) for i in range(2)]
                z2 = [sb(cpre + f"z2_{i}", [P, TS, D], fp32, c) for i in range(2)] if LAST else None
                res = [sb(cpre + f"res{i}", [P, TS, D], fp32, c) for i in range(2)] if LAST else None
                rows_x = sb(cpre + "own_x3", [P, 2 * TS, D], fp32, c) if layer == 0 else None
                den = sb(cpre + "den", [P, TS, HH], fp32, c)
                xT = sb(cpre + "xT", [P, TS * P], fp32, c)
                tout = [sb(cpre + f"tout{i}", [P, TS, TW], fp32, c) for i in range(2)]
                psT = pb(cpre + "psT", [P, TS * P], c)
                psG = [pb(cpre + f"psG{i}", [P, 2, 512], c) for i in range(2)]
                psC = pb(cpre + "psC", [P, W], c)
                loaded = names(cpre, c, "own_loaded0", "own_loaded1")
                x3_loaded = names(cpre, c, "x3_loaded0", "x3_loaded1")
                moved = names(cpre, c, "x3_moved0", "x3_moved1")
                stored = names(cpre, c, "stored0", "stored1")
                counts = names(cpre, c, "edge_weighted", "cap_ready", "sum_ready", "self_ready", "averaged", "transposed", "evacuated", "product_ready",
                              "product_evacuated", "own_copied", "chain", "chain2", "var1", "std1", "norm1", "normalized", "added", "var2", "std2", "norm2",
                              "result_ready", "carry_ready", "cleared", "indices_ready")
                (s_wtd, s_cap, s_sum, s_self, s_avg, s_tr, s_ev, s_out, s_lin, s_own, s_bch, s_ch2, s_var1, s_std1, s_norm1, s_app1, s_added, s_var2, s_std2,
                 s_norm2, s_res, s_carry, s_set, s_idx) = counts

                with nc.Block() as block:
                    @block.sync
                    def _(sp):
                        def load(s):
                            wait(sp, s_self, free(s, 1))
                            sp.dma_start(own[s.par][:, :, :], slot_rows(table, s.n)).then_inc(loaded[s.par], 16)

                        def load_x3(s):
                            wait(sp, s_added, free(s, 1))
                            sp.dma_start(x3in[s.par][:, :, :], slot_rows(X3, s.n)).then_inc(x3_loaded[s.par], 16)

                        def store(s):
                            sp.wait_ge(s_lin, s.n + 1)
                            sp.dma_start(slot_rows(next_table, s.n), tout[s.par][:, :, :]).then_inc(stored[s.par], 16)

                        def store_x3(s):
                            for k in range(TS):
                                slot_rows_moved(sp, s, k)
                            sp.dma_start(slot_rows(X3, s.n), rows_x[:, s.par * TS:(s.par + 1) * TS, :]).then_inc(moved[s.par], 16)

                        if LAST:
                            pipelined(sp, [(load, 2), (load_x3, 1)])
                        elif layer == 0:
                            pipelined(sp, [(load, 2), (store, 0), (store_x3, 0)])
                            for i in range(2):
                                sp.wait_ge(stored[i], 16 * (STEPS // 2))
                                sp.wait_ge(moved[i], 16 * (STEPS // 2))
                        else:
                            pipelined(sp, [(load, 2), (store, 0)])
                            for i in range(2):
                                sp.wait_ge(stored[i], 16 * (STEPS // 2))

                    @block.gpsimd
                    def _(pool):
                        last_node = pool.to_reg(N - 1)
                        def weigh(s):
                            if s.last:
                                return
                            tiles = bass.ds(s.n * TS, TS)
                            w = xrow[:, tiles, D:W].unsqueeze(3).to_broadcast([P, TS, HH, CH])
                            x = xrow[:, tiles, 0:D].rearrange("p t (h c) -> p t h c", h=HH)
                            nc.gpsimd.tensor_tensor(x, x, w, ALU.mult).then_inc(s_wtd, 1)

                        def fetch_x3(s):
                            wait(pool, moved[s.par], (s.n - s.par) * 8)
                            nc.gpsimd.tensor_copy(idxr[:, s.par, 0:TS], ownidx[:, bass.ds(s.n * TS, TS)]).then_inc(s_idx, 1)
                            indices(pool, s_idx, s.n + 1)
                            for k in range(TS):
                                gather(pool, rows_x[:, s.par * TS + k, :], X3[0:NPAD, :], idxr[:, s.par, k:k + 1], own_moves[s.par * TS + k], last_node)

                        def scatter(s):
                            pool.wait_ge(s_res, s.n + 1)
                            row_numbers_free(pool, s)
                            nc.gpsimd.tensor_copy(idxr[:, s.par, 0:TS], outidx[:, bass.ds(s.n * TS, TS)]).then_inc(s_idx, 1)
                            indices(pool, s_idx, s.n + 1)
                            for k in range(TS):
                                pool.indirect_dma_start(out=out, out_offset=bass.IndirectOffsetOnAxis(ap=idxr[:, s.par, k:k + 1], axis=0),
                                                        in_=res[s.par][:, k, :], in_offset=None, bounds_check=last_node, oob_is_err=False).then_inc(own_moves[s.par * TS + k], 16)

                        if LAST:
                            pipelined(pool, [(weigh, 2), (scatter, -1)])
                            for k in range(2 * TS):
                                pool.wait_ge(own_moves[k], placed[k] + 8 * STEPS)
                        elif layer == 0:
                            pipelined(pool, [(weigh, 2), (fetch_x3, 1)])
                        else:
                            pipelined(pool, [(weigh, 2)])

                    @block.tensor
                    def _(pe):
                        t = nc.tensor

                        def carry(s):
                            if s.last:
                                pe.wait_ge(s_sum, EPP)
                                t.matmul(psC[:, :], mleft[:, :], acc[:, (SIDE - 1) % (2 * TS), :], start=True, stop=True).then_inc(s_carry, 1)

                        def product(s):
                            if LAST:
                                return
                            pe.wait_ge(s_avg, s.n + 1)
                            wait(pe, s_ev, s.n)
                            for j in range(TS):
                                m = t.transpose(psT[:, j * P:(j + 1) * P], z[s.par][:, j, :], ident[:, :])
                            m.then_inc(s_tr, 1)
                            pe.wait_ge(s_ev, s.n + 1)
                            wait(pe, s_lin, free(s, 1))
                            for j in range(TS):
                                m = t.matmul(psG[s.par][:, j // 2, j % 2 * TW:(j % 2 + 1) * TW], xT[:, j * P:(j + 1) * P], wgat[:, layer + 1, :], start=True, stop=True)
                            m.then_inc(s_out, 1)

                        pipelined(pe, [(carry, 1), (product, 0)])

                    @block.scalar
                    def _(act):
                        sc = nc.scalar

                        def product(s):
                            act.wait_ge(s_tr, s.n + 1)
                            wait(act, s_out, s.n)
                            sc.activation(xT[:, :], psT[:, :], ACT.Relu, bias=gatbias[:, layer:layer + 1]).then_inc(s_ev, 1)
                            act.wait_ge(s_out, s.n + 1)
                            wait(act, stored[s.par], (s.n - s.par) * 8)
                            wait(act, s_own, free(s, 1))
                            sc.copy(tout[s.par][:, :, :].rearrange("p (b j) f -> p b (j f)", b=2), psG[s.par][:, :, 0:2 * TW]).then_inc(s_lin, 1)

                        def first_norm(s):
                            deviate(act, s, 0, 0, s_var1, s_std1, TS)
                            wait(act, s_res, free(s, 1))
                            normalize(act, s, 0, z[s.par], z2[s.par], 0, s_norm1, s_app1, TS)

                        def second_norm(s):
                            deviate(act, s, 1, 0, s_var2, s_std2, TS)
                            for k in range(TS):
                                slot_rows_free(act, s, k)
                            normalize(act, s, 1, z2[s.par], res[s.par], 0, s_norm2, s_res, TS)

                        pipelined(act, [(first_norm, 0), (second_norm, -1)] if LAST else [(product, 0)])

                    @block.vector
                    def _(dve):
                        v = nc.vector
                        v.memset(acc[:, :, :], 0.0).then_inc(s_set, 1)
                        v.memset(cap[:, :], 0.0).then_inc(s_set, 1)
                        dve.wait_ge(s_set, 2)
                        ch, ch2 = Chain(dve, s_bch, 3 + (TS + LN_LINKS + 2 if LAST else 0)), Chain(dve, s_ch2, TS + LN_LINKS + 2)

                        def edges(s):
                            if s.last:
                                side_sums(acc, cap, psC[:, :], s_sum, s_carry, dve)
                                return
                            dve.wait_ge(s_wtd, s.n + 1)
                            for k in range(TS):
                                scan_edge(s, k, xrow[:, bass.ds(s.n * TS + k, 1), 0:W].rearrange("p a w -> p (a w)"), acc, cap, s_sum, s_cap, dve)

                        def average(s):
                            ch.begin(s)
                            par, tiles = s.par, bass.ds(s.n * TS, TS)
                            dve.wait_ge(loaded[par], arrived(s))
                            if not LAST:
                                wait(dve, s_tr, free(s, 1))
                            else:
                                wait(dve, s_app1, free(s, 1))
                            z4 = z[par][:, :, :].rearrange("p t (h c) -> p t h c", h=HH)
                            sums = acc[:, par * TS:(par + 1) * TS, :]
                            v.tensor_tensor(z4, own[par][:, :, 0:D].rearrange("p t (h c) -> p t h c", h=HH),
                                            pself[:, tiles, 0:HH].unsqueeze(3).to_broadcast([P, TS, HH, CH]), ALU.mult).then_inc(s_self, 1)
                            dve.wait_ge(s_self, s.n + 1)
                            ch.mark(v.tensor_tensor(z[par][:, :, :], z[par][:, :, :], sums[:, :, 0:D], ALU.add))
                            ch.link(v.scalar_tensor_tensor(den[:, :, :], sums[:, :, D:W], 1e-16, pself[:, tiles, 0:HH], ALU.add, ALU.add))
                            ch.link(v.reciprocal(den[:, :, :], den[:, :, :]))
                            ins = v.tensor_tensor(z4, z4, den[:, :, :].unsqueeze(3).to_broadcast([P, TS, HH, CH]), ALU.mult)
                            if LAST:
                                ch.link(ins)
                                ch.link(v.tensor_tensor(z[par][:, :, :], z[par][:, :, :], spread(rows["L3_gnn_b2"], TS), ALU.add))
                                normalizing(dve, ch, s, 0, z[par], 0, s_var1, s_std1, s_norm1, TS)
                            else:
                                ins.then_inc(s_avg, 1)

                        def second_norm(s):
                            ch2.begin(s)
                            zs = z2[s.par][:, :, :]
                            dve.wait_ge(s_app1, s.n + 1)
                            ch2.link(v.tensor_tensor(zs, zs, spread(rows["L3_gnn_gamma"], TS), ALU.mult))
                            ch2.link(v.tensor_tensor(zs, zs, spread(rows["L3_gnn_beta"], TS), ALU.add))
                            dve.wait_ge(x3_loaded[s.par], arrived(s))
                            v.tensor_tensor(zs, zs, x3in[s.par][:, :, :], ALU.add).then_inc(s_added, 1)
                            dve.wait_ge(s_added, s.n + 1)
                            normalizing(dve, ch2, s, 1, z2[s.par], 0, s_var2, s_std2, s_norm2, TS)

                        def own_scores(s):
                            dve.wait_ge(s_lin, s.n + 1)
                            v.tensor_copy(ownal[:, bass.ds(s.n * TS, TS), :], tout[s.par][:, :, D:TW]).then_inc(s_own, 1)

                        pipelined(dve, [(average, 0), (edges, 1), (second_norm, -1)] if LAST else [(average, 0), (edges, 1), (own_scores, -1)])
                if layer == 0:
                    slots_moved()
                closing([*loaded, *x3_loaded, *moved, *stored, *counts])


PREP_LOADS = 16 * (6 + 2 + 2 + 2 + 4 + 2 + 3 * 3 + 9 + 3 * TS)


_INS = ["x", "src", "dst", "edge_type_8", "edge_weight",
        "L0_gnn_W_self", "L0_gnn_b_self", "L0_gnn_W_rel", "L0_gnn_gamma", "L0_gnn_beta",
        "L1_gnn_W_l0", "L1_gnn_b_l0", "L1_gnn_W_r0", "L1_gnn_gamma0", "L1_gnn_beta0",
        "L1_gnn_W_l1", "L1_gnn_b_l1", "L1_gnn_W_r1", "L1_gnn_gamma1", "L1_gnn_beta1",
        "L3_gnn_W0", "L3_gnn_a_src0", "L3_gnn_a_dst0", "L3_gnn_b0",
        "L3_gnn_W1", "L3_gnn_a_src1", "L3_gnn_a_dst1", "L3_gnn_b1",
        "L3_gnn_W2", "L3_gnn_a_src2", "L3_gnn_a_dst2", "L3_gnn_b2", "L3_gnn_gamma", "L3_gnn_beta"]


def kernel(**inputs):
    import numpy as _np
    import concourse.bacc as _bacc
    from concourse import mybir as _mybir
    from concourse.bass_utils import run_bass_kernel_spmd as _run

    nc = _bacc.Bacc("TRN2", target_bir_lowering=False, num_devices=1)
    arrays, args = {}, {}
    for name in _INS:
        arr = _np.ascontiguousarray(inputs[name])
        arrays[f"in_{name}_dram"] = arr
        args[name] = nc.dram_tensor(f"in_{name}_dram", arr.shape, _mybir.dt.from_np(arr.dtype), kind="ExternalInput").ap()
    out = nc.dram_tensor("out_0_dram", (N, D), _mybir.dt.float32, kind="ExternalOutput").ap()
    gnn_kernel(nc, args, out)
    r = _run(nc, [arrays], core_ids=[0])
    return r.results[0]["out_0_dram"]
```
